# Optimizing a Trainium2 kernel written in Bass

```python
import numpy as np
import jax
import jax.numpy as jnp

def _softmax(x, axis=-1):
    return jax.nn.softmax(x, axis=axis)

def _gelu(x):
    return jax.nn.gelu(x, approximate=True)

def _silu(x):
    return jax.nn.silu(x)

def _sigmoid(x):
    return jax.nn.sigmoid(x)

def _layernorm(x, axis=-1, eps=1e-05):
    m = jnp.mean(x, axis=axis, keepdims=True)
    v = jnp.var(x, axis=axis, keepdims=True)
    return (x - m) / jnp.sqrt(v + eps)

def _scatter_add(tgt, idx, src, axis=0):
    return tgt.at[idx].add(src)

def _segment_sum(src, seg, n):
    return jax.ops.segment_sum(src, seg, n)
kernel_name = 'mk_gnn_ffn_d1_gnn_r8_427bea'

def setup_inputs(seed: int=0):
    np.random.seed(seed)
    _w = jnp.asarray

    def _rec_inputs():
        import jax
        import jax.numpy as jnp
        _gk = jax.random.key(seed)
        x = -8.776e-05 + 1 * jax.random.normal(jax.random.fold_in(_gk, 1), (6250, 256), jnp.float32)
        src = jax.random.randint(jax.random.fold_in(_gk, 2), (200000,), 0, 6250, jnp.int32)
        dst = jnp.minimum((6250 * jax.random.uniform(jax.random.fold_in(_gk, 3), (200000,)) ** 2.0).astype(jnp.int32), 49999)
        _o = jnp.argsort(dst, stable=True)
        src = src[_o]
        dst = dst[_o]
        edge_attr_16 = 0.000398968 + 1.00027 * jax.random.normal(jax.random.fold_in(_gk, 11), (200000, 16), jnp.float32)
        return (x, src, dst, edge_attr_16)
    x, src, dst, edge_attr_16 = _rec_inputs()

    def _L0_gnn_setup():
        import jax, jax.numpy as jnp
        import numpy as np
        N_NODES = 2500
        N_EDGES = 40000
        IN_DIM = 256
        HEADS = 4
        OUT_C = 64
        HC = HEADS * OUT_C
        EDGE_DIM = 16
        NEG_SLOPE = 0.2
        key = jax.random.key(seed)
        ks = jax.random.split(key, 10)
        x = jax.random.normal(ks[0], (N_NODES, IN_DIM), dtype=jnp.float32)
        src = jax.random.randint(ks[1], (N_EDGES,), 0, N_NODES)
        off = jax.random.randint(ks[2], (N_EDGES,), 1, N_NODES)
        dst = (src + off) % N_NODES
        edge_index = jnp.stack([src, dst]).astype(jnp.int64)
        edge_attr = jax.random.normal(ks[3], (N_EDGES, EDGE_DIM), dtype=jnp.float32)
        s = 0.05
        return {'x': x, 'edge_index': edge_index, 'edge_attr': edge_attr, 'W_l': jax.random.normal(ks[4], (IN_DIM, HC), dtype=jnp.float32) * s, 'b_l': jnp.zeros((HC,), dtype=jnp.float32), 'W_r': jax.random.normal(ks[5], (IN_DIM, HC), dtype=jnp.float32) * s, 'b_r': jnp.zeros((HC,), dtype=jnp.float32), 'W_e': jax.random.normal(ks[6], (EDGE_DIM, HC), dtype=jnp.float32) * s, 'att': jax.random.normal(ks[7], (HEADS, OUT_C), dtype=jnp.float32) * s, 'W_res': jax.random.normal(ks[8], (IN_DIM, HC), dtype=jnp.float32) * s, 'bias': jnp.zeros((HC,), dtype=jnp.float32)}
    _L0_gnn_all = _L0_gnn_setup()
    _L0_gnn_in = {k: v for k, v in _L0_gnn_all.items() if k in ('W_l', 'b_l', 'W_r', 'b_r', 'W_e', 'att', 'W_res', 'bias')}
    del _L0_gnn_all

    def _L0_ffn_setup():
        import jax, jax.numpy as jnp
        import numpy as np
        B, N, D = (16, 512, 256)
        NUM_EXPERTS, TOP_K, HEADS = (4, 2, 4)
        N_EDGES = 131072
        LN_EPS = 1e-05

        def _layernorm(x, g, b):
            mu = x.mean(-1, keepdims=True)
            var = ((x - mu) ** 2).mean(-1, keepdims=True)
            return (x - mu) * jax.lax.rsqrt(var + LN_EPS) * g + b

        def _forward(x, edge_index, W_gat, att_src, att_dst, b_gat, ln_gamma, ln_beta, W1, b1, W2, b2):
            Bc, Nc, Dc = x.shape
            M = Bc * Nc
            x_flat = x.reshape(M, Dc)
            h = (x_flat @ W_gat).reshape(M, HEADS, NUM_EXPERTS)
            loops = jnp.arange(M, dtype=edge_index.dtype)
            src = jnp.concatenate([edge_index[0], loops])
            dst = jnp.concatenate([edge_index[1], loops])
            a_src = (h * att_src).sum(-1)
            a_dst = (h * att_dst).sum(-1)
            e = jax.nn.leaky_relu(a_src[src] + a_dst[dst], negative_slope=0.2)
            e_max = jax.ops.segment_max(e, dst, num_segments=M)
            ee = jnp.exp(e - e_max[dst])
            denom = jax.ops.segment_sum(ee, dst, num_segments=M)
            alpha = ee / (denom[dst] + 1e-16)
            msg = h[src] * alpha[:, :, None]
            agg = jax.ops.segment_sum(msg, dst, num_segments=M).reshape(M, HEADS * NUM_EXPERTS) + b_gat
            scores = _layernorm(agg, ln_gamma, ln_beta).reshape(M, HEADS, NUM_EXPERTS).mean(1)
            scores = scores.reshape(Bc, Nc, NUM_EXPERTS)
            topk_s, topk_i = jax.lax.top_k(scores, TOP_K)
            w = jax.nn.softmax(topk_s, axis=-1)
            out = jnp.zeros_like(x)
            for ei in range(NUM_EXPERTS):
                g = jnp.where(topk_i == ei, w, 0.0).sum(-1)
                hh = jax.nn.gelu(x @ W1[ei] + b1[ei], approximate=False)
                out = out + g[..., None] * (hh @ W2[ei] + b2[ei])
            return out
        key = jax.random.key(seed)
        ks = jax.random.split(key, 8)
        s = 0.05
        return {'x': jax.random.normal(ks[0], (B, N, D), jnp.float32), 'W_gat': jax.random.normal(ks[1], (D, HEADS * NUM_EXPERTS), jnp.float32) * s, 'att_src': jax.random.normal(ks[2], (HEADS, NUM_EXPERTS), jnp.float32) * s, 'att_dst': jax.random.normal(ks[3], (HEADS, NUM_EXPERTS), jnp.float32) * s, 'b_gat': jnp.zeros((HEADS * NUM_EXPERTS,), jnp.float32), 'ln_gamma': jnp.ones((HEADS * NUM_EXPERTS,), jnp.float32), 'ln_beta': jnp.zeros((HEADS * NUM_EXPERTS,), jnp.float32), 'W1': jax.random.normal(ks[4], (NUM_EXPERTS, D, 2 * D), jnp.float32) * s, 'b1': jnp.zeros((NUM_EXPERTS, 2 * D), jnp.float32), 'W2': jax.random.normal(ks[5], (NUM_EXPERTS, 2 * D, D), jnp.float32) * s, 'b2': jnp.zeros((NUM_EXPERTS, D), jnp.float32), 'edge_index': jax.random.randint(ks[6], (2, N_EDGES), 0, B * N, jnp.int32)}
    _L0_ffn_all = _L0_ffn_setup()
    _L0_ffn_in = {k: v for k, v in _L0_ffn_all.items() if k in ('W_gat', 'att_src', 'att_dst', 'b_gat', 'ln_gamma', 'ln_beta', 'W1', 'b1', 'W2', 'b2', 'edge_index')}
    del _L0_ffn_all
    return {'x': x, 'src': src, 'dst': dst, 'edge_attr_16': edge_attr_16, 'L0_gnn_W_l': _L0_gnn_in['W_l'], 'L0_gnn_b_l': _L0_gnn_in['b_l'], 'L0_gnn_W_r': _L0_gnn_in['W_r'], 'L0_gnn_b_r': _L0_gnn_in['b_r'], 'L0_gnn_W_e': _L0_gnn_in['W_e'], 'L0_gnn_att': _L0_gnn_in['att'], 'L0_gnn_W_res': _L0_gnn_in['W_res'], 'L0_gnn_bias': _L0_gnn_in['bias'], 'L0_ffn_W_gat': _L0_ffn_in['W_gat'], 'L0_ffn_att_src': _L0_ffn_in['att_src'], 'L0_ffn_att_dst': _L0_ffn_in['att_dst'], 'L0_ffn_b_gat': _L0_ffn_in['b_gat'], 'L0_ffn_ln_gamma': _L0_ffn_in['ln_gamma'], 'L0_ffn_ln_beta': _L0_ffn_in['ln_beta'], 'L0_ffn_W1': _L0_ffn_in['W1'], 'L0_ffn_b1': _L0_ffn_in['b1'], 'L0_ffn_W2': _L0_ffn_in['W2'], 'L0_ffn_b2': _L0_ffn_in['b2'], 'L0_ffn_edge_index': _L0_ffn_in['edge_index']}

def reference(x, src, dst, edge_attr_16, L0_gnn_W_l, L0_gnn_b_l, L0_gnn_W_r, L0_gnn_b_r, L0_gnn_W_e, L0_gnn_att, L0_gnn_W_res, L0_gnn_bias, L0_ffn_W_gat, L0_ffn_att_src, L0_ffn_att_dst, L0_ffn_b_gat, L0_ffn_ln_gamma, L0_ffn_ln_beta, L0_ffn_W1, L0_ffn_b1, L0_ffn_W2, L0_ffn_b2, L0_ffn_edge_index):
    import jax
    import jax.numpy as jnp

    def _L0_gnn_ref(x, edge_index, edge_attr, W_l, b_l, W_r, b_r, W_e, att, W_res, bias):
        import jax, jax.numpy as jnp
        import numpy as np
        N_NODES = 2500
        N_EDGES = 40000
        IN_DIM = 256
        HEADS = 4
        OUT_C = 64
        HC = HEADS * OUT_C
        EDGE_DIM = 16
        NEG_SLOPE = 0.2
        N = x.shape[0]
        H, C = att.shape
        src0, dst0 = (edge_index[0], edge_index[1])
        ones = jnp.ones((src0.shape[0],), dtype=x.dtype)
        cnt = jax.ops.segment_sum(ones, dst0, num_segments=N)
        loop_attr = jax.ops.segment_sum(edge_attr, dst0, num_segments=N) / jnp.maximum(cnt, 1.0)[:, None]
        loop = jnp.arange(N, dtype=src0.dtype)
        src = jnp.concatenate([src0, loop])
        dst = jnp.concatenate([dst0, loop])
        ea = jnp.concatenate([edge_attr, loop_attr], axis=0)
        x_l = (x @ W_l + b_l).reshape(N, H, C)
        x_r = (x @ W_r + b_r).reshape(N, H, C)
        e = x_l[src] + x_r[dst] + (ea @ W_e).reshape(-1, H, C)
        e = jnp.where(e > 0, e, NEG_SLOPE * e)
        logits = jnp.einsum('ehc,hc->eh', e, att)
        m = jax.ops.segment_max(logits, dst, num_segments=N)
        a = jnp.exp(logits - m[dst])
        denom = jax.ops.segment_sum(a, dst, num_segments=N)
        alpha = a / denom[dst]
        out = jax.ops.segment_sum(x_l[src] * alpha[..., None], dst, num_segments=N)
        out = out.reshape(N, H * C)
        out = out + x @ W_res + bias
        return jax.nn.elu(out)

    def _L0_ffn_ref(x, W_gat, att_src, att_dst, b_gat, ln_gamma, ln_beta, W1, b1, W2, b2, edge_index):
        import jax, jax.numpy as jnp
        import numpy as np
        B, N, D = (16, 512, 256)
        NUM_EXPERTS, TOP_K, HEADS = (4, 2, 4)
        N_EDGES = 131072
        LN_EPS = 1e-05

        def _layernorm(x, g, b):
            mu = x.mean(-1, keepdims=True)
            var = ((x - mu) ** 2).mean(-1, keepdims=True)
            return (x - mu) * jax.lax.rsqrt(var + LN_EPS) * g + b

        def _forward(x, edge_index, W_gat, att_src, att_dst, b_gat, ln_gamma, ln_beta, W1, b1, W2, b2):
            Bc, Nc, Dc = x.shape
            M = Bc * Nc
            x_flat = x.reshape(M, Dc)
            h = (x_flat @ W_gat).reshape(M, HEADS, NUM_EXPERTS)
            loops = jnp.arange(M, dtype=edge_index.dtype)
            src = jnp.concatenate([edge_index[0], loops])
            dst = jnp.concatenate([edge_index[1], loops])
            a_src = (h * att_src).sum(-1)
            a_dst = (h * att_dst).sum(-1)
            e = jax.nn.leaky_relu(a_src[src] + a_dst[dst], negative_slope=0.2)
            e_max = jax.ops.segment_max(e, dst, num_segments=M)
            ee = jnp.exp(e - e_max[dst])
            denom = jax.ops.segment_sum(ee, dst, num_segments=M)
            alpha = ee / (denom[dst] + 1e-16)
            msg = h[src] * alpha[:, :, None]
            agg = jax.ops.segment_sum(msg, dst, num_segments=M).reshape(M, HEADS * NUM_EXPERTS) + b_gat
            scores = _layernorm(agg, ln_gamma, ln_beta).reshape(M, HEADS, NUM_EXPERTS).mean(1)
            scores = scores.reshape(Bc, Nc, NUM_EXPERTS)
            topk_s, topk_i = jax.lax.top_k(scores, TOP_K)
            w = jax.nn.softmax(topk_s, axis=-1)
            out = jnp.zeros_like(x)
            for ei in range(NUM_EXPERTS):
                g = jnp.where(topk_i == ei, w, 0.0).sum(-1)
                hh = jax.nn.gelu(x @ W1[ei] + b1[ei], approximate=False)
                out = out + g[..., None] * (hh @ W2[ei] + b2[ei])
            return out
        return _forward(x, edge_index, W_gat, att_src, att_dst, b_gat, ln_gamma, ln_beta, W1, b1, W2, b2)
    edge_index = jnp.stack([src, dst])
    x = x + _L0_gnn_ref(_layernorm(x, axis=-1), edge_index, edge_attr_16, L0_gnn_W_l, L0_gnn_b_l, L0_gnn_W_r, L0_gnn_b_r, L0_gnn_W_e, L0_gnn_att, L0_gnn_W_res, L0_gnn_bias)
    x = x + _L0_ffn_ref(_layernorm(x, axis=-1)[None], L0_ffn_W_gat, L0_ffn_att_src, L0_ffn_att_dst, L0_ffn_b_gat, L0_ffn_ln_gamma, L0_ffn_ln_beta, L0_ffn_W1, L0_ffn_b1, L0_ffn_W2, L0_ffn_b2, L0_ffn_edge_index)[0]
    return x

_drawn_inputs = setup_inputs


def setup_inputs(seed=0):
    import zlib

    import numpy as np

    out = dict(_drawn_inputs(seed))
    spreads = {'L0_gnn_b_l': (0.0, 0.1),
     'L0_gnn_b_r': (0.0, 2.0),
     'L0_gnn_bias': (0.0, 0.1),
     'L0_ffn_b_gat': (0.0, 0.1),
     'L0_ffn_ln_gamma': (1.0, 0.2),
     'L0_ffn_ln_beta': (0.0, 0.309),
     'L0_ffn_b1': (0.0, 0.1),
     'L0_ffn_b2': (0.0, 0.1)}
    factors = {'edge_attr_16': 7.097,
     'L0_gnn_W_r': 4.851,
     'L0_gnn_W_e': 8.0,
     'L0_ffn_att_src': 3.983,
     'L0_ffn_att_dst': 6.229}
    for name, (base, spread) in spreads.items():
        noise = np.random.default_rng([zlib.crc32(name.encode()), seed]).standard_normal(out[name].shape)
        drawn = base * np.exp(spread * noise) if base else spread * noise
        out[name] = jnp.asarray(drawn.astype(out[name].dtype))
    for name, factor in factors.items():
        out[name] = (out[name] * factor).astype(out[name].dtype)
    return out
```

```python
import numpy as np
from contextlib import ExitStack
import concourse.bass as bass
from concourse import mybir

F32 = mybir.dt.float32
BF16 = mybir.dt.bfloat16
I32 = mybir.dt.int32
ALU = mybir.AluOpType
ACT = mybir.ActivationFunctionType
AX = mybir.AxisListType

P = 128
N = 6250
NW = 50
NP = NW * P
D = 256
H = 4
C = D // H
ED = 16
NX = 4
FF = 512
HX = H * NX
EG = 200000
EF = 131072 + N
U = 8
HALF = U // 2


def tiles_for(edges):
    return -(-edges // (P * U)) * U


NTG = tiles_for(EG)
NTF = tiles_for(EF)
KG = -(-(NTG + NW - 1) // U) * U
KF = -(-(NTF + NW - 1) // U) * U
BIG = 1e30
EPS = 1e-5
SLOPE = 0.2
ROW = 2 + 4 + 4 + ED + 1 + D
RV = ROW - D
CG = ROW - 2
CF = H + HX
HI = 64


class Stage:

    def __init__(self, nc, name):
        self.nc, self.name, self.ctx, self.used = nc, name, ExitStack(), []

    def __enter__(self):
        return self

    def __exit__(self, *a):
        self.ctx.__exit__(*a)
        self.nc.clear_and_free_semaphores(self.used)
        self.nc.all_engine_barrier()

    def sb(self, name, shape, dt=F32):
        return self.ctx.enter_context(self.nc.sbuf_tensor(f"{self.name}_{name}", shape, dt))

    def ps(self, name, shape, dt=F32):
        t = self.ctx.enter_context(self.nc.psum_tensor(f"{self.name}_{name}", [shape[0], 512], dt))
        if len(shape) == 2:
            return t[:, 0:shape[1]]
        return t[:, 0:shape[1] * shape[2]].rearrange("p (a b) -> p a b", a=shape[1])

    def sem(self, name):
        self.used.append(self.nc.alloc_semaphore(f"{self.name}_{name}"))
        return self.used[-1]

    def sems(self, name, n):
        return [self.sem(f"{name}{j}") for j in range(n)]

    def block(self):
        return self.ctx.enter_context(self.nc.Block())


class Chain:

    def __init__(self, sem):
        self.sem, self.n = sem, 0

    def __call__(self, eng, ins):
        self.n += 1
        ins.then_inc(self.sem, 1)
        eng.wait_ge(self.sem, self.n)


def node_projections(nc, x, w_cat, b_cat, xl_d, xr_d, res_d, ident_in):
    with Stage(nc, "proj") as s:
        ticks, ticks_sp = s.sem("ticks"), s.sem("ticks_sp")
        w = s.sb("w", [P, 2, 3 * D])
        bias = s.sb("bias", [P, 3 * D])
        ident = s.sb("ident", [P, P])
        eps = s.sb("eps", [P, 1])
        xt = s.sb("x", [P, 2, D])
        st = s.sb("st", [P, 2, 6])
        mv = s.sb("mv", [P, 2, 2])
        sd = s.sb("sd", [P, 2])
        rs = s.sb("rs", [P, 2])
        y = s.sb("y", [P, 2, D])
        yT = s.sb("yT", [P, 2, 2, P])
        o = s.sb("o", [P, 2, 3 * D])
        pT = [s.ps(f"pT{u}", [P, 2, P]) for u in range(2)]
        pA = [s.ps(f"pA{u}", [P, 2 * D]) for u in range(2)]
        pB = [s.ps(f"pB{u}", [P, D]) for u in range(2)]
        consts = s.sem("consts")
        eps_set = s.sem("eps_set")
        loaded, stats, aggr, rooted, inverted, normed, turned, copied, products, summed, stored = (
            s.sems(n, 2) for n in ("loaded", "stats", "aggr", "rooted", "inverted", "normed", "turned",
                                   "copied", "products", "summed", "stored"))
        block = s.block()

        @block.sync
        def _(sp):
            sp.dma_start(w[:, :, :], w_cat.rearrange("(c p) n -> p c n", p=P)).then_inc(consts, 16)
            sp.dma_start(bias[:, :], b_cat.to_broadcast([P, 3 * D])).then_inc(consts, 16)
            sp.dma_start(ident[:, :], ident_in).then_inc(consts, 16)
            for u in range(2):
                sp.sem_inc(normed[u], 1)
            with sp.Fori(0, NW // 2) as i:
                for u in range(2):
                    sp.wait_ge(normed[u], i + 1)
                    sp.sem_inc(ticks_sp, 1)
                    sp.dma_start(xt[:, u, :], x[bass.ds((i * 2 + u) * P, P), :]).then_inc(loaded[u], 16)
            for u in range(2):
                sp.wait_ge(stored[u], 48 * (NW // 2 + 1))

        @block.vector
        def _(v):
            nc.vector.memset(eps[:, :], EPS).then_inc(eps_set, 1)
            v.wait_ge(consts, 48)
            with v.Fori(0, NW // 2) as i:
                for u in range(2):
                    v.wait_ge(loaded[u], (i + 1) * 16)
                    nc.vector.bn_stats(st[:, u, :], xt[:, u, :]).then_inc(stats[u], 1)
                for u in range(2):
                    v.wait_ge(stats[u], i + 1)
                    v.sem_inc(ticks, 1)
                    nc.vector.bn_aggr(mv[:, u, :], st[:, u, :]).then_inc(aggr[u], 1)
                for u in range(2):
                    v.wait_ge(rooted[u], i + 1)
                    nc.vector.reciprocal(rs[:, u:u + 1], sd[:, u:u + 1]).then_inc(inverted[u], 1)
                for u in range(2):
                    v.wait_ge(inverted[u], i + 1)
                    v.wait_ge(turned[u], i + 1)
                    nc.vector.tensor_scalar(y[:, u, :], xt[:, u, :], mv[:, u, 0:1], rs[:, u:u + 1],
                                            ALU.subtract, ALU.mult).then_inc(normed[u], 1)
                for u in range(2):
                    v.wait_ge(products[u], i + 1)
                    v.wait_ge(stored[u], (i + 1) * 48)
                    nc.vector.tensor_tensor(o[:, u, 0:2 * D], pA[u][:, :], bias[:, 0:2 * D], ALU.add)
                    nc.vector.tensor_tensor(o[:, u, 2 * D:], pB[u][:, :], bias[:, 2 * D:], ALU.add)\
                        .then_inc(summed[u], 1)

        @block.scalar
        def _(act):
            act.wait_ge(eps_set, 1)
            for u in range(2):
                act.sem_inc(stored[u], 48)
            with act.Fori(0, NW // 2) as i:
                for u in range(2):
                    act.wait_ge(aggr[u], i + 1)
                    nc.scalar.activation(sd[:, u:u + 1], mv[:, u, 1:2], ACT.Sqrt, bias=eps[:, 0:1])\
                        .then_inc(rooted[u], 1)
                for u in range(2):
                    act.wait_ge(turned[u], i + 2)
                    nc.scalar.copy(yT[:, u, :, :], pT[u][:, :, :]).then_inc(copied[u], 1)
                for u in range(2):
                    act.wait_ge(summed[u], i + 1)
                    at = bass.ds((i * 2 + u) * P, P)
                    act.dma_start(xl_d[at, :], o[:, u, 0:D]).then_inc(stored[u], 16)
                    act.dma_start(xr_d[at, :], o[:, u, D:2 * D]).then_inc(stored[u], 16)
                    act.dma_start(res_d[at, :], o[:, u, 2 * D:]).then_inc(stored[u], 16)

        @block.tensor
        def _(pe):
            pe.wait_ge(consts, 48)
            for u in range(2):
                pe.sem_inc(turned[u], 1)
            with pe.Fori(0, NW // 2) as i:
                for u in range(2):
                    pe.wait_ge(normed[u], i + 2)
                    nc.tensor.transpose(pT[u][:, 0, :], y[:, u, 0:P], ident[:, :])
                    nc.tensor.transpose(pT[u][:, 1, :], y[:, u, P:], ident[:, :]).then_inc(turned[u], 1)
                for u in range(2):
                    pe.wait_ge(copied[u], i + 1)
                    for c in range(2):
                        nc.tensor.matmul(pA[u][:, :], yT[:, u, c, :], w[:, c, 0:2 * D],
                                         start=(c == 0), stop=(c == 1))
                    for c in range(2):
                        last = nc.tensor.matmul(pB[u][:, :], yT[:, u, c, :], w[:, c, 2 * D:],
                                                start=(c == 0), stop=(c == 1))
                    last.then_inc(products[u], 1)


def edge_logits(nc, idx_d, eaT_d, w_e, att_bc, xl_d, xr_d, logit_d):
    with Stage(nc, "logit") as s:
        ticks, ticks_sp = s.sem("ticks"), s.sem("ticks_sp")
        we = s.sb("we", [ED, D])
        att = s.sb("att", [P, D])
        idx = s.sb("idx", [P, 2, 2, HALF], I32)
        ea = s.sb("ea", [ED, 2, HALF * P])
        xl = s.sb("xl", [P, U, D])
        xr = s.sb("xr", [P, U, D])
        lg = s.sb("lg", [P, U, H])
        pe_out = [s.ps(f"p{u}", [P, D]) for u in range(U)]
        consts = s.sem("consts")
        steps = s.sem("steps")
        loaded, half_done, stored = (s.sems(n, 2) for n in ("loaded", "half_done", "stored"))
        got_l, got_r, edge_part, sum1, sum2, leaky, scaled, reduced = (
            s.sems(n, U) for n in ("got_l", "got_r", "edge_part", "sum1", "sum2", "leaky", "scaled", "reduced"))
        block = s.block()

        @block.sync
        def _(sp):
            sp.dma_start(we[:, :], w_e).then_inc(consts, 16)
            sp.dma_start(att[:, :], att_bc.to_broadcast([P, D])).then_inc(consts, 16)
            with sp.Fori(0, NTG // U) as i:
                for h in range(2):
                    sp.wait_ge(half_done[h], i + 1)
                    sp.sem_inc(ticks_sp, 1)
                    sp.dma_start(idx[:, h, :, :], idx_d[bass.ds(i * 2 + h, 1), :, :]
                                 .rearrange("o p n -> (o p) n")).then_inc(loaded[h], 16)
                    sp.dma_start(ea[:, h, :], eaT_d[:, bass.ds((i * 2 + h) * HALF * P, HALF * P)])\
                        .then_inc(loaded[h], 16)

        @block.gpsimd
        def _(pool):
            for u in range(U):
                pool.sem_inc(reduced[u], 1)
            with pool.Fori(0, NTG // U) as i:
                for u in range(U):
                    h, t = divmod(u, HALF)
                    if t == 0:
                        pool.wait_ge(loaded[h], (i + 1) * 32)
                    pool.wait_ge(reduced[u], i + 1)
                    pool.sem_inc(steps, 1)
                    for tab, to, k, got in ((xl_d, xl, 0, got_l), (xr_d, xr, 1, got_r)):
                        pool.indirect_dma_start(
                            out=to[:, u, :], out_offset=None, in_=tab,
                            in_offset=bass.IndirectOffsetOnAxis(ap=idx[:, h, k, t:t + 1], axis=0))\
                            .then_inc(got[u], 16)

        @block.tensor
        def _(pe):
            pe.wait_ge(consts, 32)
            with pe.Fori(0, NTG // U) as i:
                for u in range(U):
                    h, t = divmod(u, HALF)
                    if t == 0:
                        pe.wait_ge(loaded[h], (i + 1) * 32)
                    pe.wait_ge(reduced[u], i + 1)
                    nc.tensor.matmul(pe_out[u][:, :], ea[:, h, t * P:(t + 1) * P], we[:, :],
                                     start=True, stop=True).then_inc(edge_part[u], 1)

        @block.vector
        def _(v):
            v.wait_ge(consts, 32)
            for h in range(2):
                v.sem_inc(half_done[h], 1)
            with v.Fori(0, NTG // U) as i:
                for k in range(U + 4):
                    if k < U:
                        u = k
                        v.wait_ge(edge_part[u], i + 1)
                        v.wait_ge(got_l[u], (i + 1) * 16)
                        nc.vector.tensor_tensor(xl[:, u, :], xl[:, u, :], pe_out[u][:, :], ALU.add)\
                            .then_inc(sum1[u], 1)
                    if 0 <= k - 1 < U:
                        u = k - 1
                        v.wait_ge(got_r[u], (i + 1) * 16)
                        v.wait_ge(sum1[u], i + 1)
                        nc.vector.tensor_tensor(xl[:, u, :], xl[:, u, :], xr[:, u, :], ALU.add)\
                            .then_inc(sum2[u], 1)
                        if u % HALF == HALF - 1:
                            v.sem_inc(half_done[u // HALF], 1)
                    if 0 <= k - 2 < U:
                        u = k - 2
                        v.wait_ge(sum2[u], i + 1)
                        nc.vector.scalar_tensor_tensor(xl[:, u, :], xl[:, u, :], SLOPE, xl[:, u, :],
                                                       ALU.mult, ALU.max).then_inc(leaky[u], 1)
                    if 0 <= k - 3 < U:
                        u = k - 3
                        v.wait_ge(leaky[u], i + 1)
                        nc.vector.tensor_tensor(xl[:, u, :], xl[:, u, :], att[:, :], ALU.mult)\
                            .then_inc(scaled[u], 1)
                    if 0 <= k - 4 < U:
                        u = k - 4
                        v.wait_ge(scaled[u], i + 1)
                        if u % HALF == 0:
                            v.wait_ge(stored[u // HALF], (i + 1) * 16)
                        nc.vector.tensor_reduce(lg[:, u, :], xl[:, u, :].rearrange("p (h c) -> p h c", h=H),
                                                AX.X, ALU.add).then_inc(reduced[u], 1)

        @block.scalar
        def _(act):
            for h in range(2):
                act.sem_inc(stored[h], 16)
            with act.Fori(0, NTG // U) as i:
                for h in range(2):
                    act.wait_ge(reduced[h * HALF + HALF - 1], i + 2)
                    act.dma_start(logit_d[bass.ds((i * 2 + h) * HALF * P, HALF * P), :]
                                  .rearrange("(t p) c -> p t c", p=P), lg[:, h * HALF:(h + 1) * HALF, :])\
                        .then_inc(stored[h], 16)
            for h in range(2):
                act.wait_ge(stored[h], 16 * (NTG // U + 1))


def segment_max(nc, name, nt, dst_halo, src_lin, logit_d, rec_d, carry_d, back_d):
    with Stage(nc, name) as s:
        ticks, ticks_sp = s.sem("ticks"), s.sem("ticks_sp")
        words = 2 + 2 * H if src_lin is not None else 1 + H
        oa = words - H * (2 if src_lin is not None else 1)
        width = dst_halo.shape[1]
        dh = s.sb("dst", [P, (nt + 2) * width], I32)
        dv = dh[:, :].rearrange("p (n w) -> p n w", w=width)[:, :, width - 1]
        sl = s.sb("src", [P, nt], I32)
        L = s.sb("L", [P, nt, H])
        F = s.sb("F", [P, nt, H])
        B = s.sb("B", [P, nt])
        pf = s.sb("pf", [P, nt])
        pb = s.sb("pb", [P, nt])
        rec = s.sb("rec", [P, nt, words])
        ends = s.sb("ends", [P, 2 * H + 2])
        endT = s.sb("endT", [H, 2, P])
        path = s.sb("path", [H, 2, P])
        Z = s.sb("Z", [H, 2, P + 2])
        carry = s.sb("carry", [P, 2, H])
        loads, dve, moved, expd, out = (s.sem(n) for n in ("loads", "dve", "moved", "expd", "out"))
        block = s.block()
        marks = {}

        @block.vector
        def _(v):
            step = Chain(dve)
            v.wait_ge(loads, 16 * (3 if src_lin is not None else 2))
            cur = dv[:, 1:nt + 1]
            step(v, nc.vector.tensor_tensor(pf[:, :], dv[:, 0:nt], cur, ALU.not_equal))
            step(v, nc.vector.tensor_scalar(pf[:, :], pf[:, :], -BIG, None, ALU.mult))
            step(v, nc.vector.tensor_tensor(pb[:, :], dv[:, 2:nt + 2], cur, ALU.not_equal))
            step(v, nc.vector.tensor_scalar(pb[:, :], pb[:, :], -BIG, None, ALU.mult))
            step(v, nc.vector.tensor_copy(rec[:, :, oa - 1], cur))
            if src_lin is not None:
                step(v, nc.vector.tensor_copy(rec[:, :, 0].bitcast(I32), sl[:, :]))
            for h in range(H):
                step(v, nc.vector.tensor_tensor_scan(F[:, :, h], pf[:, :], L[:, :, h], -BIG, ALU.add, ALU.max))
                step(v, nc.vector.tensor_tensor_scan(B[:, ::-1], pb[:, ::-1], L[:, ::-1, h], -BIG,
                                                     ALU.add, ALU.max))
                step(v, nc.vector.tensor_copy(ends[:, h:h + 1], F[:, nt - 1, h:h + 1]))
                step(v, nc.vector.tensor_copy(ends[:, H + h:H + h + 1], B[:, 0:1]))
            step(v, nc.vector.tensor_tensor(ends[:, 2 * H:2 * H + 1], dv[:, 0:1], dv[:, nt:nt + 1], ALU.not_equal))
            step(v, nc.vector.tensor_tensor(ends[:, 2 * H + 1:2 * H + 2], dv[:, 1:2], dv[:, nt + 1:nt + 2],
                                            ALU.not_equal))
            step(v, nc.vector.tensor_scalar(ends[:, 2 * H:], ends[:, 2 * H:], -BIG, None, ALU.mult))
            step(v, nc.vector.memset(Z[:, :, :], -BIG))
            marks["ends"] = step.n
            v.wait_ge(moved, 16 * 5)
            step(v, nc.vector.tensor_tensor_scan(Z[:, 0, 1:P + 1], path[:, 0, :], endT[:, 0, :], -BIG,
                                                 ALU.add, ALU.max))
            step(v, nc.vector.tensor_tensor_scan(Z[:, 1, P:0:-1], path[:, 1, ::-1], endT[:, 1, ::-1], -BIG,
                                                 ALU.add, ALU.max))
            marks["carry"] = step.n
            v.wait_ge(moved, 16 * 9)
            for h in range(H):
                step(v, nc.vector.tensor_tensor_scan(F[:, :, h], pf[:, :], L[:, :, h], carry[:, 0, h:h + 1],
                                                     ALU.add, ALU.max))
                step(v, nc.vector.tensor_tensor_scan(B[:, ::-1], pb[:, ::-1], L[:, ::-1, h],
                                                     carry[:, 1, h:h + 1], ALU.add, ALU.max))
                step(v, nc.vector.tensor_tensor(B[:, :], B[:, :], F[:, :, h], ALU.max))
                step(v, nc.vector.tensor_tensor(L[:, :, h], L[:, :, h], B[:, :], ALU.subtract))
                if src_lin is not None:
                    step(v, nc.vector.scalar_tensor_tensor(rec[:, :, oa + H + h], pb[:, :], 0.0, B[:, :],
                                                           ALU.is_lt, ALU.mult))
            marks["all"] = step.n

        @block.scalar
        def _(act):
            act.wait_ge(dve, marks["all"])
            nc.scalar.activation(rec[:, :, oa:oa + H], L[:, :, :], ACT.Exp).then_inc(expd, 1)

        @block.sync
        def _(sp):
            rows = bass.AP(tensor=dst_halo.tensor, offset=dst_halo.offset,
                           ap=[[nt * width, P], [1, (nt + 2) * width]])
            sp.dma_start(dh[:, :], rows).then_inc(loads, 16)
            sp.dma_start(L[:, :, :], logit_d.rearrange("(p n) h -> p n h", p=P)).then_inc(loads, 16)
            if src_lin is not None:
                sp.dma_start(sl[:, :], src_lin.rearrange("(p n) -> p n", p=P)).then_inc(loads, 16)
            sp.wait_ge(dve, marks["ends"])
            sp.dma_start(carry_d, ends[:, :]).then_inc(moved, 16)
            sp.wait_ge(moved, 16)
            with nc.allow_non_contiguous_dma(reason="512 ends, turned"):
                for k in range(2):
                    sp.dma_start(endT[:, k, :], carry_d[:, k * H:(k + 1) * H].rearrange("p h -> h p"))\
                        .then_inc(moved, 16)
                    sp.dma_start(path[:, k, :], carry_d[:, 2 * H + k:2 * H + k + 1].rearrange("p o -> o p")
                                 .to_broadcast([H, P])).then_inc(moved, 16)
            sp.wait_ge(dve, marks["carry"])
            sp.dma_start(back_d[0, :, :], Z[:, 0, 0:P]).then_inc(moved, 16)
            sp.dma_start(back_d[1, :, :], Z[:, 1, 2:P + 2]).then_inc(moved, 16)
            sp.wait_ge(moved, 16 * 7)
            with nc.allow_non_contiguous_dma(reason="512 ends, turned back"):
                for k in range(2):
                    sp.dma_start(carry[:, k, :], back_d[k, :, :].rearrange("h p -> p h")).then_inc(moved, 16)
            sp.wait_ge(expd, 1)
            sp.dma_start(rec_d.rearrange("(p n) w -> p n w", p=P), rec[:, :, :]).then_inc(out, 16)
            sp.wait_ge(out, 16)


def worklist(nc, name, nt, nk, last_d, key_d, tile_d, win_d, kval_in):
    with Stage(nc, name) as s:
        ticks, ticks_sp = s.sem("ticks"), s.sem("ticks_sp")
        NB = kval_in.shape[1]
        li = s.sb("li", [1, nt], I32)
        wf = s.sb("wf", [1, nt])
        tf = s.sb("tf", [1, nt])
        key = s.sb("key", [P, nt])
        junk = s.sb("junk", [P, nt])
        kv = s.sb("kv", [P, NB])
        tk = s.sb("tk", [P, NB])
        wk = s.sb("wk", [P, NB])
        far = s.sb("far", [P, NB])
        ti = s.sb("ti", [P, 2, NB], I32)
        wm = s.sb("wm", [P, NB])
        dve, moved, tiled = s.sem("dve"), s.sem("moved"), s.sem("tiled")
        block = s.block()
        marks = {}

        @block.gpsimd
        def _(pool):
            nc.gpsimd.iota(tf[:, :], [[1, nt]], base=0, channel_multiplier=0,
                           allow_small_or_imprecise_dtypes=True).then_inc(tiled, 1)

        @block.vector
        def _(v):
            step = Chain(dve)
            v.wait_ge(moved, 32)
            v.wait_ge(tiled, 1)
            step(v, nc.vector.tensor_scalar(li[:, :], li[:, :], 7, None, ALU.arith_shift_right))
            step(v, nc.vector.tensor_scalar(wf[:, :], li[:, :], float(NW - 1), None, ALU.min))
            step(v, nc.vector.tensor_tensor(wf[:, :], wf[:, :], tf[:, :], ALU.add))
            marks["key"] = step.n
            v.wait_ge(moved, 64)
            for b in range(NB):
                step(v, nc.vector.tensor_scalar(junk[:, :], key[:, :], kv[:, b:b + 1], None, ALU.is_lt,
                                                ALU.add, accum_out=tk[:, b:b + 1]))
            step(v, nc.vector.tensor_scalar(tk[:, :], tk[:, :], float(nt - 1), None, ALU.min))
            step(v, nc.vector.tensor_tensor(wk[:, :], kv[:, :], tk[:, :], ALU.subtract))
            step(v, nc.vector.tensor_scalar(far[:, :], wk[:, :], float(NW), 1e6, ALU.is_ge, ALU.mult))
            step(v, nc.vector.tensor_scalar(wm[:, :], wk[:, :], float(P), None, ALU.mult))
            step(v, nc.vector.tensor_tensor(wm[:, :], wm[:, :], far[:, :], ALU.add))
            step(v, nc.vector.tensor_copy(ti[:, 0, :], tk[:, :]))
            step(v, nc.vector.tensor_scalar(ti[:, 1, :], wk[:, :], float(NW - 1), None, ALU.min))
            marks["all"] = step.n

        @block.sync
        def _(sp):
            with nc.allow_non_contiguous_dma(reason="one word of a tile or pair"):
                sp.dma_start(li[:, :], last_d).then_inc(moved, 16)
                sp.dma_start(kv[:, :], kval_in).then_inc(moved, 16)
                sp.wait_ge(dve, marks["key"])
                sp.dma_start(key_d, wf[:, :]).then_inc(moved, 16)
                sp.wait_ge(moved, 48)
                sp.dma_start(key[:, :], key_d.to_broadcast([P, nt])).then_inc(moved, 16)
                sp.wait_ge(dve, marks["all"])
                for j in range(2):
                    sp.dma_start(tile_d[j, :].rearrange("(b p) -> p b", p=P), ti[:, j, :]).then_inc(moved, 16)
                sp.dma_start(win_d[0, :].rearrange("(b p) -> p b", p=P), wm[:, :]).then_inc(moved, 16)
            sp.wait_ge(moved, 64 + 48)


def aggregate(nc, name, s, nt, nk, acc, cols, tile_d, win_d, iota_in, load, gather, weigh, rhs, dst_col, loads_per):
    iota = s.sb("iota", [P, P])
    wb = s.sb("wb", [P, nk])
    tt = s.sb("tt", [1, 2, nk], I32)
    hot = s.sb("hot", [P, U, P])
    part = [s.ps(f"part{u}", [P, 512]) for u in range(U)]
    ticks_sp = s.sem("ticks_agg")
    consts, cleared, steps = s.sem("consts"), s.sem("cleared"), s.sem("steps")
    loaded, gathered, hotted, weighed, summed, added = (
        s.sems(n, U) for n in ("loaded", "gathered", "hotted", "weighed", "summed", "added"))
    block = s.block()

    @block.sync
    def _(sp):
        sp.dma_start(iota[:, :], iota_in.to_broadcast([P, P])).then_inc(consts, 16)
        sp.dma_start(wb[:, :], win_d[:, 0:nk].to_broadcast([P, nk])).then_inc(consts, 16)
        sp.dma_start(tt[0:1, :, :], tile_d[:, 0:nk].rearrange("(o j) n -> o j n", o=1)).then_inc(consts, 16)
        sp.wait_ge(consts, 48)
        with sp.Fori(0, nk // U) as i:
            for u in range(U):
                t = sp.value_load(tt[0:1, 0, bass.ds(i * U + u, 1)], min_val=0, max_val=nt - 1)
                sp.wait_ge(summed[u], i + 1)
                sp.sem_inc(ticks_sp, 1)
                load(sp, u, t, loaded[u])

    if gather is not None:
        @block.gpsimd
        def _(pool):
            for u in range(U):
                pool.sem_inc(weighed[u], 1)
            with pool.Fori(0, nk // U) as i:
                for u in range(U):
                    pool.wait_ge(loaded[u], (i + 1) * 16 * loads_per)
                    pool.wait_ge(weighed[u], i + 1)
                    pool.sem_inc(steps, 1)
                    gather(pool, u).then_inc(gathered[u], 16)

    @block.tensor
    def _(pe):
        for u in range(U):
            pe.sem_inc(summed[u], 1)
        with pe.Fori(0, nk // U) as i:
            for u in range(U):
                pe.wait_ge(weighed[u], i + (2 if gather is not None else 1))
                pe.wait_ge(hotted[u], i + 1)
                pe.wait_ge(added[u], i + 1)
                nc.tensor.matmul(part[u][:, 0:cols], hot[:, u, :], rhs(u), start=True, stop=True)\
                    .then_inc(summed[u], 1)

    @block.vector
    def _(v):
        nc.vector.memset(acc[:, :, :], 0.0).then_inc(cleared, 1)
        for u in range(U):
            v.sem_inc(added[u], 1)
        v.wait_ge(consts, 48)
        v.wait_ge(cleared, 1)
        with v.Fori(0, nk // U) as i:
            def add(u):
                w = v.value_load(tt[0:1, 1, bass.ds(i * U + u, 1)], min_val=0, max_val=NW - 1)
                v.wait_ge(summed[u], i + 2)
                if u == 0:
                    v.wait_ge(added[U - 1], i + 1)
                else:
                    v.wait_ge(added[u - 1], i + 2)
                nc.vector.tensor_tensor(acc[:, bass.ds(w, 1), :].rearrange("p o n -> p (o n)"),
                                        acc[:, bass.ds(w, 1), :].rearrange("p o n -> p (o n)"),
                                        part[u][:, 0:cols], ALU.add).then_inc(added[u], 1)

            for u in range(U):
                v.wait_ge(loaded[u], (i + 1) * 16 * loads_per)
                v.wait_ge(summed[u], i + 1)
                nc.vector.tensor_scalar(hot[:, u, :], iota[:, :], wb[:, bass.ds(i * U + u, 1)], dst_col(u),
                                        ALU.add, ALU.is_equal).then_inc(hotted[u], 1)
                if gather is not None:
                    v.wait_ge(gathered[u], (i + 1) * 16)
                weigh(u).then_inc(weighed[u], 1)
                if u >= 2:
                    add(u - 2)
            add(U - 2)
            add(U - 1)


def aggregate_nodes(nc, acc, rec_d, ea_d, xl_d, tile_d, win_d, iota_in):
    with Stage(nc, "aggr") as s:
        ticks, ticks_sp = s.sem("ticks"), s.sem("ticks_sp")
        row = s.sb("row", [P, U, ROW])
        xg = s.sb("xg", [P, U, D])
        ones = s.sem("ones")
        with nc.Block() as block:
            @block.vector
            def _(v):
                nc.vector.memset(row[:, :, RV - 1:RV], 1.0).then_inc(ones, 1)
                v.wait_ge(ones, 1)

        def load(sp, u, t, loaded):
            at = bass.ds(t * P, P)
            sp.dma_start(row[:, u, 0:2 + 2 * H], rec_d[at, :]).then_inc(loaded, 16)
            sp.dma_start(row[:, u, 2 + 2 * H:RV - 1], ea_d[at, :]).then_inc(loaded, 16)

        def gather(pool, u):
            return pool.indirect_dma_start(
                out=xg[:, u, :], out_offset=None, in_=xl_d,
                in_offset=bass.IndirectOffsetOnAxis(ap=row[:, u, 0:1].bitcast(I32), axis=0))

        def weigh(u):
            return nc.vector.tensor_tensor(
                row[:, u, RV:].rearrange("p (h c) -> p h c", h=H), xg[:, u, :].rearrange("p (h c) -> p h c", h=H),
                row[:, u, 2:2 + H].unsqueeze(2).to_broadcast([P, H, C]), ALU.mult)

        aggregate(nc, "aggr", s, NTG, KG, acc, CG, tile_d, win_d, iota_in, load, gather, weigh,
                  lambda u: row[:, u, 2:], lambda u: row[:, u, 1:2], 2)


def aggregate_gate(nc, acc, rec_d, h_d, tile_d, win_d, iota_in):
    with Stage(nc, "gaggr") as s:
        ticks, ticks_sp = s.sem("ticks"), s.sem("ticks_sp")
        row = s.sb("row", [P, U, 1 + CF])
        hv = s.sb("hv", [P, U, HX])

        def load(sp, u, t, loaded):
            at = bass.ds(t * P, P)
            sp.dma_start(row[:, u, 0:1 + H], rec_d[at, :]).then_inc(loaded, 16)
            sp.dma_start(hv[:, u, :], h_d[at, :]).then_inc(loaded, 16)

        def weigh(u):
            return nc.vector.tensor_tensor(
                row[:, u, 1 + H:].rearrange("p (h c) -> p h c", h=H), hv[:, u, :].rearrange("p (h c) -> p h c", h=H),
                row[:, u, 1:1 + H].unsqueeze(2).to_broadcast([P, H, NX]), ALU.mult)

        aggregate(nc, "gaggr", s, NTF, KF, acc, CF, tile_d, win_d, iota_in, load, None, weigh,
                  lambda u: row[:, u, 1:], lambda u: row[:, u, 0:1], 2)


def nodes_after(nc, acc, xl_d, xr_d, res_d, x_d, w_e, att_bc, w_gat, asrc_bc, adst_bc, x2_d, yT_d, tab_d, ad_d,
                ident_in):
    with Stage(nc, "after") as s:
        ticks, ticks_sp = s.sem("ticks"), s.sem("ticks_sp")
        we = s.sb("we", [ED, D])
        wg = s.sb("wg", [P, 2, HX])
        att = s.sb("att", [P, D])
        asr = s.sb("asr", [P, 2, HX])
        ident = s.sb("ident", [P, P])
        eps = s.sb("eps", [P, 1])
        xl = s.sb("xl", [P, 2, D])
        xr = s.sb("xr", [P, 2, D])
        rs = s.sb("res", [P, 2, D])
        xx = s.sb("x", [P, 2, D])
        la = s.sb("la", [P, NW, ED])
        las = s.sb("las", [P, 2, ED])
        laT = s.sb("laT", [ED, 2, P])
        cnt = s.sb("cnt", [P, NW])
        ml = s.sb("ml", [P, NW, H])
        slf = s.sb("slf", [P, NW, H])
        mx = s.sb("mx", [P, NW, H])
        c1 = s.sb("c1", [P, NW, H])
        c2 = s.sb("c2", [P, NW, H])
        den = s.sb("den", [P, NW, H])
        t = s.sb("t", [P, 2, D])
        q = s.sb("q", [P, 2, D])
        st = s.sb("st", [P, 2, 6])
        mv = s.sb("mv", [P, 2, 2])
        sd = s.sb("sd", [P, 2])
        rq = s.sb("rq", [P, 2])
        yT = s.sb("yT", [P, 2, 2, P])
        tab = s.sb("tab", [P, 2, H + HX])
        pr = s.sb("pr", [P, 2, 2, HX])
        ad = s.sb("ad", [P, 2, H])
        pL = [s.ps(f"pL{u}", [ED, P]) for u in range(2)]
        pE = [s.ps(f"pE{u}", [P, D]) for u in range(2)]
        pT = [s.ps(f"pT{u}", [P, 2, P]) for u in range(2)]
        pH = [s.ps(f"pH{u}", [P, HX]) for u in range(2)]
        consts, dve, expd = s.sem("consts"), s.sem("dve"), s.sem("expd")
        counts = {}

        def sems(names):
            for n in names.split():
                counts[n] = s.sems(n, 2)
            return counts

        S = sems("loaded picked turned copied edge s1 s2 s3 s4 s5")
        with nc.Block() as block:
            @block.sync
            def _(sp):
                sp.dma_start(we[:, :], w_e).then_inc(consts, 16)
                sp.dma_start(att[:, :], att_bc.to_broadcast([P, D])).then_inc(consts, 16)
                sp.dma_start(ident[:, :], ident_in).then_inc(consts, 16)
                sp.dma_start(wg[:, :, :], w_gat.rearrange("(c p) n -> p c n", p=P)).then_inc(consts, 16)
                sp.dma_start(asr[:, 0, :], asrc_bc.to_broadcast([P, HX])).then_inc(consts, 16)
                sp.dma_start(asr[:, 1, :], adst_bc.to_broadcast([P, HX])).then_inc(consts, 16)
                with sp.Fori(0, NW // 2) as i:
                    for u in range(2):
                        at = bass.ds((i * 2 + u) * P, P)
                        sp.wait_ge(S["s5"][u], i + 1)
                        sp.sem_inc(ticks_sp, 1)
                        sp.dma_start(xl[:, u, :], xl_d[at, :]).then_inc(S["loaded"][u], 16)
                        sp.dma_start(xr[:, u, :], xr_d[at, :]).then_inc(S["loaded"][u], 16)

            @block.vector
            def _(v):
                step = Chain(dve)
                step(v, nc.vector.memset(eps[:, :], EPS))
                step(v, nc.vector.tensor_scalar(cnt[:, :], acc[:, :, 2 * H + ED], 1.0, None, ALU.max))
                step(v, nc.vector.reciprocal(cnt[:, :], cnt[:, :]))
                step(v, nc.vector.tensor_tensor(la[:, :, :], acc[:, :, 2 * H:2 * H + ED],
                                                cnt[:, :].unsqueeze(2).to_broadcast([P, NW, ED]), ALU.mult))
                for u in range(2):
                    v.sem_inc(S["s5"][u], 1)
                v.wait_ge(consts, 96)
                with v.Fori(0, NW // 2) as i:
                    for u in range(2):
                        v.wait_ge(S["edge"][u], i + 1)
                        v.wait_ge(S["loaded"][u], (i + 1) * 32)
                        nc.vector.tensor_tensor(t[:, u, :], xl[:, u, :], pE[u][:, :], ALU.add)\
                            .then_inc(S["s1"][u], 1)
                    for u in range(2):
                        v.wait_ge(S["s1"][u], i + 1)
                        nc.vector.tensor_tensor(t[:, u, :], t[:, u, :], xr[:, u, :], ALU.add)\
                            .then_inc(S["s2"][u], 1)
                    for u in range(2):
                        v.wait_ge(S["s2"][u], i + 1)
                        nc.vector.scalar_tensor_tensor(t[:, u, :], t[:, u, :], SLOPE, t[:, u, :],
                                                       ALU.mult, ALU.max).then_inc(S["s3"][u], 1)
                    for u in range(2):
                        v.wait_ge(S["s3"][u], i + 1)
                        nc.vector.tensor_tensor(t[:, u, :], t[:, u, :], att[:, :], ALU.mult)\
                            .then_inc(S["s4"][u], 1)
                    for u in range(2):
                        v.wait_ge(S["s4"][u], i + 1)
                        nc.vector.tensor_reduce(
                            slf[:, bass.ds(i * 2 + u, 1), :].rearrange("p o h -> p (o h)"),
                            t[:, u, :].rearrange("p (h c) -> p h c", h=H), AX.X, ALU.add)\
                            .then_inc(S["s5"][u], 1)
                v.wait_ge(S["s5"][1], NW // 2 + 1)
                step(v, nc.vector.tensor_scalar(cnt[:, :], acc[:, :, 2 * H + ED], 0.0, -BIG, ALU.is_equal, ALU.mult))
                step(v, nc.vector.tensor_tensor(ml[:, :, :], acc[:, :, H:2 * H],
                                                cnt[:, :].unsqueeze(2).to_broadcast([P, NW, H]), ALU.add))
                step(v, nc.vector.tensor_tensor(mx[:, :, :], ml[:, :, :], slf[:, :, :], ALU.max))
                step(v, nc.vector.tensor_tensor(ml[:, :, :], ml[:, :, :], mx[:, :, :], ALU.subtract))
                step(v, nc.vector.tensor_tensor(slf[:, :, :], slf[:, :, :], mx[:, :, :], ALU.subtract))
                counts["shifted"] = step.n
                v.wait_ge(expd, 2)
                step(v, nc.vector.tensor_tensor(den[:, :, :], acc[:, :, 0:H], c1[:, :, :], ALU.mult))
                step(v, nc.vector.tensor_tensor(den[:, :, :], den[:, :, :], c2[:, :, :], ALU.add))
                step(v, nc.vector.reciprocal(den[:, :, :], den[:, :, :]))
                step(v, nc.vector.tensor_tensor(c1[:, :, :], c1[:, :, :], den[:, :, :], ALU.mult))
                step(v, nc.vector.tensor_tensor(c2[:, :, :], c2[:, :, :], den[:, :, :], ALU.mult))

            @block.tensor
            def _(pe):
                pe.wait_ge(consts, 96)
                pe.wait_ge(dve, 4)
                with pe.Fori(0, NW // 2) as i:
                    for u in range(2):
                        pe.wait_ge(S["picked"][u], i + 1)
                        nc.tensor.transpose(pL[u][:, :], las[:, u, :], ident[:, :]).then_inc(S["turned"][u], 1)
                    for u in range(2):
                        pe.wait_ge(S["copied"][u], i + 1)
                        pe.wait_ge(S["s5"][u], i + 1)
                        nc.tensor.matmul(pE[u][:, :], laT[:, u, :], we[:, :], start=True, stop=True)\
                            .then_inc(S["edge"][u], 1)

            @block.scalar
            def _(act):
                act.wait_ge(dve, 4)
                for u in range(2):
                    act.sem_inc(S["edge"][u], 1) if False else None
                with act.Fori(0, NW // 2) as i:
                    for u in range(2):
                        act.wait_ge(S["s5"][u], i + 1)
                        nc.scalar.copy(las[:, u, :], la[:, bass.ds(i * 2 + u, 1), :]
                                       .rearrange("p o n -> p (o n)")).then_inc(S["picked"][u], 1)
                    for u in range(2):
                        act.wait_ge(S["turned"][u], i + 1)
                        nc.scalar.copy(laT[:, u, :], pL[u][:, :]).then_inc(S["copied"][u], 1)
                act.wait_ge(dve, counts["shifted"])
                nc.scalar.activation(c1[:, :, :], ml[:, :, :], ACT.Exp).then_inc(expd, 1)
                nc.scalar.activation(c2[:, :, :], slf[:, :, :], ACT.Exp).then_inc(expd, 1)

        R = {n: s.sems(f"b_{n}", 2) for n in ("loaded", "w", "wl", "o", "o2", "mn", "ex", "m1", "el", "x2",
                                              "st", "ag", "sq", "rc", "y", "turn", "cp", "h", "hc", "pr", "tb",
                                              "store")}
        with nc.Block() as block:
            @block.sync
            def _(sp):
                for u in range(2):
                    sp.sem_inc(R["loaded"][u], 64)
                with sp.Fori(0, NW // 2) as i:
                    for u in range(2):
                        at = bass.ds((i * 2 + u) * P, P)
                        sp.wait_ge(R["y"][u], i + 1)
                        sp.sem_inc(ticks_sp, 1)
                        sp.wait_ge(R["store"][u], (i + 1) * 64)
                        sp.sem_inc(ticks_sp, 1)
                        sp.dma_start(xl[:, u, :], xl_d[at, :]).then_inc(R["loaded"][u], 16)
                        sp.dma_start(rs[:, u, :], res_d[at, :]).then_inc(R["loaded"][u], 16)
                        sp.dma_start(xx[:, u, :], x_d[at, :]).then_inc(R["loaded"][u], 16)
                    for u in range(2):
                        at = bass.ds((i * 2 + u) * P, P)
                        sp.wait_ge(R["tb"][u], i + 1)
                        sp.sem_inc(ticks_sp, 1)
                        sp.dma_start(tab_d[at, :], tab[:, u, :]).then_inc(R["store"][u], 16)
                        sp.dma_start(ad_d[at, :], ad[:, u, :]).then_inc(R["store"][u], 16)
                for u in range(2):
                    sp.wait_ge(R["store"][u], 64 * (NW // 2 + 1))

            @block.vector
            def _(v):
                for u in range(2):
                    v.sem_inc(R["y"][u], 1)
                with v.Fori(0, NW // 2) as i:
                    def each(first, fn, done):
                        for u in range(2):
                            for sem, plus in first:
                                v.wait_ge(R[sem][u], (i + plus) if sem not in ("loaded", "store") else
                                          (i + plus) * (48 if sem == "loaded" else 64))
                            if done == "ag":
                                v.sem_inc(ticks, 1)
                            fn(u).then_inc(R[done][u], 1)

                    def win(buf, lo, hi):
                        return lambda u: buf[:, bass.ds(i * 2 + u, 1), lo:hi].rearrange("p o n -> p (o n)")

                    def heads(ap):
                        return ap.rearrange("p (h c) -> p h c", h=H)

                    tt = nc.vector.tensor_tensor
                    values, w1, w2 = win(acc, CG - D, CG), win(c1, 0, H), win(c2, 0, H)
                    each([("y", 1)], lambda u: tt(
                        heads(t[:, u, :]), heads(values(u)), w1(u).unsqueeze(2).to_broadcast([P, H, C]),
                        ALU.mult), "w")
                    for u in range(2):
                        v.wait_ge(R["loaded"][u], (i + 1) * 48 + 64)
                        tt(heads(q[:, u, :]), heads(xl[:, u, :]), w2(u).unsqueeze(2).to_broadcast([P, H, C]),
                           ALU.mult).then_inc(R["wl"][u], 1)
                    each([("w", 1), ("wl", 1)], lambda u: tt(t[:, u, :], t[:, u, :], q[:, u, :], ALU.add), "o")
                    each([("o", 1)], lambda u: tt(t[:, u, :], t[:, u, :], rs[:, u, :], ALU.add), "o2")
                    each([("o2", 1)], lambda u: nc.vector.tensor_scalar(q[:, u, :], t[:, u, :], 0.0, None, ALU.min), "mn")
                    each([("o2", 1)], lambda u: nc.vector.tensor_scalar(t[:, u, :], t[:, u, :], 0.0, -1.0, ALU.max,
                                                                        ALU.add), "m1")
                    each([("ex", 1), ("m1", 1)], lambda u: tt(t[:, u, :], t[:, u, :], q[:, u, :], ALU.add), "el")
                    each([("el", 1), ("store", 1)], lambda u: tt(xx[:, u, :], xx[:, u, :], t[:, u, :], ALU.add), "x2")
                    each([("x2", 1)], lambda u: nc.vector.bn_stats(st[:, u, :], xx[:, u, :]), "st")
                    each([("st", 1)], lambda u: nc.vector.bn_aggr(mv[:, u, :], st[:, u, :]), "ag")
                    each([("sq", 1)], lambda u: nc.vector.reciprocal(rq[:, u:u + 1], sd[:, u:u + 1]), "rc")
                    each([("rc", 1), ("turn", 1)], lambda u: nc.vector.tensor_scalar(
                        q[:, u, :], xx[:, u, :], mv[:, u, 0:1], rq[:, u:u + 1], ALU.subtract, ALU.mult), "y")
                    each([("h", 1)], lambda u: nc.vector.tensor_copy(tab[:, u, H:], pH[u][:, :]), "hc")
                    each([("hc", 1)], lambda u: tt(
                        pr[:, u, :, :], asr[:, :, :], tab[:, u, H:].unsqueeze(1).to_broadcast([P, 2, HX]),
                        ALU.mult), "pr")
                    for u in range(2):
                        v.wait_ge(R["pr"][u], i + 1)
                        nc.vector.tensor_reduce(tab[:, u, 0:H], pr[:, u, 0, :].rearrange("p (h c) -> p h c", h=H),
                                                AX.X, ALU.add)
                        nc.vector.tensor_reduce(ad[:, u, :], pr[:, u, 1, :].rearrange("p (h c) -> p h c", h=H),
                                                AX.X, ALU.add).then_inc(R["tb"][u], 1)

            @block.scalar
            def _(act):
                for u in range(2):
                    act.sem_inc(R["store"][u], 64)
                with act.Fori(0, NW // 2) as i:
                    for u in range(2):
                        act.wait_ge(R["mn"][u], i + 1)
                        nc.scalar.activation(q[:, u, :], q[:, u, :], ACT.Exp).then_inc(R["ex"][u], 1)
                    for u in range(2):
                        act.wait_ge(R["x2"][u], i + 1)
                        act.dma_start(x2_d[bass.ds((i * 2 + u) * P, P), :], xx[:, u, :]).then_inc(R["store"][u], 16)
                    for u in range(2):
                        act.wait_ge(R["ag"][u], i + 1)
                        nc.scalar.activation(sd[:, u:u + 1], mv[:, u, 1:2], ACT.Sqrt, bias=eps[:, 0:1])\
                            .then_inc(R["sq"][u], 1)
                    for u in range(2):
                        act.wait_ge(R["turn"][u], i + 2)
                        act.wait_ge(R["store"][u], (i + 1) * 64)
                        nc.scalar.copy(yT[:, u, :, :], pT[u][:, :, :]).then_inc(R["cp"][u], 1)
                    for u in range(2):
                        act.wait_ge(R["cp"][u], i + 1)
                        act.dma_start(yT_d[bass.ds(i * 2 + u, 1), :, :].rearrange("o p n -> (o p) n"),
                                      yT[:, u, :, :].rearrange("p c n -> p (c n)")).then_inc(R["store"][u], 16)

            @block.tensor
            def _(pe):
                for u in range(2):
                    pe.sem_inc(R["turn"][u], 1)
                with pe.Fori(0, NW // 2) as i:
                    for u in range(2):
                        pe.wait_ge(R["y"][u], i + 2)
                        nc.tensor.transpose(pT[u][:, 0, :], q[:, u, 0:P], ident[:, :])
                        nc.tensor.transpose(pT[u][:, 1, :], q[:, u, P:], ident[:, :]).then_inc(R["turn"][u], 1)
                    for u in range(2):
                        pe.wait_ge(R["cp"][u], i + 1)
                        for c in range(2):
                            last = nc.tensor.matmul(pH[u][:, :], yT[:, u, c, :], wg[:, c, :],
                                                    start=(c == 0), stop=(c == 1))
                        last.then_inc(R["h"][u], 1)


def sort_by_destination(nc, dst_tab, dst_lin, rec_in, sorted_d, ident_in, iota_in, tri_in, part_in):
    with Stage(nc, "sort") as s:
        ticks, ticks_sp = s.sem("ticks"), s.sem("ticks_sp")
        iota = s.sb("iota", [P, P])
        ident = s.sb("ident", [P, P])
        tri = s.sb("tri", [P, P])
        part = s.sb("part", [P, 1])
        ones = s.sb("ones", [P, P])
        dt_i = s.sb("dt_i", [P, NTF], I32)
        tmp_i = s.sb("tmp_i", [P, NTF], I32)
        lo = s.sb("lo", [P, NTF])
        hi = s.sb("hi", [P, NTF])
        hot_lo = s.sb("hot_lo", [P, 2, HALF, P], BF16)
        hot_hi = s.sb("hot_hi", [P, 2, HALF, HI], BF16)
        drow = s.sb("drow", [P, 2, HALF * P], I32)
        lrow = s.sb("lrow", [P, 2, HALF * P], I32)
        hot_t = s.sb("hot_t", [P, 2, HALF * P])
        same = s.sb("same", [P, U, P], BF16)
        cnt0 = s.sb("cnt0", [P, HI])
        tot = s.sb("tot", [P, HI])
        base = s.sb("base", [P, HI])
        cur = s.sb("cur", [P, 2, HI])
        junk = s.sb("junk", [P, U, HI])
        pos = s.sb("pos", [P, U])
        posi = s.sb("posi", [P, U], I32)
        rec = s.sb("rec", [P, 2, HALF, 2], I32)
        edge = s.sb("edge", [1, 2, 2], I32)
        pc = s.ps("pc", [P, 512])
        pr = s.ps("pr", [P, 512])
        pl = [s.ps(f"pl{u}", [P, 512]) for u in range(4)]
        pn = [s.ps(f"pn{u}", [P, HI]) for u in range(2)]
        consts, dve, pef, tabled = s.sem("consts"), s.sem("dve"), s.sem("pef"), s.sem("tabled")
        ended = s.sem("ended")
        first_hot, first_used = s.sems("first_hot", 2), s.sems("first_used", 2)
        GROUPS = NTF // U
        marks = {}

        def one_hots(h, tile0):
            at = bass.ds(tile0, HALF)
            nc.vector.tensor_tensor(hot_lo[:, h, :, :], lo[:, at].unsqueeze(2).to_broadcast([P, HALF, P]),
                                    iota[:, :].unsqueeze(1).to_broadcast([P, HALF, P]), ALU.is_equal)
            return nc.vector.tensor_tensor(
                hot_hi[:, h, :, :], hi[:, at].unsqueeze(2).to_broadcast([P, HALF, HI]),
                iota[:, 0:HI].unsqueeze(1).to_broadcast([P, HALF, HI]), ALU.is_equal)

        with nc.Block() as block:
            @block.sync
            def _(sp):
                sp.dma_start(iota[:, :], iota_in.to_broadcast([P, P])).then_inc(consts, 16)
                sp.dma_start(ident[:, :], ident_in).then_inc(consts, 16)
                sp.dma_start(tri[:, :], tri_in).then_inc(consts, 16)
                sp.dma_start(part[:, :], part_in).then_inc(consts, 16)
                sp.dma_start(dt_i[:, :], dst_tab).then_inc(consts, 16)
                sp.wait_ge(dve, 1)
                sp.dma_start(sorted_d[0:1, :], edge[:, 0, :]).then_inc(ended, 16)
                sp.dma_start(sorted_d[NTF * P + 1:, :], edge[:, 1, :]).then_inc(ended, 16)
                sp.wait_ge(ended, 32)

            @block.vector
            def _(v):
                step = Chain(dve)
                step(v, nc.vector.memset(edge[:, :, :], -1))
                step(v, nc.vector.memset(ones[:, :], 1.0))
                step(v, nc.vector.memset(cnt0[:, :], 0.0))
                marks["zeroed"] = step.n
                v.wait_ge(consts, 80)
                step(v, nc.vector.tensor_scalar(tmp_i[:, :], dt_i[:, :], P - 1, None, ALU.bitwise_and))
                step(v, nc.vector.tensor_copy(lo[:, :], tmp_i[:, :]))
                step(v, nc.vector.tensor_scalar(tmp_i[:, :], dt_i[:, :], 7, None, ALU.arith_shift_right))
                step(v, nc.vector.tensor_copy(hi[:, :], tmp_i[:, :]))
                for h in range(2):
                    v.sem_inc(first_used[h], 1)
                with v.Fori(0, GROUPS) as i:
                    for h in range(2):
                        v.wait_ge(first_used[h], i + 1)
                        one_hots(h, i * U + h * HALF).then_inc(first_hot[h], 1)
                v.wait_ge(pef, 1)
                step(v, nc.vector.tensor_copy(cnt0[:, :], pc[:, 0:HI]))
                marks["counted"] = step.n
                v.wait_ge(pef, 3)
                step(v, nc.vector.tensor_copy(tot[:, :], pr[:, 0:HI]))
                step(v, nc.vector.tensor_tensor_scan(base[:, :], ones[:, 0:HI], tot[:, :], 0.0, ALU.mult, ALU.add))
                step(v, nc.vector.tensor_tensor(base[:, :], base[:, :], tot[:, :], ALU.subtract))
                step(v, nc.vector.tensor_scalar(base[:, :], base[:, :], 1.0, None, ALU.add))
                step(v, nc.vector.tensor_tensor(cur[:, 0, :], base[:, :], pr[:, 128:128 + HI], ALU.add))

            @block.tensor
            def _(pe):
                pe.wait_ge(consts, 80)
                pe.wait_ge(dve, marks["zeroed"])
                nc.tensor.matmul(pc[:, 0:HI], ident[:, :], cnt0[:, :], start=True, stop=False)
                with pe.Fori(0, GROUPS) as i:
                    for h in range(2):
                        pe.wait_ge(first_hot[h], i + 1)
                        for k in range(HALF):
                            last = nc.tensor.matmul(pc[:, 0:HI], hot_lo[:, h, k, :], hot_hi[:, h, k, :],
                                                    start=False, stop=False)
                        last.then_inc(first_used[h], 1)
                nc.tensor.matmul(pc[:, 0:HI], ident[:, :], cnt0[:, :], start=False, stop=True).then_inc(pef, 1)
                pe.wait_ge(dve, marks["counted"])
                nc.tensor.matmul(pr[:, 0:HI], ones[:, :], cnt0[:, :], start=True, stop=True).then_inc(pef, 1)
                nc.tensor.matmul(pr[:, 128:128 + HI], tri[:, :], cnt0[:, :], start=True, stop=True)\
                    .then_inc(pef, 1)

        loaded, low, hots, placed_half = (s.sems(f"r_{n}", 2) for n in ("loaded", "low", "hots", "placed_half"))
        sames, counted, looked, summed, placed, wrote, current = (
            s.sems(f"r_{n}", U) for n in ("sames", "counted", "looked", "summed", "placed", "wrote", "current"))
        freed = s.sems("r_freed", 2)
        steps = s.sem("steps")
        with nc.Block() as block:
            @block.sync
            def _(sp):
                with sp.Fori(0, GROUPS) as i:
                    for h in range(2):
                        sp.wait_ge(placed_half[h], i + 1)
                        sp.sem_inc(ticks_sp, 1)
                        sp.wait_ge(freed[h], i + 1)
                        sp.sem_inc(ticks_sp, 1)
                        sp.dma_start(drow[:, h, :], dst_lin[:, bass.ds((i * 2 + h) * HALF * P, HALF * P)]
                                     .to_broadcast([P, HALF * P])).then_inc(loaded[h], 16)
                        sp.dma_start(rec[:, h, :, :], rec_in[bass.ds(i * 2 + h, 1), :, :]
                                     .rearrange("o p n -> (o p) n")).then_inc(loaded[h], 16)

            @block.vector
            def _(v):
                for h in range(2):
                    v.sem_inc(placed_half[h], 1)
                for u in range(U):
                    v.sem_inc(placed[u], 1)
                with v.Fori(0, GROUPS) as i:
                    def place(u):
                        h, k = divmod(u, HALF)
                        v.wait_ge(looked[u], i + 2)
                        nc.vector.tensor_tensor(junk[:, u, :], pl[u % 4][:, 0:HI], hot_hi[:, h, k, :],
                                                ALU.mult).then_inc(sames[u], 1)
                        v.wait_ge(sames[u], i * 3 + 2)
                        nc.vector.tensor_reduce(pos[:, u:u + 1], junk[:, u, :], AX.X, ALU.add)\
                            .then_inc(sames[u], 1)
                        v.wait_ge(sames[u], i * 3 + 3)
                        v.wait_ge(freed[h], i + 1)
                        nc.vector.tensor_copy(posi[:, u:u + 1], pos[:, u:u + 1]).then_inc(placed[u], 1)

                    for h in range(2):
                        v.wait_ge(loaded[h], (i + 1) * 32)
                        for u in range(h * HALF, (h + 1) * HALF):
                            v.wait_ge(looked[u], i + 1)
                        nc.vector.tensor_scalar(lrow[:, h, :], drow[:, h, :], P - 1, None, ALU.bitwise_and)\
                            .then_inc(low[h], 1)
                        one_hots(h, i * U + h * HALF).then_inc(hots[h], 1)
                        v.wait_ge(low[h], i + 1)
                        nc.vector.tensor_scalar(hot_t[:, h, :], lrow[:, h, :], part[:, 0:1], None, ALU.is_equal)
                        for k in range(HALF):
                            u = h * HALF + k
                            nc.vector.scalar_tensor_tensor(
                                same[:, u, :], lrow[:, h, k * P:(k + 1) * P], lo[:, bass.ds(i * U + u, 1)],
                                tri[:, :], ALU.is_equal, ALU.mult).then_inc(sames[u], 1)
                        for k in range(HALF):
                            place(h * HALF + k)
                        v.sem_inc(placed_half[h], 1)

            @block.tensor
            def _(pe):
                for u in range(U):
                    pe.sem_inc(looked[u], 1)
                with pe.Fori(0, GROUPS) as i:
                    for u in range(U):
                        h, k = divmod(u, HALF)
                        if k == 0:
                            pe.wait_ge(hots[h], i + 1)
                        pe.wait_ge(current[u], i + 1)
                        nc.tensor.matmul(pn[u % 2][:, :], ident[:, :], cur[:, u % 2, :], start=True, stop=False)
                        nc.tensor.matmul(pn[u % 2][:, :], hot_lo[:, h, k, :], hot_hi[:, h, k, :],
                                         start=False, stop=True).then_inc(counted[u], 1)
                        pe.wait_ge(sames[u], i * 3 + 1)
                        pe.wait_ge(placed[(u - 4) % U], i + (2 if u >= 4 else 1))
                        nc.tensor.matmul(pl[u % 4][:, 0:HI], hot_t[:, h, k * P:(k + 1) * P], cur[:, u % 2, :],
                                         start=True, stop=False)
                        nc.tensor.matmul(pl[u % 4][:, 0:HI], same[:, u, :], hot_hi[:, h, k, :],
                                         start=False, stop=True).then_inc(looked[u], 1)

            @block.scalar
            def _(act):
                act.sem_inc(current[0], 1)
                with act.Fori(0, GROUPS) as i:
                    for u in range(U):
                        act.wait_ge(counted[u], i + 1)
                        act.wait_ge(looked[(u - 1) % U], i + (2 if u >= 1 else 1))
                        nc.scalar.copy(cur[:, (u + 1) % 2, :], pn[u % 2][:, :]).then_inc(current[(u + 1) % U], 1)

            @block.gpsimd
            def _(pool):
                for h in range(2):
                    pool.sem_inc(freed[h], 1)
                with pool.Fori(0, GROUPS) as i:
                    for u in range(U):
                        h, k = divmod(u, HALF)
                        pool.wait_ge(loaded[h], (i + 1) * 32)
                        pool.wait_ge(placed[u], i + 2)
                        pool.sem_inc(steps, 1)
                        pool.indirect_dma_start(
                            out=sorted_d, out_offset=bass.IndirectOffsetOnAxis(ap=posi[:, u:u + 1], axis=0),
                            in_=rec[:, h, k, :], in_offset=None).then_inc(wrote[u], 16)
                    for h in range(2):
                        for k in range(HALF):
                            pool.wait_ge(wrote[h * HALF + k], (i + 1) * 16)
                        pool.sem_inc(freed[h], 1)


def gate_logits(nc, sorted_d, tab_d, ad_d, logit_d, h_d):
    with Stage(nc, "gate") as s:
        ticks, ticks_sp = s.sem("ticks"), s.sem("ticks_sp")
        raw = s.sb("raw", [P, 2, HALF, 2], I32)
        idx = s.sb("idx", [P, 2, HALF, 2], I32)
        tg = s.sb("tg", [P, U, H + HX])
        ag = s.sb("ag", [P, U, H])
        lg = s.sb("lg", [P, U, H])
        steps = s.sem("steps")
        loaded, clamped, taken, sum_, leaky, stored = (
            s.sems(n, 2) for n in ("loaded", "clamped", "taken", "sum", "leaky", "stored"))
        got = s.sems("got", U)
        block = s.block()

        @block.sync
        def _(sp):
            with sp.Fori(0, NTF // U) as i:
                for h in range(2):
                    sp.wait_ge(clamped[h], i + 1)
                    sp.sem_inc(ticks_sp, 1)
                    at = bass.ds((i * 2 + h) * HALF * P + 1, HALF * P)
                    sp.dma_start(raw[:, h, :, :], sorted_d[at, :].rearrange("(t p) w -> p t w", p=P))\
                        .then_inc(loaded[h], 16)

        @block.vector
        def _(v):
            for h in range(2):
                v.sem_inc(clamped[h], 1)
            with v.Fori(0, NTF // U) as i:
                for h in range(2):
                    v.wait_ge(loaded[h], (i + 1) * 16)
                    nc.vector.tensor_scalar(idx[:, h, :, :], raw[:, h, :, :], float(N - 1), None, ALU.min)\
                        .then_inc(clamped[h], 1)
                for h in range(2):
                    at = slice(h * HALF, (h + 1) * HALF)
                    for k in range(HALF):
                        v.wait_ge(got[h * HALF + k], (i + 1) * 32)
                    v.wait_ge(stored[h], (i + 1) * 32)
                    nc.vector.tensor_tensor(ag[:, at, :], ag[:, at, :], tg[:, at, 0:H], ALU.add)\
                        .then_inc(sum_[h], 1)
                for h in range(2):
                    at = slice(h * HALF, (h + 1) * HALF)
                    v.wait_ge(sum_[h], i + 1)
                    nc.vector.scalar_tensor_tensor(lg[:, at, :], ag[:, at, :], SLOPE, ag[:, at, :],
                                                   ALU.mult, ALU.max).then_inc(leaky[h], 1)

        @block.gpsimd
        def _(pool):
            with pool.Fori(0, NTF // U) as i:
                for h in range(2):
                    pool.wait_ge(clamped[h], i + 2)
                    pool.wait_ge(stored[h], (i + 1) * 32)
                    pool.wait_ge(leaky[h], i + 1)
                    pool.sem_inc(steps, 1)
                    for k in range(HALF):
                        u = h * HALF + k
                        pool.indirect_dma_start(
                            out=tg[:, u, :], out_offset=None, in_=tab_d,
                            in_offset=bass.IndirectOffsetOnAxis(ap=idx[:, h, k, 0:1], axis=0)).then_inc(got[u], 16)
                        pool.indirect_dma_start(
                            out=ag[:, u, :], out_offset=None, in_=ad_d,
                            in_offset=bass.IndirectOffsetOnAxis(ap=idx[:, h, k, 1:2], axis=0)).then_inc(got[u], 16)

        @block.scalar
        def _(act):
            for h in range(2):
                act.sem_inc(stored[h], 32)
                act.sem_inc(leaky[h], 1)
            with act.Fori(0, NTF // U) as i:
                for h in range(2):
                    act.wait_ge(leaky[h], i + 2)
                    at = bass.ds((i * 2 + h) * HALF * P, HALF * P)
                    act.dma_start(logit_d[at, :].rearrange("(t p) c -> p t c", p=P),
                                  lg[:, h * HALF:(h + 1) * HALF, :]).then_inc(stored[h], 16)
                    act.dma_start(h_d[at, :].rearrange("(t p) c -> p t c", p=P),
                                  tg[:, h * HALF:(h + 1) * HALF, H:]).then_inc(stored[h], 16)
            for h in range(2):
                act.wait_ge(stored[h], 32 * (NTF // U + 1))


def gate_weights(nc, acc, g, b_gat, gam, bet, below_in):
    with Stage(nc, "gatew") as s:
        ticks, ticks_sp = s.sem("ticks"), s.sem("ticks_sp")
        vec = s.sb("vec", [P, 3, HX])
        below = s.sb("below", [P, NX * NX])
        den = s.sb("den", [P, NW, H])
        a = s.sb("a", [P, NW, HX])
        b = s.sb("b", [P, NW, HX])
        m = s.sb("m", [P, NW])
        r = s.sb("r", [P, NW])
        sc = s.sb("sc", [P, NW, NX])
        cmp = s.sb("cmp", [P, NW, NX, NX])
        eq = s.sb("eq", [P, NW, NX, NX])
        rank = s.sb("rank", [P, NW, NX])
        k1 = s.sb("k1", [P, NW, NX])
        k2 = s.sb("k2", [P, NW, NX])
        s1 = s.sb("s1", [P, NW])
        s2 = s.sb("s2", [P, NW])
        eps = s.sb("eps", [P, 1])
        consts, dve, act_s = s.sem("consts"), s.sem("dve"), s.sem("act")
        block = s.block()
        marks = {}

        @block.sync
        def _(sp):
            for k, src in enumerate((b_gat, gam, bet)):
                sp.dma_start(vec[:, k, :], src.to_broadcast([P, HX])).then_inc(consts, 16)
            sp.dma_start(below[:, :], below_in.to_broadcast([P, NX * NX])).then_inc(consts, 16)

        @block.vector
        def _(v):
            step = Chain(dve)
            tt, ts = nc.vector.tensor_tensor, nc.vector.tensor_scalar

            def row(k):
                return vec[:, k, :].unsqueeze(1).to_broadcast([P, NW, HX])

            def wide(ap, n):
                return ap.unsqueeze(2).to_broadcast([P, NW, n])

            v.wait_ge(consts, 64)
            step(v, nc.vector.memset(eps[:, :], EPS))
            step(v, ts(den[:, :, :], acc[:, :, 0:H], 1e-16, None, ALU.add))
            step(v, nc.vector.reciprocal(den[:, :, :], den[:, :, :]))
            for h in range(H):
                step(v, tt(a[:, :, h * NX:(h + 1) * NX], acc[:, :, H + h * NX:H + (h + 1) * NX],
                           wide(den[:, :, h], NX), ALU.mult))
            step(v, tt(a[:, :, :], a[:, :, :], row(0), ALU.add))
            step(v, nc.vector.tensor_reduce(m[:, :], a[:, :, :], AX.X, ALU.add))
            step(v, ts(m[:, :], m[:, :], 1.0 / HX, None, ALU.mult))
            step(v, tt(a[:, :, :], a[:, :, :], wide(m[:, :], HX), ALU.subtract))
            step(v, tt(b[:, :, :], a[:, :, :], a[:, :, :], ALU.mult))
            step(v, nc.vector.tensor_reduce(r[:, :], b[:, :, :], AX.X, ALU.add))
            step(v, ts(r[:, :], r[:, :], 1.0 / HX, None, ALU.mult))
            marks["var"] = step.n
            v.wait_ge(act_s, 1)
            step(v, nc.vector.reciprocal(r[:, :], r[:, :]))
            step(v, tt(a[:, :, :], a[:, :, :], wide(r[:, :], HX), ALU.mult))
            step(v, tt(a[:, :, :], a[:, :, :], row(1), ALU.mult))
            step(v, tt(a[:, :, :], a[:, :, :], row(2), ALU.add))
            step(v, tt(sc[:, :, :], a[:, :, 0:NX], a[:, :, NX:2 * NX], ALU.add))
            step(v, tt(sc[:, :, :], sc[:, :, :], a[:, :, 2 * NX:3 * NX], ALU.add))
            step(v, tt(sc[:, :, :], sc[:, :, :], a[:, :, 3 * NX:], ALU.add))
            step(v, ts(sc[:, :, :], sc[:, :, :], 1.0 / H, None, ALU.mult))
            for i in range(NX):
                me = wide(sc[:, :, i], NX)
                step(v, tt(cmp[:, :, i, :], sc[:, :, :], me, ALU.is_gt))
                step(v, tt(eq[:, :, i, :], sc[:, :, :], me, ALU.is_equal))
                step(v, tt(eq[:, :, i, :], eq[:, :, i, :],
                           below[:, i * NX:(i + 1) * NX].unsqueeze(1).to_broadcast([P, NW, NX]), ALU.mult))
                step(v, tt(cmp[:, :, i, :], cmp[:, :, i, :], eq[:, :, i, :], ALU.add))
                step(v, nc.vector.tensor_reduce(rank[:, :, i], cmp[:, :, i, :], AX.X, ALU.add))
            step(v, ts(k1[:, :, :], rank[:, :, :], 0.0, None, ALU.is_equal))
            step(v, ts(k2[:, :, :], rank[:, :, :], 1.0, None, ALU.is_equal))
            step(v, tt(a[:, :, 0:NX], sc[:, :, :], k1[:, :, :], ALU.mult))
            step(v, nc.vector.tensor_reduce(s1[:, :], a[:, :, 0:NX], AX.X, ALU.add))
            step(v, tt(a[:, :, 0:NX], sc[:, :, :], k2[:, :, :], ALU.mult))
            step(v, nc.vector.tensor_reduce(s2[:, :], a[:, :, 0:NX], AX.X, ALU.add))
            step(v, tt(s2[:, :], s2[:, :], s1[:, :], ALU.subtract))
            marks["gap"] = step.n
            v.wait_ge(act_s, 2)
            step(v, ts(s1[:, :], s2[:, :], 1.0, None, ALU.add))
            step(v, nc.vector.reciprocal(s1[:, :], s1[:, :]))
            step(v, tt(s2[:, :], s2[:, :], s1[:, :], ALU.mult))
            step(v, tt(k1[:, :, :], k1[:, :, :], wide(s1[:, :], NX), ALU.mult))
            step(v, tt(k2[:, :, :], k2[:, :, :], wide(s2[:, :], NX), ALU.mult))
            step(v, tt(g[:, :, :], k1[:, :, :], k2[:, :, :], ALU.add))

        @block.scalar
        def _(act):
            act.wait_ge(dve, marks["var"])
            nc.scalar.activation(r[:, :], r[:, :], ACT.Sqrt, bias=eps[:, 0:1]).then_inc(act_s, 1)
            act.wait_ge(dve, marks["gap"])
            nc.scalar.activation(s2[:, :], s2[:, :], ACT.Exp).then_inc(act_s, 1)


def experts(nc, g, yT_d, x2_d, w1_d, b1_d, w2_d, b2_d, out_d):
    with Stage(nc, "experts") as s:
        ticks, ticks_sp = s.sem("ticks"), s.sem("ticks_sp")
        FB = FF // P
        w1 = s.sb("w1", [P, 2, NX * FF])
        w2 = s.sb("w2", [P, NX * FB, D])
        b1 = s.sb("b1", [P, NX * FB])
        b2 = s.sb("b2", [P, NX, D])
        yT = s.sb("yT", [P, 2, 2, P])
        x2 = s.sb("x2", [P, 2, D])
        hid = s.sb("hid", [P, NX * FB, 2 * P])
        o = s.sb("o", [P, 2, D])
        pU = [s.ps(f"pU{k}", [P, 512]) for k in range(4)]
        pD = [s.ps(f"pD{k}", [P, 512]) for k in range(4)]
        consts = s.sem("consts")
        loaded, stored, begun = s.sem("loaded"), s.sem("stored"), s.sem("begun")
        up = s.sems("up", NX * FB)
        act_done = s.sems("gelu", NX * FB)
        down = s.sems("down", NX * 2)
        mixed = s.sems("mixed", NX * 2)
        bias_s = s.sems("bias", NX * 2)
        block = s.block()

        @block.sync
        def _(sp):
            for k in range(NX):
                sp.dma_start(w1[:, :, k * FF:(k + 1) * FF], w1_d[k, :, :].rearrange("(c p) n -> p c n", p=P))\
                    .then_inc(consts, 16)
                sp.dma_start(w2[:, k * FB:(k + 1) * FB, :], w2_d[k, :, :].rearrange("(c p) n -> p c n", p=P))\
                    .then_inc(consts, 16)
            sp.dma_start(b1[:, :], b1_d).then_inc(consts, 16)
            sp.dma_start(b2[:, :, :].rearrange("p k n -> p (k n)"), b2_d.to_broadcast([P, NX * D]))\
                .then_inc(consts, 16)
            sp.sem_inc(stored, 16)
            with sp.Fori(0, NW // 2) as i:
                sp.wait_ge(mixed[NX * 2 - 1], i + 1)
                sp.sem_inc(ticks_sp, 1)
                sp.dma_start(yT[:, :, :, :].rearrange("p w c n -> p w (c n)"),
                             yT_d[bass.ds(i * 2, 2), :, :].rearrange("w p n -> p w n")).then_inc(loaded, 16)
                sp.dma_start(x2[:, :, :], x2_d[bass.ds(i * 2 * P, 2 * P), :].rearrange("(w p) n -> p w n", p=P))\
                    .then_inc(loaded, 16)
                sp.wait_ge(mixed[NX * 2 - 1], i + 2)
                sp.sem_inc(ticks_sp, 1)
                sp.dma_start(out_d[bass.ds(i * 2 * P, 2 * P), :].rearrange("(w p) n -> p w n", p=P), o[:, :, :])\
                    .then_inc(stored, 16)
            sp.wait_ge(stored, 16 * (NW // 2 + 1))

        @block.tensor
        def _(pe):
            pe.wait_ge(consts, 160)
            with pe.Fori(0, NW // 2) as i:
                pe.wait_ge(loaded, (i + 1) * 32)

                def rise(e):
                    for f in range(e * FB, (e + 1) * FB):
                        pe.wait_ge(act_done[(f - 4) % (NX * FB)], i + (2 if f >= 4 else 1))
                        for c in range(2):
                            last = nc.tensor.matmul(pU[f % 4][:, 0:2 * P].rearrange("p (w n) -> p w n", w=2),
                                                    w1[:, c, f * P:(f + 1) * P], yT[:, :, c, :],
                                                    start=(c == 0), stop=(c == 1))
                        last.then_inc(up[f], 1)

                def fall(e):
                    for w in range(2):
                        j = e * 2 + w
                        pe.wait_ge(mixed[(j - 4) % (NX * 2)], i + (2 if j >= 4 else 1))
                        for f in range(FB):
                            if w == 0:
                                pe.wait_ge(act_done[e * FB + f], i + 2)
                            last = nc.tensor.matmul(pD[j % 4][:, 0:D], hid[:, e * FB + f, w * P:(w + 1) * P],
                                                    w2[:, e * FB + f, :], start=(f == 0), stop=(f == FB - 1))
                        last.then_inc(down[j], 1)

                rise(0)
                for e in range(1, NX):
                    rise(e)
                    fall(e - 1)
                fall(NX - 1)

        @block.scalar
        def _(act):
            act.wait_ge(consts, 160)
            for f in range(NX * FB):
                act.sem_inc(act_done[f], 1)
            with act.Fori(0, NW // 2) as i:
                for f in range(NX * FB):
                    act.wait_ge(up[f], i + 1)
                    act.wait_ge(mixed[f // FB * 2 + 1], i + 1)
                    nc.scalar.activation(hid[:, f, :], pU[f % 4][:, 0:2 * P], ACT.Gelu, bias=b1[:, f:f + 1])\
                        .then_inc(act_done[f], 1)

        @block.vector
        def _(v):
            v.wait_ge(consts, 160)
            for j in range(NX * 2):
                v.sem_inc(mixed[j], 1)
            with v.Fori(0, NW // 2) as i:
                def gate(e, w):
                    return g[:, bass.ds(i * 2 + w, 1), e:e + 1].rearrange("p o n -> p (o n)")

                v.wait_ge(loaded, (i + 1) * 32)
                v.wait_ge(stored, (i + 1) * 16)
                for e in range(NX):
                    for w in range(2):
                        if e:
                            v.wait_ge(bias_s[(e - 1) * 2 + w], i + 1)
                        nc.vector.scalar_tensor_tensor(o[:, w, :], b2[:, e, :], gate(e, w),
                                                       (o if e else x2)[:, w, :], ALU.mult, ALU.add)\
                            .then_inc(bias_s[e * 2 + w], 1)
                for e in range(NX):
                    for w in range(2):
                        j = e * 2 + w
                        v.wait_ge(down[j], i + 1)
                        if e:
                            v.wait_ge(mixed[j - 2], i + 2)
                        else:
                            v.wait_ge(bias_s[(NX - 1) * 2 + w], i + 1)
                        nc.vector.scalar_tensor_tensor(o[:, w, :], pD[j % 4][:, 0:D], gate(e, w), o[:, w, :],
                                                       ALU.mult, ALU.add).then_inc(mixed[j], 1)


def build(nc, a, out_d):
    def scratch(name, shape, dt=F32):
        return nc.dram_tensor(name, shape, dt, kind="Internal").ap()

    xl_d, xr_d, res_d, x2_d = (scratch(n, (NP, D)) for n in ("xl", "xr", "res", "x2"))
    yT_d = scratch("yT", (NW, P, D))
    tab_d, ad_d = scratch("tab", (NP, H + HX)), scratch("ad", (NP, H))
    lg_d, rec_d = scratch("lg", (NTG * P, H)), scratch("rec", (NTG * P, 2 + 2 * H))
    lf_d, rf_d = scratch("lf", (NTF * P, H)), scratch("rf", (NTF * P, 1 + H))
    h_d = scratch("h", (NTF * P, HX))
    sorted_d = scratch("sorted", (NTF * P + 2, 2), I32)
    ends_d, back_d = scratch("ends", (P, 2 * H + 2)), scratch("back", (2, H, P))
    key_d = scratch("key", (1, NTG))
    KB = -(-max(KG, KF) // P)
    tile_d, win_d = scratch("tile", (2, KB * P), I32), scratch("win", (1, KB * P))

    node_projections(nc, a["x"], a["w_cat"], a["b_cat"], xl_d, xr_d, res_d, a["ident"])
    edge_logits(nc, a["idx"], a["eaT"], a["w_e"], a["att"], xl_d, xr_d, lg_d)
    segment_max(nc, "gmax", NTG, a["dst_halo"], a["src_lin"], lg_d, rec_d, ends_d, back_d)
    worklist(nc, "gwork", NTG, KG, a["last"], key_d, tile_d, win_d, a["kval"])
    with nc.sbuf_tensor("acc", [P, NW, CG], F32) as acc:
        aggregate_nodes(nc, acc, rec_d, a["ea"], xl_d, tile_d, win_d, a["iota"])
        nodes_after(nc, acc, xl_d, xr_d, res_d, a["x"], a["w_e"], a["att"], a["w_gat"], a["att_src"],
                    a["att_dst"], x2_d, yT_d, tab_d, ad_d, a["ident"])
    sort_by_destination(nc, a["f_dst_tab"], a["f_dst_lin"], a["f_rec"], sorted_d, a["ident"], a["iota"],
                        a["tri"], a["part"])
    gate_logits(nc, sorted_d, tab_d, ad_d, lf_d, h_d)
    segment_max(nc, "fmax", NTF, sorted_d, None, lf_d, rf_d, ends_d, back_d)
    last = sorted_d[1:, :].rearrange("(o t) w -> o t w", o=1)
    worklist(nc, "fwork", NTF, KF,
             bass.AP(tensor=sorted_d.tensor, offset=sorted_d.offset + P * 2 + 1, ap=[[1, 1], [P * 2, NTF]]),
             key_d[:, 0:NTF], tile_d, win_d, a["kval"])
    with nc.sbuf_tensor("gates", [P, NW, NX], F32) as g:
        with nc.sbuf_tensor("facc", [P, NW, CF], F32) as facc:
            aggregate_gate(nc, facc, rf_d, h_d, tile_d, win_d, a["iota"])
            gate_weights(nc, facc, g, a["b_gat"], a["gamma"], a["beta"], a["below"])
        experts(nc, g, yT_d, x2_d, a["w1"], a["b1"], a["w2"], a["b2"], out_d)


def lay_out(v):
    def padded(x, n, fill):
        out = np.full((n,) + x.shape[1:], fill, x.dtype)
        out[:x.shape[0]] = x
        return out

    v = {k: np.asarray(x) for k, x in v.items()}
    src = padded(v["src"], NTG * P, 0)
    dst = padded(v["dst"], NTG * P, NP - 1)
    ea = padded(v["edge_attr_16"], NTG * P, 0)
    loops = np.arange(N, dtype=np.int32)
    ei = v["L0_ffn_edge_index"]
    f_src = padded(np.concatenate([ei[0], loops]), NTF * P, 0)
    f_dst = padded(np.concatenate([ei[1], loops]), NTF * P, HI * P - 1)

    def tiles(x):
        return x.reshape(-1, HALF, P).transpose(0, 2, 1)

    row = np.arange(P, dtype=np.float32)
    kb = -(-max(KG, KF) // P)
    return {
        "x": padded(v["x"], NP, 0),
        "w_cat": np.concatenate([v["L0_gnn_W_l"], v["L0_gnn_W_r"], v["L0_gnn_W_res"]], 1),
        "b_cat": np.concatenate([v["L0_gnn_b_l"], v["L0_gnn_b_r"], v["L0_gnn_bias"]])[None],
        "w_e": v["L0_gnn_W_e"], "att": v["L0_gnn_att"].reshape(1, D),
        "idx": np.concatenate([tiles(src), tiles(dst)], 2),
        "eaT": ea.T, "ea": ea, "src_lin": src,
        "dst_halo": np.concatenate([[-1], dst, [-1]]).astype(np.int32)[:, None],
        "last": dst[P - 1::P][None],
        "w_gat": v["L0_ffn_W_gat"], "att_src": v["L0_ffn_att_src"].reshape(1, HX),
        "att_dst": v["L0_ffn_att_dst"].reshape(1, HX), "b_gat": v["L0_ffn_b_gat"][None],
        "gamma": v["L0_ffn_ln_gamma"][None], "beta": v["L0_ffn_ln_beta"][None],
        "w1": v["L0_ffn_W1"], "w2": v["L0_ffn_W2"],
        "b1": v["L0_ffn_b1"].reshape(NX * FF // P, P).T, "b2": v["L0_ffn_b2"].reshape(1, NX * D),
        "f_dst_tab": f_dst.reshape(NTF, P).T, "f_dst_lin": f_dst[None],
        "f_rec": np.stack([tiles(f_src), tiles(f_dst)], 3).reshape(-1, P, HALF * 2),
        "ident": np.eye(P, dtype=np.float32), "iota": row[None], "part": row[:, None],
        "tri": np.triu(np.ones((P, P), np.float32), 1),
        "kval": np.arange(kb * P, dtype=np.float32).reshape(kb, P).T,
        "below": np.tril(np.ones((NX, NX), np.float32), -1).reshape(1, NX * NX),
    }


def kernel(**inputs):
    import concourse.bacc as bacc
    from concourse.bass_utils import run_bass_kernel_spmd as run

    nc = bacc.Bacc("TRN2", target_bir_lowering=False, num_devices=1)
    arrays = {f"in_{k}": np.ascontiguousarray(x) for k, x in lay_out(inputs).items()}
    aps = {k[3:]: nc.dram_tensor(k, x.shape, mybir.dt.from_np(x.dtype), kind="ExternalInput").ap()
           for k, x in arrays.items()}
    out_d = nc.dram_tensor("out", (NP, D), F32, kind="ExternalOutput").ap()
    build(nc, aps, out_d)
    r = run(nc, [arrays], core_ids=[0])
    return r.results[0]["out"][:N]
```

```python
import numpy as np
from contextlib import ExitStack
import concourse.bass as bass
from concourse import mybir

F32 = mybir.dt.float32
BF16 = mybir.dt.bfloat16
I32 = mybir.dt.int32
ALU = mybir.AluOpType
ACT = mybir.ActivationFunctionType
AX = mybir.AxisListType

P = 128
N = 6250
NW = 50
NP = NW * P
D = 256
H = 4
C = D // H
ED = 16
NX = 4
FF = 512
HX = H * NX
EG = 200000
EF = 131072 + N
U = 8
HALF = U // 2


def tiles_for(edges):
    return -(-edges // (P * U)) * U


NTG = tiles_for(EG)
NTF = tiles_for(EF)
KG = -(-(NTG + NW - 1) // U) * U
KF = -(-(NTF + NW - 1) // U) * U
BIG = 1e30
EPS = 1e-5
SLOPE = 0.2
ROW = 2 + 4 + 4 + ED + 1 + D
RV = ROW - D
CG = ROW - 2
CF = H + HX
FROW = H + HX + 1 + H
HI = 64


class Stage:

    def __init__(self, nc, name):
        self.nc, self.name, self.ctx, self.used = nc, name, ExitStack(), []

    def __enter__(self):
        return self

    def __exit__(self, *a):
        self.ctx.__exit__(*a)
        self.nc.clear_and_free_semaphores(self.used)
        self.nc.all_engine_barrier()

    def sb(self, name, shape, dt=F32):
        return self.ctx.enter_context(self.nc.sbuf_tensor(f"{self.name}_{name}", shape, dt))

    def ps(self, name, shape, dt=F32):
        t = self.ctx.enter_context(self.nc.psum_tensor(f"{self.name}_{name}", [shape[0], 512], dt))
        if len(shape) == 2:
            return t[:, 0:shape[1]]
        return t[:, 0:shape[1] * shape[2]].rearrange("p (a b) -> p a b", a=shape[1])

    def sem(self, name):
        self.used.append(self.nc.alloc_semaphore(f"{self.name}_{name}"))
        return self.used[-1]

    def sems(self, name, n):
        return [self.sem(f"{name}{j}") for j in range(n)]

    def block(self):
        return self.ctx.enter_context(self.nc.Block())


class Chain:

    def __init__(self, sem):
        self.sem, self.n = sem, 0

    def __call__(self, eng, ins):
        self.n += 1
        ins.then_inc(self.sem, 1)
        eng.wait_ge(self.sem, self.n)


def node_projections(nc, x, w_cat, b_cat, xl_d, xr_d, res_d, ident_in):
    with Stage(nc, "proj") as s:
        ticks, ticks_sp = s.sem("ticks"), s.sem("ticks_sp")
        w = s.sb("w", [P, 2, 3 * D])
        bias = s.sb("bias", [P, 3 * D])
        ident = s.sb("ident", [P, P])
        eps = s.sb("eps", [P, 1])
        xt = s.sb("x", [P, 2, D])
        st = s.sb("st", [P, 2, 6])
        mv = s.sb("mv", [P, 2, 2])
        sd = s.sb("sd", [P, 2])
        rs = s.sb("rs", [P, 2])
        y = s.sb("y", [P, 2, D])
        yT = s.sb("yT", [P, 2, 2, P])
        o = s.sb("o", [P, 2, 3 * D])
        pT = [s.ps(f"pT{u}", [P, 2, P]) for u in range(2)]
        pA = [s.ps(f"pA{u}", [P, 2 * D]) for u in range(2)]
        pB = [s.ps(f"pB{u}", [P, D]) for u in range(2)]
        consts = s.sem("consts")
        eps_set = s.sem("eps_set")
        loaded, stats, aggr, rooted, inverted, normed, turned, copied, products, summed, stored = (
            s.sems(n, 2) for n in ("loaded", "stats", "aggr", "rooted", "inverted", "normed", "turned",
                                   "copied", "products", "summed", "stored"))
        block = s.block()

        @block.sync
        def _(sp):
            sp.dma_start(w[:, :, :], w_cat.rearrange("(c p) n -> p c n", p=P)).then_inc(consts, 16)
            sp.dma_start(bias[:, :], b_cat.to_broadcast([P, 3 * D])).then_inc(consts, 16)
            sp.dma_start(ident[:, :], ident_in).then_inc(consts, 16)
            for u in range(2):
                sp.sem_inc(normed[u], 1)
            with sp.Fori(0, NW // 2) as i:
                for u in range(2):
                    sp.wait_ge(normed[u], i + 1)
                    sp.sem_inc(ticks_sp, 1)
                    sp.dma_start(xt[:, u, :], x[bass.ds((i * 2 + u) * P, P), :]).then_inc(loaded[u], 16)
            for u in range(2):
                sp.wait_ge(stored[u], 48 * (NW // 2 + 1))

        @block.vector
        def _(v):
            nc.vector.memset(eps[:, :], EPS).then_inc(eps_set, 1)
            v.wait_ge(consts, 48)
            with v.Fori(0, NW // 2) as i:
                for u in range(2):
                    v.wait_ge(loaded[u], (i + 1) * 16)
                    nc.vector.bn_stats(st[:, u, :], xt[:, u, :]).then_inc(stats[u], 1)
                for u in range(2):
                    v.wait_ge(stats[u], i + 1)
                    v.sem_inc(ticks, 1)
                    nc.vector.bn_aggr(mv[:, u, :], st[:, u, :]).then_inc(aggr[u], 1)
                for u in range(2):
                    v.wait_ge(rooted[u], i + 1)
                    nc.vector.reciprocal(rs[:, u:u + 1], sd[:, u:u + 1]).then_inc(inverted[u], 1)
                for u in range(2):
                    v.wait_ge(inverted[u], i + 1)
                    v.wait_ge(turned[u], i + 1)
                    nc.vector.tensor_scalar(y[:, u, :], xt[:, u, :], mv[:, u, 0:1], rs[:, u:u + 1],
                                            ALU.subtract, ALU.mult).then_inc(normed[u], 1)
                for u in range(2):
                    v.wait_ge(products[u], i + 1)
                    v.wait_ge(stored[u], (i + 1) * 48)
                    nc.vector.tensor_tensor(o[:, u, 0:2 * D], pA[u][:, :], bias[:, 0:2 * D], ALU.add)
                    nc.vector.tensor_tensor(o[:, u, 2 * D:], pB[u][:, :], bias[:, 2 * D:], ALU.add)\
                        .then_inc(summed[u], 1)

        @block.scalar
        def _(act):
            act.wait_ge(eps_set, 1)
            for u in range(2):
                act.sem_inc(stored[u], 48)
            with act.Fori(0, NW // 2) as i:
                for u in range(2):
                    act.wait_ge(aggr[u], i + 1)
                    nc.scalar.activation(sd[:, u:u + 1], mv[:, u, 1:2], ACT.Sqrt, bias=eps[:, 0:1])\
                        .then_inc(rooted[u], 1)
                for u in range(2):
                    act.wait_ge(turned[u], i + 2)
                    nc.scalar.copy(yT[:, u, :, :], pT[u][:, :, :]).then_inc(copied[u], 1)
                for u in range(2):
                    act.wait_ge(summed[u], i + 1)
                    at = bass.ds((i * 2 + u) * P, P)
                    act.dma_start(xl_d[at, :], o[:, u, 0:D]).then_inc(stored[u], 16)
                    act.dma_start(xr_d[at, :], o[:, u, D:2 * D]).then_inc(stored[u], 16)
                    act.dma_start(res_d[at, :], o[:, u, 2 * D:]).then_inc(stored[u], 16)

        @block.tensor
        def _(pe):
            pe.wait_ge(consts, 48)
            for u in range(2):
                pe.sem_inc(turned[u], 1)
            with pe.Fori(0, NW // 2) as i:
                for u in range(2):
                    pe.wait_ge(normed[u], i + 2)
                    nc.tensor.transpose(pT[u][:, 0, :], y[:, u, 0:P], ident[:, :])
                    nc.tensor.transpose(pT[u][:, 1, :], y[:, u, P:], ident[:, :]).then_inc(turned[u], 1)
                for u in range(2):
                    pe.wait_ge(copied[u], i + 1)
                    for c in range(2):
                        nc.tensor.matmul(pA[u][:, :], yT[:, u, c, :], w[:, c, 0:2 * D],
                                         start=(c == 0), stop=(c == 1))
                    for c in range(2):
                        last = nc.tensor.matmul(pB[u][:, :], yT[:, u, c, :], w[:, c, 2 * D:],
                                                start=(c == 0), stop=(c == 1))
                    last.then_inc(products[u], 1)


def edge_logits(nc, idx_d, eaT_d, w_e, att_bc, xl_d, xr_d, logit_d):
    with Stage(nc, "logit") as s:
        ticks, ticks_sp = s.sem("ticks"), s.sem("ticks_sp")
        we = s.sb("we", [ED, D])
        att = s.sb("att", [P, D])
        idx = s.sb("idx", [P, 2, 2, HALF], I32)
        ea = s.sb("ea", [ED, 2, HALF * P])
        xl = s.sb("xl", [P, U, D])
        xr = s.sb("xr", [P, U, D])
        lg = s.sb("lg", [P, U, H])
        pe_out = [s.ps(f"p{u}", [P, D]) for u in range(U)]
        consts = s.sem("consts")
        steps = s.sem("steps")
        loaded, half_done, stored = (s.sems(n, 2) for n in ("loaded", "half_done", "stored"))
        got_l, got_r, edge_part, sum1, sum2, leaky, scaled, reduced = (
            s.sems(n, U) for n in ("got_l", "got_r", "edge_part", "sum1", "sum2", "leaky", "scaled", "reduced"))
        block = s.block()

        @block.sync
        def _(sp):
            sp.dma_start(we[:, :], w_e).then_inc(consts, 16)
            sp.dma_start(att[:, :], att_bc.to_broadcast([P, D])).then_inc(consts, 16)
            with sp.Fori(0, NTG // U) as i:
                for h in range(2):
                    sp.wait_ge(half_done[h], i + 1)
                    sp.sem_inc(ticks_sp, 1)
                    sp.dma_start(idx[:, h, :, :], idx_d[bass.ds(i * 2 + h, 1), :, :]
                                 .rearrange("o p n -> (o p) n")).then_inc(loaded[h], 16)
                    sp.dma_start(ea[:, h, :], eaT_d[:, bass.ds((i * 2 + h) * HALF * P, HALF * P)])\
                        .then_inc(loaded[h], 16)

        @block.gpsimd
        def _(pool):
            for u in range(U):
                pool.sem_inc(reduced[u], 1)
            with pool.Fori(0, NTG // U) as i:
                for u in range(U):
                    h, t = divmod(u, HALF)
                    if t == 0:
                        pool.wait_ge(loaded[h], (i + 1) * 32)
                    pool.wait_ge(reduced[u], i + 1)
                    pool.sem_inc(steps, 1)
                    for tab, to, k, got in ((xl_d, xl, 0, got_l), (xr_d, xr, 1, got_r)):
                        pool.indirect_dma_start(
                            out=to[:, u, :], out_offset=None, in_=tab,
                            in_offset=bass.IndirectOffsetOnAxis(ap=idx[:, h, k, t:t + 1], axis=0))\
                            .then_inc(got[u], 16)

        @block.tensor
        def _(pe):
            pe.wait_ge(consts, 32)
            with pe.Fori(0, NTG // U) as i:
                for u in range(U):
                    h, t = divmod(u, HALF)
                    if t == 0:
                        pe.wait_ge(loaded[h], (i + 1) * 32)
                    pe.wait_ge(reduced[u], i + 1)
                    nc.tensor.matmul(pe_out[u][:, :], ea[:, h, t * P:(t + 1) * P], we[:, :],
                                     start=True, stop=True).then_inc(edge_part[u], 1)

        @block.vector
        def _(v):
            v.wait_ge(consts, 32)
            for h in range(2):
                v.sem_inc(half_done[h], 1)
            with v.Fori(0, NTG // U) as i:
                for k in range(U + 4):
                    if k < U:
                        u = k
                        v.wait_ge(edge_part[u], i + 1)
                        v.wait_ge(got_l[u], (i + 1) * 16)
                        nc.vector.tensor_tensor(xl[:, u, :], xl[:, u, :], pe_out[u][:, :], ALU.add)\
                            .then_inc(sum1[u], 1)
                    if 0 <= k - 1 < U:
                        u = k - 1
                        v.wait_ge(got_r[u], (i + 1) * 16)
                        v.wait_ge(sum1[u], i + 1)
                        nc.vector.tensor_tensor(xl[:, u, :], xl[:, u, :], xr[:, u, :], ALU.add)\
                            .then_inc(sum2[u], 1)
                        if u % HALF == HALF - 1:
                            v.sem_inc(half_done[u // HALF], 1)
                    if 0 <= k - 2 < U:
                        u = k - 2
                        v.wait_ge(sum2[u], i + 1)
                        nc.vector.scalar_tensor_tensor(xl[:, u, :], xl[:, u, :], SLOPE, xl[:, u, :],
                                                       ALU.mult, ALU.max).then_inc(leaky[u], 1)
                    if 0 <= k - 3 < U:
                        u = k - 3
                        v.wait_ge(leaky[u], i + 1)
                        nc.vector.tensor_tensor(xl[:, u, :], xl[:, u, :], att[:, :], ALU.mult)\
                            .then_inc(scaled[u], 1)
                    if 0 <= k - 4 < U:
                        u = k - 4
                        v.wait_ge(scaled[u], i + 1)
                        if u % HALF == 0:
                            v.wait_ge(stored[u // HALF], (i + 1) * 16)
                        nc.vector.tensor_reduce(lg[:, u, :], xl[:, u, :].rearrange("p (h c) -> p h c", h=H),
                                                AX.X, ALU.add).then_inc(reduced[u], 1)

        @block.scalar
        def _(act):
            for h in range(2):
                act.sem_inc(stored[h], 16)
            with act.Fori(0, NTG // U) as i:
                for h in range(2):
                    act.wait_ge(reduced[h * HALF + HALF - 1], i + 2)
                    act.dma_start(logit_d[bass.ds((i * 2 + h) * HALF * P, HALF * P), :]
                                  .rearrange("(t p) c -> p t c", p=P), lg[:, h * HALF:(h + 1) * HALF, :])\
                        .then_inc(stored[h], 16)
            for h in range(2):
                act.wait_ge(stored[h], 16 * (NTG // U + 1))


def segment_max(nc, name, nt, dst_halo, src_lin, ea_d, logit_d, rec_d, carry_d, back_d, ad_d=None, fill_d=None):
    with Stage(nc, name) as s:
        ticks, ticks_sp = s.sem("ticks"), s.sem("ticks_sp")
        words = 2 + 2 * H if src_lin is not None else 1 + H
        oa = words - H * (2 if src_lin is not None else 1)
        width = dst_halo.shape[1]
        dh = s.sb("dst", [P, (nt + 2) * width], I32)
        dv = dh[:, :].rearrange("p (n w) -> p n w", w=width)[:, :, width - 1]
        sl = s.sb("src", [P, nt], I32)
        L = s.sb("L", [P, nt, H])
        F = s.sb("F", [P, nt, H])
        B = s.sb("B", [P, nt])
        pf = s.sb("pf", [P, nt])
        pb = s.sb("pb", [P, nt])
        rec = s.sb("rec", [P, nt, words])
        ends = s.sb("ends", [P, 2 * H + 2])
        endT = s.sb("endT", [H, 2, P])
        path = s.sb("path", [H, 2, P])
        Z = s.sb("Z", [H, 2, P + 2])
        carry = s.sb("carry", [P, 2, H])
        first = s.sb("first", [P, 1], I32)
        first_ad = s.sb("first_ad", [P, H])
        loads, dve, moved, expd, out, firsts = (s.sem(n) for n in ("loads", "dve", "moved", "expd", "out", "firsts"))
        block = s.block()
        marks = {}

        @block.vector
        def _(v):
            step = Chain(dve)
            v.wait_ge(loads, 16 * 3)
            cur = dv[:, 1:nt + 1]
            step(v, nc.vector.tensor_tensor(pf[:, :], dv[:, 0:nt], cur, ALU.not_equal))
            step(v, nc.vector.tensor_scalar(pf[:, :], pf[:, :], -BIG, None, ALU.mult))
            step(v, nc.vector.tensor_tensor(pb[:, :], dv[:, 2:nt + 2], cur, ALU.not_equal))
            step(v, nc.vector.tensor_scalar(pb[:, :], pb[:, :], -BIG, None, ALU.mult))
            step(v, nc.vector.tensor_copy(rec[:, :, oa - 1], cur))
            if src_lin is not None:
                step(v, nc.vector.tensor_copy(rec[:, :, 0].bitcast(I32), sl[:, :]))
            if ad_d is not None:
                step(v, nc.vector.tensor_scalar(first[:, :], dv[:, 1:2], float(N - 1), None, ALU.min))
                marks["first"] = step.n
                step(v, nc.vector.tensor_scalar(B[:, :], pf[:, :], 0.0, None, ALU.is_equal))
                v.wait_ge(firsts, 16)
                for h in range(H):
                    step(v, nc.vector.tensor_tensor_scan(F[:, :, h], B[:, :], F[:, :, h], first_ad[:, h:h + 1],
                                                         ALU.mult, ALU.add))
                step(v, nc.vector.tensor_tensor(L[:, :, :], L[:, :, :], F[:, :, :], ALU.add))
                step(v, nc.vector.scalar_tensor_tensor(L[:, :, :], L[:, :, :], SLOPE, L[:, :, :],
                                                       ALU.mult, ALU.max))
            for h in range(H):
                step(v, nc.vector.tensor_tensor_scan(F[:, :, h], pf[:, :], L[:, :, h], -BIG, ALU.add, ALU.max))
                step(v, nc.vector.tensor_tensor_scan(B[:, ::-1], pb[:, ::-1], L[:, ::-1, h], -BIG,
                                                     ALU.add, ALU.max))
                step(v, nc.vector.tensor_copy(ends[:, h:h + 1], F[:, nt - 1, h:h + 1]))
                step(v, nc.vector.tensor_copy(ends[:, H + h:H + h + 1], B[:, 0:1]))
            step(v, nc.vector.tensor_tensor(ends[:, 2 * H:2 * H + 1], dv[:, 0:1], dv[:, nt:nt + 1], ALU.not_equal))
            step(v, nc.vector.tensor_tensor(ends[:, 2 * H + 1:2 * H + 2], dv[:, 1:2], dv[:, nt + 1:nt + 2],
                                            ALU.not_equal))
            step(v, nc.vector.tensor_scalar(ends[:, 2 * H:], ends[:, 2 * H:], -BIG, None, ALU.mult))
            step(v, nc.vector.memset(Z[:, :, :], -BIG))
            marks["ends"] = step.n
            v.wait_ge(moved, 16 * 5)
            step(v, nc.vector.tensor_tensor_scan(Z[:, 0, 1:P + 1], path[:, 0, :], endT[:, 0, :], -BIG,
                                                 ALU.add, ALU.max))
            step(v, nc.vector.tensor_tensor_scan(Z[:, 1, P:0:-1], path[:, 1, ::-1], endT[:, 1, ::-1], -BIG,
                                                 ALU.add, ALU.max))
            marks["carry"] = step.n
            v.wait_ge(moved, 16 * 9)
            for h in range(H):
                step(v, nc.vector.tensor_tensor_scan(F[:, :, h], pf[:, :], L[:, :, h], carry[:, 0, h:h + 1],
                                                     ALU.add, ALU.max))
                step(v, nc.vector.tensor_tensor_scan(B[:, ::-1], pb[:, ::-1], L[:, ::-1, h],
                                                     carry[:, 1, h:h + 1], ALU.add, ALU.max))
                step(v, nc.vector.tensor_tensor(B[:, :], B[:, :], F[:, :, h], ALU.max))
                step(v, nc.vector.tensor_tensor(L[:, :, h], L[:, :, h], B[:, :], ALU.subtract))
                if src_lin is not None:
                    step(v, nc.vector.scalar_tensor_tensor(rec[:, :, oa + H + h], pb[:, :], 0.0, B[:, :],
                                                           ALU.is_lt, ALU.mult))
            marks["all"] = step.n

        if ad_d is not None:
            @block.gpsimd
            def _(pool):
                pool.wait_ge(dve, marks["first"])
                pool.indirect_dma_start(out=first_ad[:, :], out_offset=None, in_=ad_d,
                                        in_offset=bass.IndirectOffsetOnAxis(ap=first[:, 0:1], axis=0))\
                    .then_inc(firsts, 16)

        @block.scalar
        def _(act):
            act.wait_ge(dve, marks["all"])
            nc.scalar.activation(rec[:, :, oa:oa + H], L[:, :, :], ACT.Exp).then_inc(expd, 1)

        @block.sync
        def _(sp):
            rows = bass.AP(tensor=dst_halo.tensor, offset=dst_halo.offset,
                           ap=[[nt * width, P], [1, (nt + 2) * width]])
            sp.dma_start(dh[:, :], rows).then_inc(loads, 16)
            sp.dma_start(L[:, :, :], logit_d.rearrange("(p n) h -> p n h", p=P)).then_inc(loads, 16)
            if src_lin is not None:
                sp.dma_start(sl[:, :], src_lin.rearrange("(p n) -> p n", p=P)).then_inc(loads, 16)
                sp.dma_start(rec_d[:, words:].rearrange("(p n) w -> p n w", p=P),
                             ea_d.rearrange("(p n) w -> p n w", p=P)).then_inc(out, 16)
            else:
                sp.dma_start(F[:, :, :], fill_d[1:nt * P + 1, :].rearrange("(p n) h -> p n h", p=P))\
                    .then_inc(loads, 16)
            sp.wait_ge(dve, marks["ends"])
            sp.dma_start(carry_d, ends[:, :]).then_inc(moved, 16)
            sp.wait_ge(moved, 16)
            with nc.allow_non_contiguous_dma(reason="512 ends, turned"):
                for k in range(2):
                    sp.dma_start(endT[:, k, :], carry_d[:, k * H:(k + 1) * H].rearrange("p h -> h p"))\
                        .then_inc(moved, 16)
                    sp.dma_start(path[:, k, :], carry_d[:, 2 * H + k:2 * H + k + 1].rearrange("p o -> o p")
                                 .to_broadcast([H, P])).then_inc(moved, 16)
            sp.wait_ge(dve, marks["carry"])
            sp.dma_start(back_d[0, :, :], Z[:, 0, 0:P]).then_inc(moved, 16)
            sp.dma_start(back_d[1, :, :], Z[:, 1, 2:P + 2]).then_inc(moved, 16)
            sp.wait_ge(moved, 16 * 7)
            with nc.allow_non_contiguous_dma(reason="512 ends, turned back"):
                for k in range(2):
                    sp.dma_start(carry[:, k, :], back_d[k, :, :].rearrange("h p -> p h")).then_inc(moved, 16)
            sp.wait_ge(expd, 1)
            to = rec_d[:, 0:words] if src_lin is not None else rec_d[:, H + HX:]
            sp.dma_start(to.rearrange("(p n) w -> p n w", p=P), rec[:, :, :]).then_inc(out, 16)
            sp.wait_ge(out, 32 if src_lin is not None else 16)


def worklist(nc, name, nt, nk, last_d, key_d, tile_d, win_d, kval_in):
    with Stage(nc, name) as s:
        ticks, ticks_sp = s.sem("ticks"), s.sem("ticks_sp")
        NB = kval_in.shape[1]
        li = s.sb("li", [1, nt], I32)
        wf = s.sb("wf", [1, nt])
        tf = s.sb("tf", [1, nt])
        key = s.sb("key", [P, nt])
        junk = s.sb("junk", [P, nt])
        kv = s.sb("kv", [P, NB])
        tk = s.sb("tk", [P, NB])
        wk = s.sb("wk", [P, NB])
        far = s.sb("far", [P, NB])
        ti = s.sb("ti", [P, 2, NB], I32)
        wm = s.sb("wm", [P, NB])
        dve, moved, tiled = s.sem("dve"), s.sem("moved"), s.sem("tiled")
        block = s.block()
        marks = {}

        @block.gpsimd
        def _(pool):
            nc.gpsimd.iota(tf[:, :], [[1, nt]], base=0, channel_multiplier=0,
                           allow_small_or_imprecise_dtypes=True).then_inc(tiled, 1)

        @block.vector
        def _(v):
            step = Chain(dve)
            v.wait_ge(moved, 32)
            v.wait_ge(tiled, 1)
            step(v, nc.vector.tensor_scalar(li[:, :], li[:, :], 7, None, ALU.arith_shift_right))
            step(v, nc.vector.tensor_scalar(wf[:, :], li[:, :], float(NW - 1), None, ALU.min))
            step(v, nc.vector.tensor_tensor(wf[:, :], wf[:, :], tf[:, :], ALU.add))
            marks["key"] = step.n
            v.wait_ge(moved, 64)
            for b in range(NB):
                step(v, nc.vector.tensor_scalar(junk[:, :], key[:, :], kv[:, b:b + 1], None, ALU.is_lt,
                                                ALU.add, accum_out=tk[:, b:b + 1]))
            step(v, nc.vector.tensor_scalar(tk[:, :], tk[:, :], float(nt - 1), None, ALU.min))
            step(v, nc.vector.tensor_tensor(wk[:, :], kv[:, :], tk[:, :], ALU.subtract))
            step(v, nc.vector.tensor_scalar(far[:, :], wk[:, :], float(NW), 1e6, ALU.is_ge, ALU.mult))
            step(v, nc.vector.tensor_scalar(wm[:, :], wk[:, :], float(P), None, ALU.mult))
            step(v, nc.vector.tensor_tensor(wm[:, :], wm[:, :], far[:, :], ALU.add))
            step(v, nc.vector.tensor_copy(ti[:, 0, :], tk[:, :]))
            step(v, nc.vector.tensor_scalar(ti[:, 1, :], wk[:, :], float(NW - 1), None, ALU.min))
            marks["all"] = step.n

        @block.sync
        def _(sp):
            with nc.allow_non_contiguous_dma(reason="one word of a tile or pair"):
                sp.dma_start(li[:, :], last_d).then_inc(moved, 16)
                sp.dma_start(kv[:, :], kval_in).then_inc(moved, 16)
                sp.wait_ge(dve, marks["key"])
                sp.dma_start(key_d, wf[:, :]).then_inc(moved, 16)
                sp.wait_ge(moved, 48)
                sp.dma_start(key[:, :], key_d.to_broadcast([P, nt])).then_inc(moved, 16)
                sp.wait_ge(dve, marks["all"])
                for j in range(2):
                    sp.dma_start(tile_d[j, :].rearrange("(b p) -> p b", p=P), ti[:, j, :]).then_inc(moved, 16)
                sp.dma_start(win_d[0, :].rearrange("(b p) -> p b", p=P), wm[:, :]).then_inc(moved, 16)
            sp.wait_ge(moved, 64 + 48)


def aggregate(nc, name, s, nt, nk, acc, cols, tile_d, win_d, iota_in, load, gather, weigh, rhs, dst_col):
    iota = s.sb("iota", [P, P])
    wb = s.sb("wb", [P, nk])
    tt = s.sb("tt", [1, 2, nk], I32)
    hot = s.sb("hot", [P, U, P])
    part = [s.ps(f"part{u}", [P, 512]) for u in range(U)]
    ticks_sp, ticks_act = s.sem("ticks_agg"), s.sem("ticks_agg_act")
    consts, cleared, steps = s.sem("consts"), s.sem("cleared"), s.sem("steps")
    loaded, gathered, hotted, weighed, summed, added = (
        s.sems(n, U) for n in ("loaded", "gathered", "hotted", "weighed", "summed", "added"))
    block = s.block()

    def loads(eng, first, ticks):
        with eng.Fori(0, nk // U) as i:
            _, tiles = nc.values_load_multi_w_load_instructions(
                tt[0:1, 0, bass.ds(i * U, U)], engines=[eng.engine], min_val=0, max_val=nt - 1,
                skip_runtime_bounds_check_because="the worklist clamps its tiles")
            for u in range(first, U, 2):
                t = tiles[u]
                eng.wait_ge(summed[u], i + 1)
                eng.sem_inc(ticks, 1)
                load(eng, u, t, loaded[u])

    @block.sync
    def _(sp):
        sp.dma_start(iota[:, :], iota_in.to_broadcast([P, P])).then_inc(consts, 16)
        sp.dma_start(wb[:, :], win_d[:, 0:nk].to_broadcast([P, nk])).then_inc(consts, 16)
        sp.dma_start(tt[0:1, :, :], tile_d[:, 0:nk].rearrange("(o j) n -> o j n", o=1)).then_inc(consts, 16)
        sp.wait_ge(consts, 48)
        loads(sp, 0, ticks_sp)

    @block.scalar
    def _(act):
        act.wait_ge(consts, 48)
        loads(act, 1, ticks_act)

    if gather is not None:
        @block.gpsimd
        def _(pool):
            for u in range(U):
                pool.sem_inc(weighed[u], 1)
            with pool.Fori(0, nk // U) as i:
                for u in range(U):
                    pool.wait_ge(loaded[u], (i + 1) * 16)
                    pool.wait_ge(weighed[u], i + 1)
                    pool.sem_inc(steps, 1)
                    gather(pool, u).then_inc(gathered[u], 16)

    @block.tensor
    def _(pe):
        for u in range(U):
            pe.sem_inc(summed[u], 1)
        with pe.Fori(0, nk // U) as i:
            for u in range(U):
                pe.wait_ge(weighed[u], i + (2 if gather is not None else 1))
                pe.wait_ge(hotted[u], i + 1)
                pe.wait_ge(added[u], i + 1)
                nc.tensor.matmul(part[u][:, 0:cols], hot[:, u, :], rhs(u), start=True, stop=True)\
                    .then_inc(summed[u], 1)

    @block.vector
    def _(v):
        nc.vector.memset(acc[:, :, :], 0.0).then_inc(cleared, 1)
        for u in range(U):
            v.sem_inc(added[u], 1)
        v.wait_ge(consts, 48)
        v.wait_ge(cleared, 1)
        with v.Fori(0, nk // U) as i:
            _, windows = nc.values_load_multi_w_load_instructions(
                tt[0:1, 1, bass.ds(i * U, U)], engines=[v.engine], min_val=0, max_val=NW - 1,
                skip_runtime_bounds_check_because="the worklist clamps its windows")

            def add(u):
                w = windows[u]
                v.wait_ge(summed[u], i + 2)
                if u == 0:
                    v.wait_ge(added[U - 1], i + 1)
                else:
                    v.wait_ge(added[u - 1], i + 2)
                nc.vector.tensor_tensor(acc[:, bass.ds(w, 1), :].rearrange("p o n -> p (o n)"),
                                        acc[:, bass.ds(w, 1), :].rearrange("p o n -> p (o n)"),
                                        part[u][:, 0:cols], ALU.add).then_inc(added[u], 1)

            for u in range(U):
                v.wait_ge(loaded[u], (i + 1) * 16)
                v.wait_ge(summed[u], i + 1)
                nc.vector.tensor_scalar(hot[:, u, :], iota[:, :], wb[:, bass.ds(i * U + u, 1)], dst_col(u),
                                        ALU.add, ALU.is_equal).then_inc(hotted[u], 1)
                if gather is not None:
                    v.wait_ge(gathered[u], (i + 1) * 16)
                weigh(u).then_inc(weighed[u], 1)
                if u >= 2:
                    add(u - 2)
            add(U - 2)
            add(U - 1)


def aggregate_nodes(nc, acc, rec_d, xl_d, tile_d, win_d, iota_in):
    with Stage(nc, "aggr") as s:
        ticks, ticks_sp = s.sem("ticks"), s.sem("ticks_sp")
        row = s.sb("row", [P, U, ROW])
        xg = s.sb("xg", [P, U, D])
        ones = s.sem("ones")
        with nc.Block() as block:
            @block.vector
            def _(v):
                nc.vector.memset(row[:, :, RV - 1:RV], 1.0).then_inc(ones, 1)
                v.wait_ge(ones, 1)

        def load(sp, u, t, loaded):
            at = bass.ds(t * P, P)
            sp.dma_start(row[:, u, 0:RV - 1], rec_d[at, :]).then_inc(loaded, 16)

        def gather(pool, u):
            return pool.indirect_dma_start(
                out=xg[:, u, :], out_offset=None, in_=xl_d,
                in_offset=bass.IndirectOffsetOnAxis(ap=row[:, u, 0:1].bitcast(I32), axis=0))

        def weigh(u):
            return nc.vector.tensor_tensor(
                row[:, u, RV:].rearrange("p (h c) -> p h c", h=H), xg[:, u, :].rearrange("p (h c) -> p h c", h=H),
                row[:, u, 2:2 + H].unsqueeze(2).to_broadcast([P, H, C]), ALU.mult)

        aggregate(nc, "aggr", s, NTG, KG, acc, CG, tile_d, win_d, iota_in, load, gather, weigh,
                  lambda u: row[:, u, 2:], lambda u: row[:, u, 1:2])


def aggregate_gate(nc, acc, rec_d, tile_d, win_d, iota_in):
    with Stage(nc, "gaggr") as s:
        row = s.sb("row", [P, U, FROW + HX])

        def load(eng, u, t, loaded):
            eng.dma_start(row[:, u, 0:FROW], rec_d[bass.ds(t * P, P), :]).then_inc(loaded, 16)

        def weigh(u):
            return nc.vector.tensor_tensor(
                row[:, u, FROW:].rearrange("p (h c) -> p h c", h=H),
                row[:, u, H:H + HX].rearrange("p (h c) -> p h c", h=H),
                row[:, u, FROW - H:FROW].unsqueeze(2).to_broadcast([P, H, NX]), ALU.mult)

        aggregate(nc, "gaggr", s, NTF, KF, acc, CF, tile_d, win_d, iota_in, load, None, weigh,
                  lambda u: row[:, u, FROW - H:], lambda u: row[:, u, H + HX:H + HX + 1])


def nodes_after(nc, acc, xl_d, xr_d, res_d, x_d, w_e, att_bc, w_gat, asrc_bc, adst_bc, x2_d, yT_d, tab_d, ad_d,
                ident_in):
    with Stage(nc, "after") as s:
        ticks, ticks_sp = s.sem("ticks"), s.sem("ticks_sp")
        we = s.sb("we", [ED, D])
        wg = s.sb("wg", [P, 2, HX])
        att = s.sb("att", [P, D])
        asr = s.sb("asr", [P, 2, HX])
        ident = s.sb("ident", [P, P])
        eps = s.sb("eps", [P, 1])
        xl = s.sb("xl", [P, 2, D])
        xr = s.sb("xr", [P, 2, D])
        rs = s.sb("res", [P, 2, D])
        xx = s.sb("x", [P, 2, D])
        la = s.sb("la", [P, NW, ED])
        las = s.sb("las", [P, 2, ED])
        laT = s.sb("laT", [ED, 2, P])
        cnt = s.sb("cnt", [P, NW])
        ml = s.sb("ml", [P, NW, H])
        slf = s.sb("slf", [P, NW, H])
        mx = s.sb("mx", [P, NW, H])
        c1 = s.sb("c1", [P, NW, H])
        c2 = s.sb("c2", [P, NW, H])
        den = s.sb("den", [P, NW, H])
        t = s.sb("t", [P, 2, D])
        q = s.sb("q", [P, 2, D])
        st = s.sb("st", [P, 2, 6])
        mv = s.sb("mv", [P, 2, 2])
        sd = s.sb("sd", [P, 2])
        rq = s.sb("rq", [P, 2])
        yT = s.sb("yT", [P, 2, 2, P])
        tab = s.sb("tab", [P, 2, H + HX])
        pr = s.sb("pr", [P, 2, 2, HX])
        ad = s.sb("ad", [P, 2, H])
        pL = [s.ps(f"pL{u}", [ED, P]) for u in range(2)]
        pE = [s.ps(f"pE{u}", [P, D]) for u in range(2)]
        pT = [s.ps(f"pT{u}", [P, 2, P]) for u in range(2)]
        pH = [s.ps(f"pH{u}", [P, HX]) for u in range(2)]
        consts, dve, expd = s.sem("consts"), s.sem("dve"), s.sem("expd")
        counts = {}

        def sems(names):
            for n in names.split():
                counts[n] = s.sems(n, 2)
            return counts

        S = sems("loaded picked turned copied edge s1 s2 s3 s4 s5")
        with nc.Block() as block:
            @block.sync
            def _(sp):
                sp.dma_start(we[:, :], w_e).then_inc(consts, 16)
                sp.dma_start(att[:, :], att_bc.to_broadcast([P, D])).then_inc(consts, 16)
                sp.dma_start(ident[:, :], ident_in).then_inc(consts, 16)
                sp.dma_start(wg[:, :, :], w_gat.rearrange("(c p) n -> p c n", p=P)).then_inc(consts, 16)
                sp.dma_start(asr[:, 0, :], asrc_bc.to_broadcast([P, HX])).then_inc(consts, 16)
                sp.dma_start(asr[:, 1, :], adst_bc.to_broadcast([P, HX])).then_inc(consts, 16)
                with sp.Fori(0, NW // 2) as i:
                    for u in range(2):
                        at = bass.ds((i * 2 + u) * P, P)
                        sp.wait_ge(S["s5"][u], i + 1)
                        sp.sem_inc(ticks_sp, 1)
                        sp.dma_start(xl[:, u, :], xl_d[at, :]).then_inc(S["loaded"][u], 16)
                        sp.dma_start(xr[:, u, :], xr_d[at, :]).then_inc(S["loaded"][u], 16)

            @block.vector
            def _(v):
                step = Chain(dve)
                step(v, nc.vector.memset(eps[:, :], EPS))
                step(v, nc.vector.tensor_scalar(cnt[:, :], acc[:, :, 2 * H + ED], 1.0, None, ALU.max))
                step(v, nc.vector.reciprocal(cnt[:, :], cnt[:, :]))
                step(v, nc.vector.tensor_tensor(la[:, :, :], acc[:, :, 2 * H:2 * H + ED],
                                                cnt[:, :].unsqueeze(2).to_broadcast([P, NW, ED]), ALU.mult))
                for u in range(2):
                    v.sem_inc(S["s5"][u], 1)
                v.wait_ge(consts, 96)
                with v.Fori(0, NW // 2) as i:
                    for u in range(2):
                        v.wait_ge(S["edge"][u], i + 1)
                        v.wait_ge(S["loaded"][u], (i + 1) * 32)
                        nc.vector.tensor_tensor(t[:, u, :], xl[:, u, :], pE[u][:, :], ALU.add)\
                            .then_inc(S["s1"][u], 1)
                    for u in range(2):
                        v.wait_ge(S["s1"][u], i + 1)
                        nc.vector.tensor_tensor(t[:, u, :], t[:, u, :], xr[:, u, :], ALU.add)\
                            .then_inc(S["s2"][u], 1)
                    for u in range(2):
                        v.wait_ge(S["s2"][u], i + 1)
                        nc.vector.scalar_tensor_tensor(t[:, u, :], t[:, u, :], SLOPE, t[:, u, :],
                                                       ALU.mult, ALU.max).then_inc(S["s3"][u], 1)
                    for u in range(2):
                        v.wait_ge(S["s3"][u], i + 1)
                        nc.vector.tensor_tensor(t[:, u, :], t[:, u, :], att[:, :], ALU.mult)\
                            .then_inc(S["s4"][u], 1)
                    for u in range(2):
                        v.wait_ge(S["s4"][u], i + 1)
                        nc.vector.tensor_reduce(
                            slf[:, bass.ds(i * 2 + u, 1), :].rearrange("p o h -> p (o h)"),
                            t[:, u, :].rearrange("p (h c) -> p h c", h=H), AX.X, ALU.add)\
                            .then_inc(S["s5"][u], 1)
                v.wait_ge(S["s5"][1], NW // 2 + 1)
                step(v, nc.vector.tensor_scalar(cnt[:, :], acc[:, :, 2 * H + ED], 0.0, -BIG, ALU.is_equal, ALU.mult))
                step(v, nc.vector.tensor_tensor(ml[:, :, :], acc[:, :, H:2 * H],
                                                cnt[:, :].unsqueeze(2).to_broadcast([P, NW, H]), ALU.add))
                step(v, nc.vector.tensor_tensor(mx[:, :, :], ml[:, :, :], slf[:, :, :], ALU.max))
                step(v, nc.vector.tensor_tensor(ml[:, :, :], ml[:, :, :], mx[:, :, :], ALU.subtract))
                step(v, nc.vector.tensor_tensor(slf[:, :, :], slf[:, :, :], mx[:, :, :], ALU.subtract))
                counts["shifted"] = step.n
                v.wait_ge(expd, 2)
                step(v, nc.vector.tensor_tensor(den[:, :, :], acc[:, :, 0:H], c1[:, :, :], ALU.mult))
                step(v, nc.vector.tensor_tensor(den[:, :, :], den[:, :, :], c2[:, :, :], ALU.add))
                step(v, nc.vector.reciprocal(den[:, :, :], den[:, :, :]))
                step(v, nc.vector.tensor_tensor(c1[:, :, :], c1[:, :, :], den[:, :, :], ALU.mult))
                step(v, nc.vector.tensor_tensor(c2[:, :, :], c2[:, :, :], den[:, :, :], ALU.mult))

            @block.tensor
            def _(pe):
                pe.wait_ge(consts, 96)
                pe.wait_ge(dve, 4)
                with pe.Fori(0, NW // 2) as i:
                    for u in range(2):
                        pe.wait_ge(S["picked"][u], i + 1)
                        nc.tensor.transpose(pL[u][:, :], las[:, u, :], ident[:, :]).then_inc(S["turned"][u], 1)
                    for u in range(2):
                        pe.wait_ge(S["copied"][u], i + 1)
                        pe.wait_ge(S["s5"][u], i + 1)
                        nc.tensor.matmul(pE[u][:, :], laT[:, u, :], we[:, :], start=True, stop=True)\
                            .then_inc(S["edge"][u], 1)

            @block.scalar
            def _(act):
                act.wait_ge(dve, 4)
                for u in range(2):
                    act.sem_inc(S["edge"][u], 1) if False else None
                with act.Fori(0, NW // 2) as i:
                    for u in range(2):
                        act.wait_ge(S["s5"][u], i + 1)
                        nc.scalar.copy(las[:, u, :], la[:, bass.ds(i * 2 + u, 1), :]
                                       .rearrange("p o n -> p (o n)")).then_inc(S["picked"][u], 1)
                    for u in range(2):
                        act.wait_ge(S["turned"][u], i + 1)
                        nc.scalar.copy(laT[:, u, :], pL[u][:, :]).then_inc(S["copied"][u], 1)
                act.wait_ge(dve, counts["shifted"])
                nc.scalar.activation(c1[:, :, :], ml[:, :, :], ACT.Exp).then_inc(expd, 1)
                nc.scalar.activation(c2[:, :, :], slf[:, :, :], ACT.Exp).then_inc(expd, 1)

        R = {n: s.sems(f"b_{n}", 2) for n in ("loaded", "w", "wl", "o", "o2", "mn", "ex", "m1", "el", "x2",
                                              "st", "ag", "sq", "rc", "y", "turn", "cp", "h", "hc", "pr", "tb",
                                              "store")}
        with nc.Block() as block:
            @block.sync
            def _(sp):
                for u in range(2):
                    sp.sem_inc(R["loaded"][u], 64)
                with sp.Fori(0, NW // 2) as i:
                    for u in range(2):
                        at = bass.ds((i * 2 + u) * P, P)
                        sp.wait_ge(R["y"][u], i + 1)
                        sp.sem_inc(ticks_sp, 1)
                        sp.wait_ge(R["store"][u], (i + 1) * 64)
                        sp.sem_inc(ticks_sp, 1)
                        sp.dma_start(xl[:, u, :], xl_d[at, :]).then_inc(R["loaded"][u], 16)
                        sp.dma_start(rs[:, u, :], res_d[at, :]).then_inc(R["loaded"][u], 16)
                        sp.dma_start(xx[:, u, :], x_d[at, :]).then_inc(R["loaded"][u], 16)
                    for u in range(2):
                        at = bass.ds((i * 2 + u) * P, P)
                        sp.wait_ge(R["tb"][u], i + 1)
                        sp.sem_inc(ticks_sp, 1)
                        sp.dma_start(tab_d[at, :], tab[:, u, :]).then_inc(R["store"][u], 16)
                        sp.dma_start(ad_d[at, :], ad[:, u, :]).then_inc(R["store"][u], 16)
                for u in range(2):
                    sp.wait_ge(R["store"][u], 64 * (NW // 2 + 1))

            @block.vector
            def _(v):
                for u in range(2):
                    v.sem_inc(R["y"][u], 1)
                with v.Fori(0, NW // 2) as i:
                    def each(first, fn, done):
                        for u in range(2):
                            for sem, plus in first:
                                v.wait_ge(R[sem][u], (i + plus) if sem not in ("loaded", "store") else
                                          (i + plus) * (48 if sem == "loaded" else 64))
                            if done == "ag":
                                v.sem_inc(ticks, 1)
                            fn(u).then_inc(R[done][u], 1)

                    def win(buf, lo, hi):
                        return lambda u: buf[:, bass.ds(i * 2 + u, 1), lo:hi].rearrange("p o n -> p (o n)")

                    def heads(ap):
                        return ap.rearrange("p (h c) -> p h c", h=H)

                    tt = nc.vector.tensor_tensor
                    values, w1, w2 = win(acc, CG - D, CG), win(c1, 0, H), win(c2, 0, H)
                    each([("y", 1)], lambda u: tt(
                        heads(t[:, u, :]), heads(values(u)), w1(u).unsqueeze(2).to_broadcast([P, H, C]),
                        ALU.mult), "w")
                    for u in range(2):
                        v.wait_ge(R["loaded"][u], (i + 1) * 48 + 64)
                        tt(heads(q[:, u, :]), heads(xl[:, u, :]), w2(u).unsqueeze(2).to_broadcast([P, H, C]),
                           ALU.mult).then_inc(R["wl"][u], 1)
                    each([("w", 1), ("wl", 1)], lambda u: tt(t[:, u, :], t[:, u, :], q[:, u, :], ALU.add), "o")
                    each([("o", 1)], lambda u: tt(t[:, u, :], t[:, u, :], rs[:, u, :], ALU.add), "o2")
                    each([("o2", 1)], lambda u: nc.vector.tensor_scalar(q[:, u, :], t[:, u, :], 0.0, None, ALU.min), "mn")
                    each([("o2", 1)], lambda u: nc.vector.tensor_scalar(t[:, u, :], t[:, u, :], 0.0, -1.0, ALU.max,
                                                                        ALU.add), "m1")
                    each([("ex", 1), ("m1", 1)], lambda u: tt(t[:, u, :], t[:, u, :], q[:, u, :], ALU.add), "el")
                    each([("el", 1), ("store", 1)], lambda u: tt(xx[:, u, :], xx[:, u, :], t[:, u, :], ALU.add), "x2")
                    each([("x2", 1)], lambda u: nc.vector.bn_stats(st[:, u, :], xx[:, u, :]), "st")
                    each([("st", 1)], lambda u: nc.vector.bn_aggr(mv[:, u, :], st[:, u, :]), "ag")
                    each([("sq", 1)], lambda u: nc.vector.reciprocal(rq[:, u:u + 1], sd[:, u:u + 1]), "rc")
                    each([("rc", 1), ("turn", 1)], lambda u: nc.vector.tensor_scalar(
                        q[:, u, :], xx[:, u, :], mv[:, u, 0:1], rq[:, u:u + 1], ALU.subtract, ALU.mult), "y")
                    each([("h", 1)], lambda u: nc.vector.tensor_copy(tab[:, u, H:], pH[u][:, :]), "hc")
                    each([("hc", 1)], lambda u: tt(
                        pr[:, u, :, :], asr[:, :, :], tab[:, u, H:].unsqueeze(1).to_broadcast([P, 2, HX]),
                        ALU.mult), "pr")
                    for u in range(2):
                        v.wait_ge(R["pr"][u], i + 1)
                        nc.vector.tensor_reduce(tab[:, u, 0:H], pr[:, u, 0, :].rearrange("p (h c) -> p h c", h=H),
                                                AX.X, ALU.add)
                        nc.vector.tensor_reduce(ad[:, u, :], pr[:, u, 1, :].rearrange("p (h c) -> p h c", h=H),
                                                AX.X, ALU.add).then_inc(R["tb"][u], 1)

            @block.scalar
            def _(act):
                for u in range(2):
                    act.sem_inc(R["store"][u], 64)
                with act.Fori(0, NW // 2) as i:
                    for u in range(2):
                        act.wait_ge(R["mn"][u], i + 1)
                        nc.scalar.activation(q[:, u, :], q[:, u, :], ACT.Exp).then_inc(R["ex"][u], 1)
                    for u in range(2):
                        act.wait_ge(R["x2"][u], i + 1)
                        act.dma_start(x2_d[bass.ds((i * 2 + u) * P, P), :], xx[:, u, :]).then_inc(R["store"][u], 16)
                    for u in range(2):
                        act.wait_ge(R["ag"][u], i + 1)
                        nc.scalar.activation(sd[:, u:u + 1], mv[:, u, 1:2], ACT.Sqrt, bias=eps[:, 0:1])\
                            .then_inc(R["sq"][u], 1)
                    for u in range(2):
                        act.wait_ge(R["turn"][u], i + 2)
                        act.wait_ge(R["store"][u], (i + 1) * 64)
                        nc.scalar.copy(yT[:, u, :, :], pT[u][:, :, :]).then_inc(R["cp"][u], 1)
                    for u in range(2):
                        act.wait_ge(R["cp"][u], i + 1)
                        act.dma_start(yT_d[bass.ds(i * 2 + u, 1), :, :].rearrange("o p n -> (o p) n"),
                                      yT[:, u, :, :].rearrange("p c n -> p (c n)")).then_inc(R["store"][u], 16)

            @block.tensor
            def _(pe):
                for u in range(2):
                    pe.sem_inc(R["turn"][u], 1)
                with pe.Fori(0, NW // 2) as i:
                    for u in range(2):
                        pe.wait_ge(R["y"][u], i + 2)
                        nc.tensor.transpose(pT[u][:, 0, :], q[:, u, 0:P], ident[:, :])
                        nc.tensor.transpose(pT[u][:, 1, :], q[:, u, P:], ident[:, :]).then_inc(R["turn"][u], 1)
                    for u in range(2):
                        pe.wait_ge(R["cp"][u], i + 1)
                        for c in range(2):
                            last = nc.tensor.matmul(pH[u][:, :], yT[:, u, c, :], wg[:, c, :],
                                                    start=(c == 0), stop=(c == 1))
                        last.then_inc(R["h"][u], 1)


def sort_by_destination(nc, dst_tab, dst_lin, rec_in, low_d, start_d, sorted_d, ident_in, iota_in, tri_in, part_in):
    with Stage(nc, "sort") as s:
        ticks, ticks_sp = s.sem("ticks"), s.sem("ticks_sp")
        iota = s.sb("iota", [P, P])
        ident = s.sb("ident", [P, P])
        tri = s.sb("tri", [P, P])
        part = s.sb("part", [P, 1])
        ones = s.sb("ones", [P, P])
        dt_i = s.sb("dt_i", [P, NTF], I32)
        dl_i = s.sb("dl_i", [P, NTF], I32)
        tmp_i = s.sb("tmp_i", [P, NTF], I32)
        lowf = s.sb("lowf", [P, NTF], BF16)
        rows = s.sb("rows", [P, NTF, 2], I32)
        lo = s.sb("lo", [P, NTF])
        hi = s.sb("hi", [P, NTF])
        hot_lo = s.sb("hot_lo", [P, 2, HALF, P], BF16)
        hot_hi = s.sb("hot_hi", [P, 2, HALF, HI], BF16)
        tri_b = s.sb("tri_b", [P, P], BF16)
        lrow = s.sb("lrow", [P, 2, HALF * P], BF16)
        hot_t = s.sb("hot_t", [P, 2, HALF * P])
        same = s.sb("same", [P, U, P], BF16)
        cnt0 = s.sb("cnt0", [P, HI])
        tot = s.sb("tot", [P, HI])
        base = s.sb("base", [P, HI])
        cur = s.sb("cur", [P, 2, HI])
        picked = s.sb("picked", [P, 2, HALF, HI])
        pos = s.sb("pos", [P, 2, HALF])
        posi = s.sb("posi", [P, 2, HALF], I32)
        starti = s.sb("starti", [P, HI], I32)
        rec = s.sb("rec", [P, 2, HALF, 2], I32)
        edge = s.sb("edge", [1, 2, 2], I32)
        pc = s.ps("pc", [P, 512])
        pr = s.ps("pr", [P, 512])
        pl = [s.ps(f"pl{h}", [P, HALF, HI]) for h in range(2)]
        pn = [s.ps(f"pn{u}", [P, HI]) for u in range(2)]
        consts, dve, pef, tabled = s.sem("consts"), s.sem("dve"), s.sem("pef"), s.sem("tabled")
        ended = s.sem("ended")
        first_hot, first_used = s.sems("first_hot", 2), s.sems("first_used", 2)
        GROUPS = NTF // U
        marks = {}

        def one_hots(h, tile0):
            at = bass.ds(tile0, HALF)
            nc.vector.tensor_tensor(hot_lo[:, h, :, :], lo[:, at].unsqueeze(2).to_broadcast([P, HALF, P]),
                                    iota[:, :].unsqueeze(1).to_broadcast([P, HALF, P]), ALU.is_equal)
            return nc.vector.tensor_tensor(
                hot_hi[:, h, :, :], hi[:, at].unsqueeze(2).to_broadcast([P, HALF, HI]),
                iota[:, 0:HI].unsqueeze(1).to_broadcast([P, HALF, HI]), ALU.is_equal)

        with nc.Block() as block:
            @block.vector
            def _(v):
                step = Chain(dve)
                step(v, nc.vector.memset(edge[:, :, :], -1))
                step(v, nc.vector.memset(ones[:, :], 1.0))
                step(v, nc.vector.memset(cnt0[:, :], 0.0))
                marks["zeroed"] = step.n
                v.wait_ge(consts, 112)
                step(v, nc.vector.tensor_copy(tri_b[:, :], tri[:, :]))
                step(v, nc.vector.tensor_scalar(rows[:, :, 0], rows[:, :, 0], float(N - 1), None, ALU.min))
                step(v, nc.vector.tensor_scalar(tmp_i[:, :], dl_i[:, :], P - 1, None, ALU.bitwise_and))
                step(v, nc.vector.tensor_copy(lowf[:, :], tmp_i[:, :]))
                marks["low"] = step.n
                step(v, nc.vector.tensor_scalar(tmp_i[:, :], dt_i[:, :], P - 1, None, ALU.bitwise_and))
                step(v, nc.vector.tensor_copy(lo[:, :], tmp_i[:, :]))
                step(v, nc.vector.tensor_scalar(tmp_i[:, :], dt_i[:, :], 7, None, ALU.arith_shift_right))
                step(v, nc.vector.tensor_copy(hi[:, :], tmp_i[:, :]))
                for h in range(2):
                    v.sem_inc(first_used[h], 1)
                with v.Fori(0, GROUPS) as i:
                    for h in range(2):
                        v.wait_ge(first_used[h], i + 1)
                        one_hots(h, i * U + h * HALF).then_inc(first_hot[h], 1)
                v.wait_ge(pef, 1)
                step(v, nc.vector.tensor_copy(cnt0[:, :], pc[:, 0:HI]))
                marks["counted"] = step.n
                v.wait_ge(pef, 3)
                step(v, nc.vector.tensor_copy(tot[:, :], pr[:, 0:HI]))
                step(v, nc.vector.tensor_tensor_scan(base[:, :], ones[:, 0:HI], tot[:, :], 0.0, ALU.mult, ALU.add))
                step(v, nc.vector.tensor_tensor(base[:, :], base[:, :], tot[:, :], ALU.subtract))
                step(v, nc.vector.tensor_scalar(base[:, :], base[:, :], 1.0, None, ALU.add))
                step(v, nc.vector.tensor_tensor(cur[:, 0, :], base[:, :], pr[:, 128:128 + HI], ALU.add))
                step(v, nc.vector.tensor_copy(starti[:, :], cur[:, 0, :]))
                marks["started"] = step.n

            @block.sync
            def _(sp):
                sp.dma_start(iota[:, :], iota_in.to_broadcast([P, P])).then_inc(consts, 16)
                sp.dma_start(ident[:, :], ident_in).then_inc(consts, 16)
                sp.dma_start(tri[:, :], tri_in).then_inc(consts, 16)
                sp.dma_start(part[:, :], part_in).then_inc(consts, 16)
                sp.dma_start(dt_i[:, :], dst_tab).then_inc(consts, 16)
                sp.dma_start(rows[:, :, :], rec_in).then_inc(consts, 16)
                sp.dma_start(dl_i[:, :], dst_lin.rearrange("o (p n) -> (o p) n", p=P)).then_inc(consts, 16)
                sp.wait_ge(dve, 1)
                sp.dma_start(sorted_d[0:1, :], edge[:, 0, :]).then_inc(ended, 16)
                sp.dma_start(sorted_d[NTF * P + 1:, :], edge[:, 1, :]).then_inc(ended, 16)
                sp.wait_ge(dve, marks["low"])
                sp.dma_start(low_d.rearrange("o (p n) -> (o p) n", p=P), lowf[:, :]).then_inc(ended, 16)
                sp.wait_ge(dve, marks["started"])
                sp.dma_start(start_d, starti[:, :]).then_inc(ended, 16)
                sp.wait_ge(ended, 64)

            @block.tensor
            def _(pe):
                pe.wait_ge(consts, 112)
                pe.wait_ge(dve, marks["zeroed"])
                nc.tensor.matmul(pc[:, 0:HI], ident[:, :], cnt0[:, :], start=True, stop=False)
                with pe.Fori(0, GROUPS) as i:
                    for h in range(2):
                        pe.wait_ge(first_hot[h], i + 1)
                        for k in range(HALF):
                            last = nc.tensor.matmul(pc[:, 0:HI], hot_lo[:, h, k, :], hot_hi[:, h, k, :],
                                                    start=False, stop=False)
                        last.then_inc(first_used[h], 1)
                nc.tensor.matmul(pc[:, 0:HI], ident[:, :], cnt0[:, :], start=False, stop=True).then_inc(pef, 1)
                pe.wait_ge(dve, marks["counted"])
                nc.tensor.matmul(pr[:, 0:HI], ones[:, :], cnt0[:, :], start=True, stop=True).then_inc(pef, 1)
                nc.tensor.matmul(pr[:, 128:128 + HI], tri[:, :], cnt0[:, :], start=True, stop=True)\
                    .then_inc(pef, 1)

        loaded, hots, masks, picks, sums, placed, freed = (
            s.sems(f"r_{n}", 2) for n in ("loaded", "hots", "masks", "picks", "sums", "placed", "freed"))
        counted, looked, wrote, current = (
            s.sems(f"r_{n}", U) for n in ("counted", "looked", "wrote", "current"))
        steps = s.sem("steps")
        with nc.Block() as block:
            @block.sync
            def _(sp):
                with sp.Fori(0, GROUPS) as i:
                    for h in range(2):
                        sp.wait_ge(masks[h], i + 1)
                        sp.sem_inc(ticks_sp, 1)
                        sp.dma_start(lrow[:, h, :], low_d[:, bass.ds((i * 2 + h) * HALF * P, HALF * P)]
                                     .to_broadcast([P, HALF * P])).then_inc(loaded[h], 16)

            @block.vector
            def _(v):
                for u in range(U):
                    v.sem_inc(looked[u], 1)
                for h in range(2):
                    v.sem_inc(masks[h], 1)

                def build_masks(i, h):
                    v.wait_ge(loaded[h], (i + 1) * 16)
                    for u in range(h * HALF, (h + 1) * HALF):
                        v.wait_ge(looked[u], i + 1)
                    v.wait_ge(picks[h], i + 1)
                    one_hots(h, i * U + h * HALF).then_inc(hots[h], 1)
                    nc.vector.tensor_scalar(hot_t[:, h, :], lrow[:, h, :], part[:, 0:1], None, ALU.is_equal)
                    for k in range(HALF):
                        u = h * HALF + k
                        last = nc.vector.scalar_tensor_tensor(
                            same[:, u, :], lrow[:, h, k * P:(k + 1) * P], lo[:, bass.ds(i * U + u, 1)],
                            tri_b[:, :], ALU.is_equal, ALU.mult)
                    last.then_inc(masks[h], 1)

                def place(i, h):
                    v.wait_ge(looked[h * HALF + HALF - 1], i + 2)
                    nc.vector.tensor_tensor(picked[:, h, :, :], pl[h], hot_hi[:, h, :, :], ALU.mult)\
                        .then_inc(picks[h], 1)
                    v.wait_ge(picks[h], i + 2)
                    nc.vector.tensor_reduce(pos[:, h, :], picked[:, h, :, :], AX.X, ALU.add).then_inc(sums[h], 1)
                    v.wait_ge(sums[h], i + 1)
                    v.wait_ge(freed[h], i + 1)
                    nc.vector.tensor_copy(rec[:, h, :, :], rows[:, bass.ds(i * U + h * HALF, HALF), :])
                    nc.vector.tensor_copy(posi[:, h, :], pos[:, h, :]).then_inc(placed[h], 1)

                for h in range(2):
                    v.sem_inc(picks[h], 1)
                build_masks(0, 0)
                with v.Fori(0, GROUPS - 1) as i:
                    build_masks(i, 1)
                    place(i, 0)
                    build_masks(i + 1, 0)
                    place(i, 1)
                build_masks(GROUPS - 1, 1)
                place(GROUPS - 1, 0)
                place(GROUPS - 1, 1)

            @block.tensor
            def _(pe):
                for h in range(2):
                    pe.sem_inc(placed[h], 1)
                with pe.Fori(0, GROUPS) as i:
                    now, next_ = pe.snap(i + 1), pe.snap(i + 2)
                    for u in range(U):
                        h, k = divmod(u, HALF)
                        if k == 0:
                            pe.wait_ge(hots[h], now)
                            pe.wait_ge(masks[h], next_)
                            pe.wait_ge(placed[h], now)
                        pe.wait_ge(current[u], now)
                        nc.tensor.matmul(pn[u % 2][:, :], ident[:, :], cur[:, u % 2, :], start=True, stop=False)
                        nc.tensor.matmul(pn[u % 2][:, :], hot_lo[:, h, k, :], hot_hi[:, h, k, :],
                                         start=False, stop=True).then_inc(counted[u], 1)
                        nc.tensor.matmul(pl[h][:, k, :], hot_t[:, h, k * P:(k + 1) * P], cur[:, u % 2, :],
                                         start=True, stop=False)
                        nc.tensor.matmul(pl[h][:, k, :], same[:, u, :], hot_hi[:, h, k, :],
                                         start=False, stop=True).then_inc(looked[u], 1)

            @block.scalar
            def _(act):
                act.sem_inc(current[0], 1)
                with act.Fori(0, GROUPS) as i:
                    now, next_ = act.snap(i + 1), act.snap(i + 2)
                    for u in range(U):
                        act.wait_ge(counted[u], now)
                        act.wait_ge(looked[(u - 1) % U], next_ if u >= 1 else now)
                        nc.scalar.copy(cur[:, (u + 1) % 2, :], pn[u % 2][:, :]).then_inc(current[(u + 1) % U], 1)

            @block.gpsimd
            def _(pool):
                for h in range(2):
                    pool.sem_inc(freed[h], 1)
                def scatter(i, h):
                    pool.wait_ge(placed[h], i + 2)
                    pool.sem_inc(steps, 1)
                    for k in range(HALF):
                        pool.indirect_dma_start(
                            out=sorted_d, out_offset=bass.IndirectOffsetOnAxis(ap=posi[:, h, k:k + 1], axis=0),
                            in_=rec[:, h, k, :], in_offset=None).then_inc(wrote[h * HALF + k], 16)

                def written(count, h):
                    for k in range(HALF):
                        pool.wait_ge(wrote[h * HALF + k], count * 16)
                    pool.sem_inc(freed[h], 1)

                scatter(0, 0)
                scatter(0, 1)
                written(1, 0)
                with pool.Fori(1, GROUPS) as i:
                    scatter(i, 0)
                    written(i, 1)
                    scatter(i, 1)
                    written(i + 1, 0)
                written(GROUPS, 1)


def gate_rows_and_experts(nc, sorted_d, start_d, tab_d, ad_d, fill_d, rec_d, yT_d, w1_d, b1_d, w2_d, b2_d, z_d):
    with Stage(nc, "gate") as s:
        start = s.sb("start", [P, HI], I32)
        zeros = s.sb("zeros", [P, NTF * H])
        ad = s.sb("ad", [P, NW, H])
        idx = s.sb("idx", [P, 2, HALF, 2], I32)
        tg = s.sb("tg", [P, U, H + HX])
        steps, consts, zeroed, filled, spread, ticks_sp = (
            s.sem(n) for n in ("steps", "consts", "zeroed", "filled", "spread", "ticks_sp"))
        loaded, stored = s.sems("loaded", 2), s.sems("stored", 2)
        got = s.sems("got", U)
        GROUPS = NTF // U
        FB = FF // P
        w1 = s.sb("w1", [P, 2, NX * FF])
        w2 = s.sb("w2", [P, NX * FB, D])
        b1 = s.sb("b1", [P, NX * FB])
        b2 = s.sb("b2", [P, NX, D])
        yT = s.sb("yT", [P, 2, 2, P])
        hid = s.sb("hid", [P, NX * FB, 2 * P])
        z = s.sb("z", [P, NX, 2, D])
        pU = [s.ps(f"pU{k}", [P, 512]) for k in range(4)]
        pD = [s.ps(f"pD{k}", [P, 512]) for k in range(4)]
        weights = s.sem("weights")
        y_here = s.sem("y_here")
        z_out = s.sems("z_out", NX)
        up, hidden = s.sems("up", NX * FB), s.sems("hidden", NX * FB)
        down, biased = s.sems("down", NX * 2), s.sems("biased", NX * 2)
        ticks_act = s.sem("ticks_act")
        block = s.block()

        @block.sync
        def _(sp):
            def load_indices(i, h):
                at = bass.ds((i * 2 + h) * HALF * P + 1, HALF * P)
                sp.dma_start(idx[:, h, :, :], sorted_d[at, :].rearrange("(t p) w -> p t w", p=P))\
                    .then_inc(loaded[h], 16)

            def store_rows(i, h):
                for k in range(HALF):
                    sp.wait_ge(got[h * HALF + k], (i + 1) * 16)
                sp.sem_inc(ticks_sp, 1)
                at = bass.ds((i * 2 + h) * HALF * P, HALF * P)
                sp.dma_start(rec_d[at, 0:H + HX].rearrange("(t p) c -> p t c", p=P),
                             tg[:, h * HALF:(h + 1) * HALF, :]).then_inc(stored[h], 16)

            sp.dma_start(start[:, :], start_d).then_inc(consts, 16)
            sp.dma_start(ad[:, :, :], ad_d.rearrange("(w p) h -> p w h", p=P)).then_inc(consts, 16)
            sp.wait_ge(zeroed, 1)
            sp.dma_start(fill_d[1:NTF * P + 1, :].rearrange("(p n) h -> p (n h)", p=P), zeros[:, :])\
                .then_inc(filled, 16)
            for h in range(2):
                sp.sem_inc(stored[h], 16)
                load_indices(0, h)
            with sp.Fori(0, GROUPS - 1) as i:
                for h in range(2):
                    store_rows(i, h)
                    load_indices(i + 1, h)
            for h in range(2):
                store_rows(GROUPS - 1, h)
            for h in range(2):
                sp.wait_ge(stored[h], 16 * (GROUPS + 1))

        @block.gpsimd
        def _(pool):
            with pool.Fori(0, GROUPS) as i:
                for h in range(2):
                    pool.wait_ge(loaded[h], (i + 1) * 16)
                    pool.wait_ge(stored[h], (i + 1) * 16)
                    pool.sem_inc(steps, 1)
                    for k in range(HALF):
                        pool.indirect_dma_start(
                            out=tg[:, h * HALF + k, :], out_offset=None, in_=tab_d,
                            in_offset=bass.IndirectOffsetOnAxis(ap=idx[:, h, k, 0:1], axis=0))\
                            .then_inc(got[h * HALF + k], 16)
            pool.wait_ge(consts, 32)
            pool.wait_ge(filled, 16)
            windows = -(-N // P)
            for w in range(windows):
                n = min(P, N - w * P)
                pool.indirect_dma_start(
                    out=fill_d, out_offset=bass.IndirectOffsetOnAxis(ap=start[0:n, w:w + 1], axis=0),
                    in_=ad[0:n, w, :], in_offset=None).then_inc(spread, 16)
            pool.wait_ge(spread, 16 * windows)

        @block.tensor
        def _(pe):
            pe.wait_ge(weights, 16 * (2 * NX + 2))
            with pe.Fori(0, NW // 2) as i:
                pe.wait_ge(y_here, (i + 1) * 16)

                def rise(e):
                    for f in range(e * FB, (e + 1) * FB):
                        pe.wait_ge(hidden[(f - 4) % (NX * FB)], i + (2 if f >= 4 else 1))
                        for c in range(2):
                            last = nc.tensor.matmul(pU[f % 4][:, 0:2 * P].rearrange("p (w n) -> p w n", w=2),
                                                    w1[:, c, f * P:(f + 1) * P], yT[:, :, c, :],
                                                    start=(c == 0), stop=(c == 1))
                        last.then_inc(up[f], 1)

                def fall(e):
                    for w in range(2):
                        j = e * 2 + w
                        pe.wait_ge(biased[(j - 4) % (NX * 2)], i + (2 if j >= 4 else 1))
                        for f in range(FB):
                            if w == 0:
                                pe.wait_ge(hidden[e * FB + f], i + 2)
                            last = nc.tensor.matmul(pD[j % 4][:, 0:D], hid[:, e * FB + f, w * P:(w + 1) * P],
                                                    w2[:, e * FB + f, :], start=(f == 0), stop=(f == FB - 1))
                        last.then_inc(down[j], 1)

                rise(0)
                for e in range(1, NX):
                    rise(e)
                    fall(e - 1)
                fall(NX - 1)

        @block.scalar
        def _(act):
            for k in range(NX):
                act.dma_start(w1[:, :, k * FF:(k + 1) * FF], w1_d[k, :, :].rearrange("(c p) n -> p c n", p=P))\
                    .then_inc(weights, 16)
                act.dma_start(w2[:, k * FB:(k + 1) * FB, :], w2_d[k, :, :].rearrange("(c p) n -> p c n", p=P))\
                    .then_inc(weights, 16)
            act.dma_start(b1[:, :], b1_d).then_inc(weights, 16)
            act.dma_start(b2[:, :, :].rearrange("p k n -> p (k n)"), b2_d.to_broadcast([P, NX * D]))\
                .then_inc(weights, 16)
            act.wait_ge(weights, 16 * (2 * NX + 2))
            act.preload_act_table(ACT.Gelu)
            for f in range(NX * FB):
                act.sem_inc(hidden[f], 1)
            for e in range(NX):
                act.sem_inc(z_out[e], 16)

            def load_y(i):
                act.dma_start(yT[:, :, :, :].rearrange("p w c n -> p w (c n)"),
                              yT_d[bass.ds(i * 2, 2), :, :].rearrange("w p n -> p w n")).then_inc(y_here, 16)

            def body(i, last):
                for f in range(NX * FB):
                    act.wait_ge(up[f], i + 1)
                    act.wait_ge(down[f // FB * 2 + 1], i + 1)
                    nc.scalar.activation(hid[:, f, :], pU[f % 4][:, 0:2 * P], ACT.Gelu, bias=b1[:, f:f + 1])\
                        .then_inc(hidden[f], 1)
                if not last:
                    load_y(i + 1)
                for e in range(NX):
                    act.wait_ge(biased[e * 2 + 1], i + 2)
                    act.dma_start(z_d[e, bass.ds(i * 2 * P, 2 * P), :].rearrange("(w p) n -> p w n", p=P),
                                  z[:, e, :, :]).then_inc(z_out[e], 16)

            load_y(0)
            with act.Fori(0, NW // 2 - 1) as i:
                body(i, False)
            body(NW // 2 - 1, True)
            for e in range(NX):
                act.wait_ge(z_out[e], 16 * (NW // 2 + 1))

        @block.vector
        def _(v):
            nc.vector.memset(zeros[:, :], 0.0).then_inc(zeroed, 1)
            for j in range(NX * 2):
                v.sem_inc(biased[j], 1)
                if j % 2:
                    v.sem_inc(down[j], 1)
            v.wait_ge(weights, 16 * (2 * NX + 2))
            with v.Fori(0, NW // 2) as i:
                for e in range(NX):
                    v.wait_ge(z_out[e], (i + 1) * 16)
                    for w in range(2):
                        j = e * 2 + w
                        v.wait_ge(down[j], i + 1 + j % 2)
                        nc.vector.tensor_tensor(z[:, e, w, :], pD[j % 4][:, 0:D], b2[:, e, :], ALU.add)\
                            .then_inc(biased[j], 1)


def gate_weights(nc, acc, g, b_gat, gam, bet, below_in):
    with Stage(nc, "gatew") as s:
        ticks, ticks_sp = s.sem("ticks"), s.sem("ticks_sp")
        vec = s.sb("vec", [P, 3, HX])
        below = s.sb("below", [P, NX * NX])
        den = s.sb("den", [P, NW, H])
        a = s.sb("a", [P, NW, HX])
        b = s.sb("b", [P, NW, HX])
        m = s.sb("m", [P, NW])
        r = s.sb("r", [P, NW])
        sc = s.sb("sc", [P, NW, NX])
        cmp = s.sb("cmp", [P, NW, NX, NX])
        eq = s.sb("eq", [P, NW, NX, NX])
        rank = s.sb("rank", [P, NW, NX])
        k1 = s.sb("k1", [P, NW, NX])
        k2 = s.sb("k2", [P, NW, NX])
        s1 = s.sb("s1", [P, NW])
        s2 = s.sb("s2", [P, NW])
        eps = s.sb("eps", [P, 1])
        consts, dve, act_s = s.sem("consts"), s.sem("dve"), s.sem("act")
        block = s.block()
        marks = {}

        @block.sync
        def _(sp):
            for k, src in enumerate((b_gat, gam, bet)):
                sp.dma_start(vec[:, k, :], src.to_broadcast([P, HX])).then_inc(consts, 16)
            sp.dma_start(below[:, :], below_in.to_broadcast([P, NX * NX])).then_inc(consts, 16)

        @block.vector
        def _(v):
            step = Chain(dve)
            tt, ts = nc.vector.tensor_tensor, nc.vector.tensor_scalar

            def row(k):
                return vec[:, k, :].unsqueeze(1).to_broadcast([P, NW, HX])

            def wide(ap, n):
                return ap.unsqueeze(2).to_broadcast([P, NW, n])

            v.wait_ge(consts, 64)
            step(v, nc.vector.memset(eps[:, :], EPS))
            step(v, ts(den[:, :, :], acc[:, :, 0:H], 1e-16, None, ALU.add))
            step(v, nc.vector.reciprocal(den[:, :, :], den[:, :, :]))
            for h in range(H):
                step(v, tt(a[:, :, h * NX:(h + 1) * NX], acc[:, :, H + h * NX:H + (h + 1) * NX],
                           wide(den[:, :, h], NX), ALU.mult))
            step(v, tt(a[:, :, :], a[:, :, :], row(0), ALU.add))
            step(v, nc.vector.tensor_reduce(m[:, :], a[:, :, :], AX.X, ALU.add))
            step(v, ts(m[:, :], m[:, :], 1.0 / HX, None, ALU.mult))
            step(v, tt(a[:, :, :], a[:, :, :], wide(m[:, :], HX), ALU.subtract))
            step(v, tt(b[:, :, :], a[:, :, :], a[:, :, :], ALU.mult))
            step(v, nc.vector.tensor_reduce(r[:, :], b[:, :, :], AX.X, ALU.add))
            step(v, ts(r[:, :], r[:, :], 1.0 / HX, None, ALU.mult))
            marks["var"] = step.n
            v.wait_ge(act_s, 1)
            step(v, nc.vector.reciprocal(r[:, :], r[:, :]))
            step(v, tt(a[:, :, :], a[:, :, :], wide(r[:, :], HX), ALU.mult))
            step(v, tt(a[:, :, :], a[:, :, :], row(1), ALU.mult))
            step(v, tt(a[:, :, :], a[:, :, :], row(2), ALU.add))
            step(v, tt(sc[:, :, :], a[:, :, 0:NX], a[:, :, NX:2 * NX], ALU.add))
            step(v, tt(sc[:, :, :], sc[:, :, :], a[:, :, 2 * NX:3 * NX], ALU.add))
            step(v, tt(sc[:, :, :], sc[:, :, :], a[:, :, 3 * NX:], ALU.add))
            step(v, ts(sc[:, :, :], sc[:, :, :], 1.0 / H, None, ALU.mult))
            for i in range(NX):
                me = wide(sc[:, :, i], NX)
                step(v, tt(cmp[:, :, i, :], sc[:, :, :], me, ALU.is_gt))
                step(v, tt(eq[:, :, i, :], sc[:, :, :], me, ALU.is_equal))
                step(v, tt(eq[:, :, i, :], eq[:, :, i, :],
                           below[:, i * NX:(i + 1) * NX].unsqueeze(1).to_broadcast([P, NW, NX]), ALU.mult))
                step(v, tt(cmp[:, :, i, :], cmp[:, :, i, :], eq[:, :, i, :], ALU.add))
                step(v, nc.vector.tensor_reduce(rank[:, :, i], cmp[:, :, i, :], AX.X, ALU.add))
            step(v, ts(k1[:, :, :], rank[:, :, :], 0.0, None, ALU.is_equal))
            step(v, ts(k2[:, :, :], rank[:, :, :], 1.0, None, ALU.is_equal))
            step(v, tt(a[:, :, 0:NX], sc[:, :, :], k1[:, :, :], ALU.mult))
            step(v, nc.vector.tensor_reduce(s1[:, :], a[:, :, 0:NX], AX.X, ALU.add))
            step(v, tt(a[:, :, 0:NX], sc[:, :, :], k2[:, :, :], ALU.mult))
            step(v, nc.vector.tensor_reduce(s2[:, :], a[:, :, 0:NX], AX.X, ALU.add))
            step(v, tt(s2[:, :], s2[:, :], s1[:, :], ALU.subtract))
            marks["gap"] = step.n
            v.wait_ge(act_s, 2)
            step(v, ts(s1[:, :], s2[:, :], 1.0, None, ALU.add))
            step(v, nc.vector.reciprocal(s1[:, :], s1[:, :]))
            step(v, tt(s2[:, :], s2[:, :], s1[:, :], ALU.mult))
            step(v, tt(k1[:, :, :], k1[:, :, :], wide(s1[:, :], NX), ALU.mult))
            step(v, tt(k2[:, :, :], k2[:, :, :], wide(s2[:, :], NX), ALU.mult))
            step(v, tt(g[:, :, :], k1[:, :, :], k2[:, :, :], ALU.add))

        @block.scalar
        def _(act):
            act.wait_ge(dve, marks["var"])
            nc.scalar.activation(r[:, :], r[:, :], ACT.Sqrt, bias=eps[:, 0:1]).then_inc(act_s, 1)
            act.wait_ge(dve, marks["gap"])
            nc.scalar.activation(s2[:, :], s2[:, :], ACT.Exp).then_inc(act_s, 1)


def mix(nc, g, x2_d, z_d, out_d):
    with Stage(nc, "mix") as s:
        ticks_sp = s.sem("ticks_sp")
        x2 = s.sb("x2", [P, 2, 2, D])
        z = s.sb("z", [P, 2, NX, 2, D])
        here, mixed, out = s.sems("here", 2), s.sems("mixed", 2 * NX * 2), s.sems("out", 2)
        steps = NW // 2
        block = s.block()

        def at(i):
            return bass.ds(i * 2 * P, 2 * P)

        def load(eng, i, b):
            eng.dma_start(x2[:, b, :, :], x2_d[at(i), :].rearrange("(w p) n -> p w n", p=P)).then_inc(here[b], 16)
            for e in range(NX):
                eng.dma_start(z[:, b, e, :, :], z_d[e, at(i), :].rearrange("(w p) n -> p w n", p=P))\
                    .then_inc(here[b], 16)

        @block.sync
        def _(sp):
            load(sp, 0, 0)
            load(sp, 1, 1)
            with sp.Fori(0, steps // 2 - 1) as i:
                for b in range(2):
                    sp.wait_ge(out[b], (i + 1) * 16)
                    sp.sem_inc(ticks_sp, 1)
                    load(sp, i * 2 + 2 + b, b)
            sp.wait_ge(out[0], steps // 2 * 16)
            load(sp, steps - 1, 0)

        @block.vector
        def _(v):
            def blend(i, b, n):
                v.wait_ge(here[b], (n + 1) * 80)
                for e in range(NX):
                    for w in range(2):
                        j = (b * NX + e) * 2 + w
                        if e:
                            v.wait_ge(mixed[j - 2], n + 1)
                        gate = g[:, bass.ds(i * 2 + w, 1), e:e + 1].rearrange("p o n -> p (o n)")
                        nc.vector.scalar_tensor_tensor(x2[:, b, w, :], z[:, b, e, w, :], gate, x2[:, b, w, :],
                                                       ALU.mult, ALU.add).then_inc(mixed[j], 1)

            with v.Fori(0, steps // 2) as i:
                for b in range(2):
                    blend(i * 2 + b, b, i)
            blend(steps - 1, 0, steps // 2)

        @block.scalar
        def _(act):
            def store(i, b, n):
                for w in range(2):
                    act.wait_ge(mixed[(b * NX + NX - 1) * 2 + w], n + 1)
                act.dma_start(out_d[at(i), :].rearrange("(w p) n -> p w n", p=P), x2[:, b, :, :])\
                    .then_inc(out[b], 16)

            with act.Fori(0, steps // 2) as i:
                for b in range(2):
                    store(i * 2 + b, b, i)
            store(steps - 1, 0, steps // 2)
            act.wait_ge(out[0], 16 * (steps // 2 + 1))
            act.wait_ge(out[1], 16 * (steps // 2))


def build(nc, a, out_d):
    def scratch(name, shape, dt=F32):
        return nc.dram_tensor(name, shape, dt, kind="Internal").ap()

    xl_d, xr_d, res_d, x2_d = (scratch(n, (NP, D)) for n in ("xl", "xr", "res", "x2"))
    yT_d = scratch("yT", (NW, P, D))
    z_d = scratch("z", (NX, NP, D))
    tab_d, ad_d = scratch("tab", (NP, H + HX)), scratch("ad", (NP, H))
    lg_d, rec_d = scratch("lg", (NTG * P, H)), scratch("rec", (NTG * P, RV - 1))
    rf_d, fill_d = scratch("rf", (NTF * P, FROW)), scratch("fill", (NTF * P + 2, H))
    sorted_d = scratch("sorted", (NTF * P + 2, 2), I32)
    low_d, start_d = scratch("low", (1, NTF * P), BF16), scratch("start", (P, HI), I32)
    ends_d, back_d = scratch("ends", (P, 2 * H + 2)), scratch("back", (2, H, P))
    key_d = scratch("key", (1, NTG))
    KB = -(-max(KG, KF) // P)
    tile_d, win_d = scratch("tile", (2, KB * P), I32), scratch("win", (1, KB * P))

    node_projections(nc, a["x"], a["w_cat"], a["b_cat"], xl_d, xr_d, res_d, a["ident"])
    edge_logits(nc, a["idx"], a["eaT"], a["w_e"], a["att"], xl_d, xr_d, lg_d)
    segment_max(nc, "gmax", NTG, a["dst_halo"], a["src_lin"], a["ea"], lg_d, rec_d, ends_d, back_d)
    worklist(nc, "gwork", NTG, KG, a["last"], key_d, tile_d, win_d, a["kval"])
    with nc.sbuf_tensor("acc", [P, NW, CG], F32) as acc:
        aggregate_nodes(nc, acc, rec_d, xl_d, tile_d, win_d, a["iota"])
        nodes_after(nc, acc, xl_d, xr_d, res_d, a["x"], a["w_e"], a["att"], a["w_gat"], a["att_src"],
                    a["att_dst"], x2_d, yT_d, tab_d, ad_d, a["ident"])
    sort_by_destination(nc, a["f_dst_tab"], a["f_dst_lin"], a["f_rec"], low_d, start_d, sorted_d, a["ident"],
                        a["iota"], a["tri"], a["part"])
    gate_rows_and_experts(nc, sorted_d, start_d, tab_d, ad_d, fill_d, rf_d, yT_d, a["w1"], a["b1"], a["w2"],
                          a["b2"], z_d)
    segment_max(nc, "fmax", NTF, sorted_d, None, None, rf_d[:, 0:H], rf_d, ends_d, back_d, ad_d, fill_d)
    worklist(nc, "fwork", NTF, KF,
             bass.AP(tensor=sorted_d.tensor, offset=sorted_d.offset + P * 2 + 1, ap=[[1, 1], [P * 2, NTF]]),
             key_d[:, 0:NTF], tile_d, win_d, a["kval"])
    with nc.sbuf_tensor("gates", [P, NW, NX], F32) as g:
        with nc.sbuf_tensor("facc", [P, NW, CF], F32) as facc:
            aggregate_gate(nc, facc, rf_d, tile_d, win_d, a["iota"])
            gate_weights(nc, facc, g, a["b_gat"], a["gamma"], a["beta"], a["below"])
        mix(nc, g, x2_d, z_d, out_d)


def lay_out(v):
    def padded(x, n, fill):
        out = np.full((n,) + x.shape[1:], fill, x.dtype)
        out[:x.shape[0]] = x
        return out

    v = {k: np.asarray(x) for k, x in v.items()}
    src = padded(v["src"], NTG * P, 0)
    dst = padded(v["dst"], NTG * P, NP - 1)
    ea = padded(v["edge_attr_16"], NTG * P, 0)
    loops = np.arange(N, dtype=np.int32)
    ei = v["L0_ffn_edge_index"]
    f_src = padded(np.concatenate([ei[0], loops]), NTF * P, 0)
    f_dst = padded(np.concatenate([ei[1], loops]), NTF * P, HI * P - 1)

    def tiles(x):
        return x.reshape(-1, HALF, P).transpose(0, 2, 1)

    row = np.arange(P, dtype=np.float32)
    kb = -(-max(KG, KF) // P)
    return {
        "x": padded(v["x"], NP, 0),
        "w_cat": np.concatenate([v["L0_gnn_W_l"], v["L0_gnn_W_r"], v["L0_gnn_W_res"]], 1),
        "b_cat": np.concatenate([v["L0_gnn_b_l"], v["L0_gnn_b_r"], v["L0_gnn_bias"]])[None],
        "w_e": v["L0_gnn_W_e"], "att": v["L0_gnn_att"].reshape(1, D),
        "idx": np.concatenate([tiles(src), tiles(dst)], 2),
        "eaT": ea.T, "ea": ea, "src_lin": src,
        "dst_halo": np.concatenate([[-1], dst, [-1]]).astype(np.int32)[:, None],
        "last": dst[P - 1::P][None],
        "w_gat": v["L0_ffn_W_gat"], "att_src": v["L0_ffn_att_src"].reshape(1, HX),
        "att_dst": v["L0_ffn_att_dst"].reshape(1, HX), "b_gat": v["L0_ffn_b_gat"][None],
        "gamma": v["L0_ffn_ln_gamma"][None], "beta": v["L0_ffn_ln_beta"][None],
        "w1": v["L0_ffn_W1"], "w2": v["L0_ffn_W2"],
        "b1": v["L0_ffn_b1"].reshape(NX * FF // P, P).T, "b2": v["L0_ffn_b2"].reshape(1, NX * D),
        "f_dst_tab": f_dst.reshape(NTF, P).T, "f_dst_lin": f_dst[None],
        "f_rec": np.stack([f_src, f_dst], 1).reshape(NTF, P, 2).transpose(1, 0, 2),
        "ident": np.eye(P, dtype=np.float32), "iota": row[None], "part": row[:, None],
        "tri": np.triu(np.ones((P, P), np.float32), 1),
        "kval": np.arange(kb * P, dtype=np.float32).reshape(kb, P).T,
        "below": np.tril(np.ones((NX, NX), np.float32), -1).reshape(1, NX * NX),
    }


def kernel(**inputs):
    import concourse.bacc as bacc
    from concourse.bass_utils import run_bass_kernel_spmd as run

    nc = bacc.Bacc("TRN2", target_bir_lowering=False, num_devices=1)
    arrays = {f"in_{k}": np.ascontiguousarray(x) for k, x in lay_out(inputs).items()}
    aps = {k[3:]: nc.dram_tensor(k, x.shape, mybir.dt.from_np(x.dtype), kind="ExternalInput").ap()
           for k, x in arrays.items()}
    out_d = nc.dram_tensor("out", (NP, D), F32, kind="ExternalOutput").ap()
    build(nc, aps, out_d)
    r = run(nc, [arrays], core_ids=[0])
    return r.results[0]["out"][:N]
```

```python
import numpy as np
from contextlib import ExitStack
import concourse.bass as bass
from concourse import mybir

F32 = mybir.dt.float32
BF16 = mybir.dt.bfloat16
I32 = mybir.dt.int32
ALU = mybir.AluOpType
ACT = mybir.ActivationFunctionType
AX = mybir.AxisListType

P = 128
N = 6250
NW = 50
NP = NW * P
D = 256
H = 4
C = D // H
ED = 16
NX = 4
FF = 512
HX = H * NX
EG = 200000
EF = 131072 + N
U = 8
HALF = U // 2


def tiles_for(edges):
    return -(-edges // (P * U)) * U


NTG = tiles_for(EG)
NTF = tiles_for(EF)
KG = -(-(NTG + NW - 1) // U) * U
KF = -(-(NTF + NW - 1) // (2 * U)) * 2 * U
BIG = 1e30
EPS = 1e-5
SLOPE = 0.2
ROW = 2 + 4 + 4 + ED + 1 + D
RV = ROW - D
WX = D + H + 1
WT = 2 * WX + D
CG = ROW - 2
CF = HX + 1 + H
FROW = H + HX + 1 + H
LAG = 10
HI = 64


class Stage:

    def __init__(self, nc, name):
        self.nc, self.name, self.ctx, self.used = nc, name, ExitStack(), []

    def __enter__(self):
        return self

    def __exit__(self, *a):
        self.ctx.__exit__(*a)
        self.nc.clear_and_free_semaphores(self.used)
        self.nc.all_engine_barrier()

    def sb(self, name, shape, dt=F32):
        return self.ctx.enter_context(self.nc.sbuf_tensor(f"{self.name}_{name}", shape, dt))

    def ps(self, name, shape, dt=F32):
        t = self.ctx.enter_context(self.nc.psum_tensor(f"{self.name}_{name}", [shape[0], 512], dt))
        if len(shape) == 2:
            return t[:, 0:shape[1]]
        return t[:, 0:shape[1] * shape[2]].rearrange("p (a b) -> p a b", a=shape[1])

    def sem(self, name):
        self.used.append(self.nc.alloc_semaphore(f"{self.name}_{name}"))
        return self.used[-1]

    def sems(self, name, n):
        return [self.sem(f"{name}{j}") for j in range(n)]

    def block(self):
        return self.ctx.enter_context(self.nc.Block())


class Chain:

    def __init__(self, sem):
        self.sem, self.n = sem, 0

    def __call__(self, eng, ins):
        self.n += 1
        ins.then_inc(self.sem, 1)
        eng.wait_ge(self.sem, self.n)


def one_hots(nc, h, at, lo, hi, iota, hot_lo, hot_hi):
    nc.vector.tensor_tensor(hot_lo[:, h, :, :], lo[:, at].unsqueeze(2).to_broadcast([P, HALF, P]),
                            iota[:, :].unsqueeze(1).to_broadcast([P, HALF, P]), ALU.is_equal)
    return nc.vector.tensor_tensor(
        hot_hi[:, h, :, :], hi[:, at].unsqueeze(2).to_broadcast([P, HALF, HI]),
        iota[:, 0:HI].unsqueeze(1).to_broadcast([P, HALF, HI]), ALU.is_equal)


def split_destinations(nc, v, step, dt_i, tmp_i, lo, hi):
    step(v, nc.vector.tensor_scalar(tmp_i[:, :], dt_i[:, :], P - 1, None, ALU.bitwise_and))
    step(v, nc.vector.tensor_copy(lo[:, :], tmp_i[:, :]))
    step(v, nc.vector.tensor_scalar(tmp_i[:, :], dt_i[:, :], 7, None, ALU.arith_shift_right))
    step(v, nc.vector.tensor_copy(hi[:, :], tmp_i[:, :]))


def linear_columns(nc, v, step, table, att, prod):
    step(v, nc.vector.tensor_tensor(prod, table[:, 0:D], att, ALU.mult))
    step(v, nc.vector.tensor_reduce(table[:, D:D + H], prod.rearrange("p (h c) -> p h c", h=H), AX.X, ALU.add))
    step(v, nc.vector.tensor_scalar(table[:, D:D + H], table[:, D:D + H], SLOPE, None, ALU.mult))


def node_projections(nc, x, w_cat, b_cat, att_bc, xl_d, xlx_d, xrx_d, res_d, ident_in,
                     dst_tab, dst_lin, low_d, start_d, first_d, sorted_d, iota_in, tri_in):
    with Stage(nc, "proj") as s:
        ticks, ticks_sp = s.sem("ticks"), s.sem("ticks_sp")
        w = s.sb("w", [P, 2, WT])
        att = s.sb("att", [P, D])
        prod = s.sb("prod", [P, D])
        bias = s.sb("bias", [P, WT])
        ident = s.sb("ident", [P, P])
        eps = s.sb("eps", [P, 1])
        xt = s.sb("x", [P, 2, D])
        st = s.sb("st", [P, 2, 6])
        mv = s.sb("mv", [P, 2, 2])
        sd = s.sb("sd", [P, 2])
        rs = s.sb("rs", [P, 2])
        y = s.sb("y", [P, 2, D])
        yT = s.sb("yT", [P, 2, 2, P])
        o = s.sb("o", [P, 2, WT])
        pT = [s.ps(f"pT{u}", [P, 2, P]) for u in range(2)]
        pA = [s.ps(f"pA{u}", [P, 2 * D]) for u in range(2)]
        pB = [s.ps(f"pB{u}", [P, WT - 2 * D]) for u in range(2)]
        iota = s.sb("iota", [P, P])
        tri = s.sb("tri", [P, P])
        ones = s.sb("ones", [P, P])
        dt_i = s.sb("dt_i", [P, NTF], I32)
        dl_i = s.sb("dl_i", [P, NTF], I32)
        tmp_i = s.sb("tmp_i", [P, NTF], I32)
        lowf = s.sb("lowf", [P, NTF], BF16)
        lo = s.sb("lo", [P, NTF])
        hi = s.sb("hi", [P, NTF])
        hot_lo = s.sb("hot_lo", [P, 2, HALF, P], BF16)
        hot_hi = s.sb("hot_hi", [P, 2, HALF, HI], BF16)
        cnt0 = s.sb("cnt0", [P, HI])
        tot = s.sb("tot", [P, HI])
        base = s.sb("base", [P, HI])
        first = s.sb("first", [P, HI])
        starti = s.sb("starti", [P, HI], I32)
        edge = s.sb("edge", [1, 2, 2], I32)
        pc = s.ps("pc", [P, 512])
        pr = s.ps("pr", [P, 512])
        dests, dve, pef, ended = s.sem("dests"), s.sem("dve"), s.sem("pef"), s.sem("ended")
        first_hot, first_used = s.sems("first_hot", 2), s.sems("first_used", 2)
        BODIES, GROUPS = NW // 2, NTF // U
        PER = GROUPS // BODIES
        halves = [(j, h) for j in range(PER) for h in range(2)]
        marks = {}
        consts = s.sem("consts")
        eps_set, lined = s.sem("eps_set"), s.sem("lined")
        loaded, stats, aggr, rooted, inverted, normed, turned, copied, products, summed, stored = (
            s.sems(n, 2) for n in ("loaded", "stats", "aggr", "rooted", "inverted", "normed", "turned",
                                   "copied", "products", "summed", "stored"))
        block = s.block()

        @block.vector
        def _(v):
            nc.vector.memset(eps[:, :], EPS).then_inc(eps_set, 1)
            v.wait_ge(consts, 64)
            step = Chain(lined)
            for tab in (w[:, 0, :], w[:, 1, :], bias[:, :]):
                for k in range(2):
                    linear_columns(nc, v, step, tab[:, k * WX:(k + 1) * WX], att[:, :], prod[:, :])
            step = Chain(dve)
            step(v, nc.vector.memset(edge[:, :, :], -1))
            step(v, nc.vector.memset(ones[:, :], 1.0))
            step(v, nc.vector.memset(cnt0[:, :], 0.0))
            marks["zeroed"] = step.n
            v.wait_ge(dests, 64)
            step(v, nc.vector.tensor_scalar(tmp_i[:, :], dl_i[:, :], P - 1, None, ALU.bitwise_and))
            step(v, nc.vector.tensor_copy(lowf[:, :], tmp_i[:, :]))
            marks["low"] = step.n
            split_destinations(nc, v, step, dt_i, tmp_i, lo, hi)
            for h in range(2):
                v.sem_inc(first_used[h], 1)

            def compare(i, pieces, per):
                for j, h in pieces:
                    v.wait_ge(first_used[h], i * per + j + 1)
                    one_hots(nc, h, bass.ds((i * per + j) * U + h * HALF, HALF), lo, hi, iota, hot_lo, hot_hi)\
                        .then_inc(first_hot[h], 1)

            def statistics(i):
                for u in range(2):
                    v.wait_ge(loaded[u], (i + 1) * 16)
                    nc.vector.bn_stats(st[:, u, :], xt[:, u, :]).then_inc(stats[u], 1)
                for u in range(2):
                    v.wait_ge(stats[u], i + 1)
                    v.sem_inc(ticks, 1)
                    nc.vector.bn_aggr(mv[:, u, :], st[:, u, :]).then_inc(aggr[u], 1)

            def body(i, last):
                for u in range(2):
                    v.wait_ge(rooted[u], i + 1)
                    nc.vector.reciprocal(rs[:, u:u + 1], sd[:, u:u + 1]).then_inc(inverted[u], 1)
                for u in range(2):
                    v.wait_ge(inverted[u], i + 1)
                    v.wait_ge(turned[u], i + 1)
                    nc.vector.tensor_scalar(y[:, u, :], xt[:, u, :], mv[:, u, 0:1], rs[:, u:u + 1],
                                            ALU.subtract, ALU.mult).then_inc(normed[u], 1)
                compare(i, halves[:PER], PER)
                if not last:
                    statistics(i + 1)
                compare(i, halves[PER:], PER)
                for u in range(2):
                    v.wait_ge(products[u], i + 1)
                    v.wait_ge(stored[u], (i + 1) * 64)
                    nc.vector.tensor_tensor(o[:, u, 0:2 * D], pA[u][:, :], bias[:, 0:2 * D], ALU.add)
                    nc.vector.tensor_tensor(o[:, u, 2 * D:], pB[u][:, :], bias[:, 2 * D:], ALU.add)\
                        .then_inc(summed[u], 1)

            statistics(0)
            with v.Fori(0, BODIES - 1) as i:
                body(i, False)
            body(BODIES - 1, True)
            with v.Fori(PER * BODIES, GROUPS) as i:
                compare(i, [(0, 0), (0, 1)], 1)
            v.wait_ge(pef, 1)
            step(v, nc.vector.tensor_copy(cnt0[:, :], pc[:, 0:HI]))
            marks["counted"] = step.n
            v.wait_ge(pef, 3)
            step(v, nc.vector.tensor_copy(tot[:, :], pr[:, 0:HI]))
            step(v, nc.vector.tensor_tensor_scan(base[:, :], ones[:, 0:HI], tot[:, :], 0.0, ALU.mult, ALU.add))
            step(v, nc.vector.tensor_tensor(base[:, :], base[:, :], tot[:, :], ALU.subtract))
            step(v, nc.vector.tensor_scalar(base[:, :], base[:, :], 1.0, None, ALU.add))
            step(v, nc.vector.tensor_tensor(first[:, :], base[:, :], pr[:, 128:128 + HI], ALU.add))
            step(v, nc.vector.tensor_copy(starti[:, :], first[:, :]))
            marks["started"] = step.n

        @block.sync
        def _(sp):
            sp.dma_start(w[:, :, :], w_cat.rearrange("(c p) n -> p c n", p=P)).then_inc(consts, 16)
            sp.dma_start(bias[:, :], b_cat.to_broadcast([P, WT])).then_inc(consts, 16)
            sp.dma_start(att[:, :], att_bc.to_broadcast([P, D])).then_inc(consts, 16)
            sp.dma_start(ident[:, :], ident_in).then_inc(consts, 16)
            sp.dma_start(iota[:, :], iota_in.to_broadcast([P, P])).then_inc(dests, 16)
            sp.dma_start(tri[:, :], tri_in).then_inc(dests, 16)
            sp.dma_start(dt_i[:, :], dst_tab).then_inc(dests, 16)
            sp.dma_start(dl_i[:, :], dst_lin.rearrange("o (p n) -> (o p) n", p=P)).then_inc(dests, 16)
            for u in range(2):
                sp.sem_inc(normed[u], 1)
            with sp.Fori(0, NW // 2) as i:
                for u in range(2):
                    sp.wait_ge(normed[u], i + 1)
                    sp.sem_inc(ticks_sp, 1)
                    sp.dma_start(xt[:, u, :], x[bass.ds((i * 2 + u) * P, P), :]).then_inc(loaded[u], 16)
            sp.wait_ge(dve, marks["low"])
            sp.dma_start(sorted_d[0:1, :], edge[:, 0, :]).then_inc(ended, 16)
            sp.dma_start(sorted_d[NTF * P + 1:, :], edge[:, 1, :]).then_inc(ended, 16)
            sp.dma_start(low_d.rearrange("o (p n) -> (o p) n", p=P), lowf[:, :]).then_inc(ended, 16)
            sp.wait_ge(dve, marks["started"])
            sp.dma_start(start_d, starti[:, :]).then_inc(ended, 16)
            sp.dma_start(first_d, first[:, :]).then_inc(ended, 16)
            sp.wait_ge(ended, 80)
            for u in range(2):
                sp.wait_ge(stored[u], 64 * (NW // 2 + 1))

        @block.scalar
        def _(act):
            act.wait_ge(eps_set, 1)
            for u in range(2):
                act.sem_inc(stored[u], 64)

            def roots(i):
                for u in range(2):
                    act.wait_ge(aggr[u], i + 1)
                    nc.scalar.activation(sd[:, u:u + 1], mv[:, u, 1:2], ACT.Sqrt, bias=eps[:, 0:1])\
                        .then_inc(rooted[u], 1)

            def body(i, last):
                for u in range(2):
                    act.wait_ge(turned[u], i + 2)
                    nc.scalar.copy(yT[:, u, :, :], pT[u][:, :, :]).then_inc(copied[u], 1)
                if not last:
                    roots(i + 1)
                for u in range(2):
                    act.wait_ge(summed[u], i + 1)
                    at = bass.ds((i * 2 + u) * P, P)
                    act.dma_start(xl_d[at, :], o[:, u, 0:D]).then_inc(stored[u], 16)
                    act.dma_start(xlx_d[at, :], o[:, u, 0:WX]).then_inc(stored[u], 16)
                    act.dma_start(xrx_d[at, :], o[:, u, WX:2 * WX]).then_inc(stored[u], 16)
                    act.dma_start(res_d[at, :], o[:, u, 2 * WX:]).then_inc(stored[u], 16)

            roots(0)
            with act.Fori(0, BODIES - 1) as i:
                body(i, False)
            body(BODIES - 1, True)

        @block.tensor
        def _(pe):
            pe.wait_ge(consts, 64)
            pe.wait_ge(lined, 3 * 2 * 3)
            for u in range(2):
                pe.sem_inc(turned[u], 1)
            pe.wait_ge(dests, 64)
            pe.wait_ge(dve, marks["zeroed"])
            nc.tensor.matmul(pc[:, 0:HI], ident[:, :], cnt0[:, :], start=True, stop=False)

            def count(i, pieces, per):
                for j, h in pieces:
                    pe.wait_ge(first_hot[h], i * per + j + 1)
                    for k in range(HALF):
                        last = nc.tensor.matmul(pc[:, 0:HI], hot_lo[:, h, k, :], hot_hi[:, h, k, :],
                                                start=False, stop=False)
                    last.then_inc(first_used[h], 1)

            with pe.Fori(0, NW // 2) as i:
                for u in range(2):
                    pe.wait_ge(normed[u], i + 2)
                    nc.tensor.transpose(pT[u][:, 0, :], y[:, u, 0:P], ident[:, :])
                    nc.tensor.transpose(pT[u][:, 1, :], y[:, u, P:], ident[:, :]).then_inc(turned[u], 1)
                count(i, halves[:PER], PER)
                for u in range(2):
                    pe.wait_ge(copied[u], i + 1)
                    for c in range(2):
                        nc.tensor.matmul(pA[u][:, :], yT[:, u, c, :], w[:, c, 0:2 * D],
                                         start=(c == 0), stop=(c == 1))
                    for c in range(2):
                        last = nc.tensor.matmul(pB[u][:, :], yT[:, u, c, :], w[:, c, 2 * D:],
                                                start=(c == 0), stop=(c == 1))
                    last.then_inc(products[u], 1)
                count(i, halves[PER:], PER)
            with pe.Fori(PER * BODIES, GROUPS) as i:
                count(i, [(0, 0), (0, 1)], 1)
            nc.tensor.matmul(pc[:, 0:HI], ident[:, :], cnt0[:, :], start=False, stop=True).then_inc(pef, 1)
            pe.wait_ge(dve, marks["counted"])
            nc.tensor.matmul(pr[:, 0:HI], ones[:, :], cnt0[:, :], start=True, stop=True).then_inc(pef, 1)
            nc.tensor.matmul(pr[:, 128:128 + HI], tri[:, :], cnt0[:, :], start=True, stop=True).then_inc(pef, 1)


def edge_logits(nc, idx_in, dst_lin, eaT_d, w_e, att_bc, xlx_d, xrx_d, tile_d, win_d, part_in, logit_d):
    nb, G = KG // U, 5
    with Stage(nc, "logit") as s:
        ticks_sp, ticks_pool = s.sem("ticks_sp"), s.sem("ticks_pool")
        we = s.sb("we", [ED, WX])
        prod = s.sb("prod", [P, D])
        att = s.sb("att", [P, D])
        part = s.sb("part", [P, 1])
        base = s.sb("base", [P, KG])
        tt = s.sb("tt", [1, 2, KG], I32)
        src_all = s.sb("src_all", [P, NTG], I32)
        xw = s.sb("xw", [P, 2, G, WX])
        xr = s.sb("xr", [P, NW, 3, WX], BF16)
        dstb = s.sb("dstb", [P, U, P], I32)
        hot = s.sb("hot", [P, U, P], BF16)
        ea = s.sb("ea", [ED, U, P])
        idx = s.sb("idx", [P, U], I32)
        z = s.sb("z", [P, U, WX])
        lg = s.sb("lg", [P, U, H])
        logits = s.sb("logits", [P, NTG, H])
        psum = [s.ps(f"p{u}", [P, WX]) for u in range(U)]
        consts, dve, flushed, split = s.sem("consts"), s.sem("dve"), s.sem("flushed"), s.sem("split")
        wloaded, part1, rest1, part2, rest2, part3 = (
            s.sems(n, 2) for n in ("wloaded", "part1", "rest1", "part2", "rest2", "part3"))
        loaded, indexed, gathered, hotted, multiplied, summed, positive, scaled, reduced, whole, kept = (
            s.sems(n, U) for n in ("loaded", "indexed", "gathered", "hotted", "multiplied", "summed",
                                   "positive", "scaled", "reduced", "whole", "kept"))
        block = s.block()
        ready = 6

        def first(i):
            return isinstance(i, int) and i == 0

        def exists(i, k):
            return k < U and (k >= 0 or not first(i))

        def slot(i, k):
            return (k, i) if k >= 0 else (k + U, i - 1)

        def values(eng, row, at):
            return nc.values_load_multi_w_load_instructions(
                tt[0:1, row, at], engines=[eng.engine], min_val=0, max_val=(NTG, NW)[row] - 1,
                skip_runtime_bounds_check_because="the worklist clamps its tiles and windows")[1]

        @block.sync
        def _(sp):
            with nc.allow_non_contiguous_dma(reason="one word of a partition"):
                sp.dma_start(part[:, :], part_in).then_inc(consts, 16)
            sp.dma_start(we[:, :], w_e).then_inc(consts, 16)
            sp.dma_start(att[:, :], att_bc.to_broadcast([P, D])).then_inc(consts, 16)
            sp.dma_start(base[:, :], win_d[:, 0:KG].to_broadcast([P, KG])).then_inc(consts, 16)
            sp.dma_start(tt[0:1, :, :], tile_d[:, 0:KG].rearrange("(o j) n -> o j n", o=1)).then_inc(consts, 16)
            sp.dma_start(src_all[:, :], idx_in).then_inc(consts, 16)
            for g in range(NW // G):
                if g >= 2:
                    sp.wait_ge(part3[g % 2], g // 2)
                sp.dma_start(xw[:, g % 2, :, :], xrx_d[g * G * P:(g + 1) * G * P, :]
                             .rearrange("(w p) n -> p w n", p=P)).then_inc(wloaded[g % 2], 16)
            sp.wait_ge(consts, 96)

            def load(i):
                tiles = values(sp, 0, bass.ds(i * U, U))
                for u in range(U):
                    sp.wait_ge(multiplied[u], i + 1)
                    sp.sem_inc(ticks_sp, 1)
                    at = bass.ds(tiles[u] * P, P)
                    sp.dma_start(dstb[:, u, :], dst_lin[:, at].to_broadcast([P, P])).then_inc(loaded[u], 16)
                    sp.dma_start(ea[:, u, :], eaT_d[:, at]).then_inc(loaded[u], 16)

            with sp.Fori(0, LAG) as i:
                load(i)
            with sp.Fori(LAG, nb) as i:
                load(i)
                sp.wait_ge(kept[U - 1], i - 1)
                sp.sem_inc(ticks_sp, 1)
                sp.dma_start(logit_d[bass.ds((i - LAG) * U * P, U * P), :].rearrange("(t p) c -> p t c", p=P),
                             logits[:, bass.ds((i - LAG) * U, U), :]).then_inc(flushed, 16)
            sp.wait_ge(kept[U - 1], nb + 1)
            first = (nb - LAG) * U
            sp.dma_start(logit_d[first * P:, :].rearrange("(t p) c -> p t c", p=P), logits[:, first:, :])\
                .then_inc(flushed, 16)
            sp.wait_ge(flushed, 16 * (nb - LAG + 1))

        @block.gpsimd
        def _(pool):
            for u in range(U):
                pool.sem_inc(kept[u], 1)
            with pool.Fori(0, nb) as i:
                for u in range(U):
                    pool.wait_ge(indexed[u], i + 1)
                    pool.wait_ge(kept[u], i + 1)
                    pool.sem_inc(ticks_pool, 1)
                    pool.indirect_dma_start(
                        out=z[:, u, :], out_offset=None, in_=xlx_d,
                        in_offset=bass.IndirectOffsetOnAxis(ap=idx[:, u:u + 1], axis=0)).then_inc(gathered[u], 16)

        @block.tensor
        def _(pe):
            pe.wait_ge(consts, 96)
            pe.wait_ge(dve, ready)
            for h in range(2):
                pe.wait_ge(part3[h], NW // G // 2)
            for u in range(U):
                pe.sem_inc(multiplied[u], 1)
                pe.sem_inc(summed[u], 1)
            with pe.Fori(0, nb) as i:
                windows = values(pe, 1, bass.ds(i * U, U))
                for u in range(U):
                    pe.wait_ge(hotted[u], i + 1)
                    pe.wait_ge(summed[u], i + 1)
                    nc.tensor.matmul(psum[u][:, :], ea[:, u, :], we[:, :], start=True, stop=False)
                    for k in range(3):
                        last = nc.tensor.matmul(
                            psum[u][:, :], hot[:, u, :],
                            xr[:, bass.ds(windows[u], 1), k, :].rearrange("p o n -> p (o n)"),
                            start=False, stop=(k == 2))
                    last.then_inc(multiplied[u], 1)

        @block.vector
        def _(v):
            step = Chain(dve)
            v.wait_ge(consts, 96)
            step(v, nc.vector.memset(logits[:, :, :], 0.0))
            linear_columns(nc, v, step, we[:, :], att[0:ED, :], prod[0:ED, :])
            step(v, nc.vector.tensor_scalar(att[:, :], att[:, :], 1.0 - SLOPE, None, ALU.mult))
            step(v, nc.vector.tensor_scalar(base[:, :], base[:, :], part[:, 0:1], None, ALU.add))
            for g in range(0, NW // G, 2):
                for k, (part_done, rest) in enumerate(((part1, rest1), (part2, rest2))):
                    for h in range(2):
                        v.wait_ge(part_done[h], g // 2 + 1)
                        nc.vector.tensor_tensor(xw[:, h, :, :], xw[:, h, :, :],
                                                xr[:, (g + h) * G:(g + h + 1) * G, k, :], ALU.subtract)\
                            .then_inc(rest[h], 1)

            def steps(i, ks, tile_of):
                for k in ks:
                    if k < U:
                        v.wait_ge(loaded[k], (i + 1) * 32)
                        nc.vector.tensor_scalar(hot[:, k, :], dstb[:, k, :], base[:, bass.ds(i * U + k, 1)],
                                                None, ALU.is_equal).then_inc(hotted[k], 1)
                    if exists(i, k - 3):
                        u, b = slot(i, k - 3)
                        v.wait_ge(positive[u], b + 1)
                        nc.vector.tensor_tensor(z[:, u, 0:D], z[:, u, 0:D], att[:, :], ALU.mult)\
                            .then_inc(scaled[u], 1)
                    if exists(i, k - 2):
                        u, b = slot(i, k - 2)
                        v.wait_ge(gathered[u], (b + 1) * 16)
                        v.wait_ge(multiplied[u], b + 2)
                        nc.vector.tensor_tensor(z[:, u, :], z[:, u, :], psum[u][:, :], ALU.add)\
                            .then_inc(summed[u], 1)
                    if exists(i, k - 3):
                        u, b = slot(i, k - 3)
                        v.wait_ge(scaled[u], b + 1)
                        nc.vector.tensor_reduce(lg[:, u, :], z[:, u, 0:D].rearrange("p (h c) -> p h c", h=H),
                                                AX.X, ALU.add).then_inc(reduced[u], 1)
                    if exists(i, k - 4):
                        u, b = slot(i, k - 4)
                        v.wait_ge(reduced[u], b + 1)
                        nc.vector.tensor_tensor(lg[:, u, :], lg[:, u, :], z[:, u, D:D + H], ALU.add)\
                            .then_inc(whole[u], 1)
                    if exists(i, k - 5):
                        u, b = slot(i, k - 5)
                        v.wait_ge(whole[u], b + 1)
                        v.wait_ge(kept[(u - 1) % U], b + 2 if u else b + 1)
                        at = bass.ds(tile_of[k], 1)
                        nc.vector.scalar_tensor_tensor(
                            logits[:, at, :].rearrange("p o n -> p (o n)"), lg[:, u, :], z[:, u, WX - 1:WX],
                            logits[:, at, :].rearrange("p o n -> p (o n)"), ALU.mult, ALU.add)\
                            .then_inc(kept[u], 1)

            steps(0, range(U), dict(zip(range(5, U + 5), values(v, 0, slice(0, U)))))
            with v.Fori(1, nb) as i:
                steps(i, range(U), values(v, 0, bass.ds(i * U - 5, U)))
            steps(nb - 1, range(U, U + 5), dict(zip(range(U, U + 5), values(v, 0, slice(nb * U - 5, nb * U)))))

        @block.scalar
        def _(act):
            act.wait_ge(consts, 96)
            for g in range(0, NW // G, 2):
                for k, (ready_for, part_done) in enumerate(((wloaded, part1), (rest1, part2), (rest2, part3))):
                    for h in range(2):
                        act.wait_ge(ready_for[h], (g // 2 + 1) * (1 if k else 16))
                        nc.scalar.copy(xr[:, (g + h) * G:(g + h + 1) * G, k, :], xw[:, h, :, :])\
                            .then_inc(part_done[h], 1)

            def steps(i, ks, tile_of):
                for k in ks:
                    if k < U:
                        if not first(i):
                            act.wait_ge(gathered[k], i * 16)
                        nc.scalar.copy(idx[:, k:k + 1], src_all[:, bass.ds(tile_of[k], 1)])\
                            .then_inc(indexed[k], 1)
                    if exists(i, k - 3):
                        u, b = slot(i, k - 3)
                        act.wait_ge(summed[u], b + 2)
                        nc.scalar.activation(z[:, u, 0:D], z[:, u, 0:D], ACT.Relu).then_inc(positive[u], 1)

            steps(0, range(U), values(act, 0, slice(0, U)))
            with act.Fori(1, nb) as i:
                steps(i, range(U), values(act, 0, bass.ds(i * U, U)))
            steps(nb - 1, range(U, U + 3), None)


def segment_max(nc, name, nt, dst_halo, src_lin, ea_d, logit_d, rec_d, carry_d, back_d, ad_d=None, fill_d=None):
    with Stage(nc, name) as s:
        ticks, ticks_sp = s.sem("ticks"), s.sem("ticks_sp")
        words = 2 + 2 * H if src_lin is not None else 1 + H
        oa = words - H * (2 if src_lin is not None else 1)
        width = dst_halo.shape[1]
        dh = s.sb("dst", [P, (nt + 2) * width], I32)
        dv = dh[:, :].rearrange("p (n w) -> p n w", w=width)[:, :, width - 1]
        sl = s.sb("src", [P, nt], I32)
        L = s.sb("L", [P, nt, H])
        F = s.sb("F", [P, nt, H])
        B = s.sb("B", [P, nt])
        pf = s.sb("pf", [P, nt])
        pb = s.sb("pb", [P, nt])
        rec = s.sb("rec", [P, nt, words])
        ends = s.sb("ends", [P, 2 * H + 2])
        endT = s.sb("endT", [H, 2, P])
        path = s.sb("path", [H, 2, P])
        Z = s.sb("Z", [H, 2, P + 2])
        carry = s.sb("carry", [P, 2, H])
        first = s.sb("first", [P, 1], I32)
        first_ad = s.sb("first_ad", [P, H])
        loads, dve, moved, expd, out, firsts = (s.sem(n) for n in ("loads", "dve", "moved", "expd", "out", "firsts"))
        block = s.block()
        marks = {}

        @block.vector
        def _(v):
            step = Chain(dve)
            v.wait_ge(loads, 16 * 3)
            cur = dv[:, 1:nt + 1]
            step(v, nc.vector.tensor_tensor(pf[:, :], dv[:, 0:nt], cur, ALU.not_equal))
            step(v, nc.vector.tensor_scalar(pf[:, :], pf[:, :], -BIG, None, ALU.mult))
            step(v, nc.vector.tensor_tensor(pb[:, :], dv[:, 2:nt + 2], cur, ALU.not_equal))
            step(v, nc.vector.tensor_scalar(pb[:, :], pb[:, :], -BIG, None, ALU.mult))
            step(v, nc.vector.tensor_copy(rec[:, :, oa - 1], cur))
            if src_lin is not None:
                step(v, nc.vector.tensor_copy(rec[:, :, 0].bitcast(I32), sl[:, :]))
            if ad_d is not None:
                step(v, nc.vector.tensor_scalar(first[:, :], dv[:, 1:2], float(N - 1), None, ALU.min))
                marks["first"] = step.n
                step(v, nc.vector.tensor_scalar(B[:, :], pf[:, :], 0.0, None, ALU.is_equal))
                v.wait_ge(firsts, 16)
                for h in range(H):
                    step(v, nc.vector.tensor_tensor_scan(F[:, :, h], B[:, :], F[:, :, h], first_ad[:, h:h + 1],
                                                         ALU.mult, ALU.add))
                step(v, nc.vector.tensor_tensor(L[:, :, :], L[:, :, :], F[:, :, :], ALU.add))
                step(v, nc.vector.scalar_tensor_tensor(L[:, :, :], L[:, :, :], SLOPE, L[:, :, :],
                                                       ALU.mult, ALU.max))
            for h in range(H):
                step(v, nc.vector.tensor_tensor_scan(F[:, :, h], pf[:, :], L[:, :, h], -BIG, ALU.add, ALU.max))
                step(v, nc.vector.tensor_tensor_scan(B[:, ::-1], pb[:, ::-1], L[:, ::-1, h], -BIG,
                                                     ALU.add, ALU.max))
                step(v, nc.vector.tensor_copy(ends[:, h:h + 1], F[:, nt - 1, h:h + 1]))
                step(v, nc.vector.tensor_copy(ends[:, H + h:H + h + 1], B[:, 0:1]))
            step(v, nc.vector.tensor_tensor(ends[:, 2 * H:2 * H + 1], dv[:, 0:1], dv[:, nt:nt + 1], ALU.not_equal))
            step(v, nc.vector.tensor_tensor(ends[:, 2 * H + 1:2 * H + 2], dv[:, 1:2], dv[:, nt + 1:nt + 2],
                                            ALU.not_equal))
            step(v, nc.vector.tensor_scalar(ends[:, 2 * H:], ends[:, 2 * H:], -BIG, None, ALU.mult))
            step(v, nc.vector.memset(Z[:, :, :], -BIG))
            marks["ends"] = step.n
            v.wait_ge(moved, 16 * 5)
            step(v, nc.vector.tensor_tensor_scan(Z[:, 0, 1:P + 1], path[:, 0, :], endT[:, 0, :], -BIG,
                                                 ALU.add, ALU.max))
            step(v, nc.vector.tensor_tensor_scan(Z[:, 1, P:0:-1], path[:, 1, ::-1], endT[:, 1, ::-1], -BIG,
                                                 ALU.add, ALU.max))
            marks["carry"] = step.n
            v.wait_ge(moved, 16 * 9)
            for h in range(H):
                step(v, nc.vector.tensor_tensor_scan(F[:, :, h], pf[:, :], L[:, :, h], carry[:, 0, h:h + 1],
                                                     ALU.add, ALU.max))
                step(v, nc.vector.tensor_tensor_scan(B[:, ::-1], pb[:, ::-1], L[:, ::-1, h],
                                                     carry[:, 1, h:h + 1], ALU.add, ALU.max))
                step(v, nc.vector.tensor_tensor(B[:, :], B[:, :], F[:, :, h], ALU.max))
                step(v, nc.vector.tensor_tensor(L[:, :, h], L[:, :, h], B[:, :], ALU.subtract))
                if src_lin is not None:
                    step(v, nc.vector.scalar_tensor_tensor(rec[:, :, oa + H + h], pb[:, :], 0.0, B[:, :],
                                                           ALU.is_lt, ALU.mult))
            marks["all"] = step.n

        if ad_d is not None:
            @block.gpsimd
            def _(pool):
                pool.wait_ge(dve, marks["first"])
                pool.indirect_dma_start(out=first_ad[:, :], out_offset=None, in_=ad_d,
                                        in_offset=bass.IndirectOffsetOnAxis(ap=first[:, 0:1], axis=0))\
                    .then_inc(firsts, 16)

        @block.scalar
        def _(act):
            act.wait_ge(dve, marks["all"])
            nc.scalar.activation(rec[:, :, oa:oa + H], L[:, :, :], ACT.Exp).then_inc(expd, 1)

        @block.sync
        def _(sp):
            rows = bass.AP(tensor=dst_halo.tensor, offset=dst_halo.offset,
                           ap=[[nt * width, P], [1, (nt + 2) * width]])
            sp.dma_start(dh[:, :], rows).then_inc(loads, 16)
            sp.dma_start(L[:, :, :], logit_d.rearrange("(p n) h -> p n h", p=P)).then_inc(loads, 16)
            if src_lin is not None:
                sp.dma_start(sl[:, :], src_lin.rearrange("(p n) -> p n", p=P)).then_inc(loads, 16)
                sp.dma_start(rec_d[:, words:].rearrange("(p n) w -> p n w", p=P),
                             ea_d.rearrange("(p n) w -> p n w", p=P)).then_inc(out, 16)
            else:
                sp.dma_start(F[:, :, :], fill_d[1:nt * P + 1, :].rearrange("(p n) h -> p n h", p=P))\
                    .then_inc(loads, 16)
            sp.wait_ge(dve, marks["ends"])
            sp.dma_start(carry_d, ends[:, :]).then_inc(moved, 16)
            sp.wait_ge(moved, 16)
            with nc.allow_non_contiguous_dma(reason="512 ends, turned"):
                for k in range(2):
                    sp.dma_start(endT[:, k, :], carry_d[:, k * H:(k + 1) * H].rearrange("p h -> h p"))\
                        .then_inc(moved, 16)
                    sp.dma_start(path[:, k, :], carry_d[:, 2 * H + k:2 * H + k + 1].rearrange("p o -> o p")
                                 .to_broadcast([H, P])).then_inc(moved, 16)
            sp.wait_ge(dve, marks["carry"])
            sp.dma_start(back_d[0, :, :], Z[:, 0, 0:P]).then_inc(moved, 16)
            sp.dma_start(back_d[1, :, :], Z[:, 1, 2:P + 2]).then_inc(moved, 16)
            sp.wait_ge(moved, 16 * 7)
            with nc.allow_non_contiguous_dma(reason="512 ends, turned back"):
                for k in range(2):
                    sp.dma_start(carry[:, k, :], back_d[k, :, :].rearrange("h p -> p h")).then_inc(moved, 16)
            sp.wait_ge(expd, 1)
            to = rec_d[:, 0:words] if src_lin is not None else rec_d[:, H + HX:]
            sp.dma_start(to.rearrange("(p n) w -> p n w", p=P), rec[:, :, :]).then_inc(out, 16)
            sp.wait_ge(out, 32 if src_lin is not None else 16)


def worklist(nc, name, nt, nk, last_d, key_d, tile_d, win_d, kval_in):
    with Stage(nc, name) as s:
        ticks, ticks_sp = s.sem("ticks"), s.sem("ticks_sp")
        NB = kval_in.shape[1]
        li = s.sb("li", [1, nt], I32)
        wf = s.sb("wf", [1, nt])
        tf = s.sb("tf", [1, nt])
        key = s.sb("key", [P, nt])
        junk = s.sb("junk", [P, nt])
        kv = s.sb("kv", [P, NB])
        tk = s.sb("tk", [P, NB])
        wk = s.sb("wk", [P, NB])
        far = s.sb("far", [P, NB])
        ti = s.sb("ti", [P, 2, NB], I32)
        wm = s.sb("wm", [P, NB])
        dve, moved, tiled = s.sem("dve"), s.sem("moved"), s.sem("tiled")
        block = s.block()
        marks = {}

        @block.gpsimd
        def _(pool):
            nc.gpsimd.iota(tf[:, :], [[1, nt]], base=0, channel_multiplier=0,
                           allow_small_or_imprecise_dtypes=True).then_inc(tiled, 1)

        @block.vector
        def _(v):
            step = Chain(dve)
            v.wait_ge(moved, 32)
            v.wait_ge(tiled, 1)
            step(v, nc.vector.tensor_scalar(li[:, :], li[:, :], 7, None, ALU.arith_shift_right))
            step(v, nc.vector.tensor_scalar(wf[:, :], li[:, :], float(NW - 1), None, ALU.min))
            step(v, nc.vector.tensor_tensor(wf[:, :], wf[:, :], tf[:, :], ALU.add))
            marks["key"] = step.n
            v.wait_ge(moved, 64)
            for b in range(NB):
                step(v, nc.vector.tensor_scalar(junk[:, :], key[:, :], kv[:, b:b + 1], None, ALU.is_lt,
                                                ALU.add, accum_out=tk[:, b:b + 1]))
            step(v, nc.vector.tensor_scalar(tk[:, :], tk[:, :], float(nt - 1), None, ALU.min))
            step(v, nc.vector.tensor_tensor(wk[:, :], kv[:, :], tk[:, :], ALU.subtract))
            step(v, nc.vector.tensor_scalar(far[:, :], wk[:, :], float(NW), 1e6, ALU.is_ge, ALU.mult))
            step(v, nc.vector.tensor_scalar(wm[:, :], wk[:, :], float(P), None, ALU.mult))
            step(v, nc.vector.tensor_tensor(wm[:, :], wm[:, :], far[:, :], ALU.add))
            step(v, nc.vector.tensor_copy(ti[:, 0, :], tk[:, :]))
            step(v, nc.vector.tensor_scalar(ti[:, 1, :], wk[:, :], float(NW - 1), None, ALU.min))
            marks["all"] = step.n

        @block.sync
        def _(sp):
            with nc.allow_non_contiguous_dma(reason="one word of a tile or pair"):
                sp.dma_start(li[:, :], last_d).then_inc(moved, 16)
                sp.dma_start(kv[:, :], kval_in).then_inc(moved, 16)
                sp.wait_ge(dve, marks["key"])
                sp.dma_start(key_d, wf[:, :]).then_inc(moved, 16)
                sp.wait_ge(moved, 48)
                sp.dma_start(key[:, :], key_d.to_broadcast([P, nt])).then_inc(moved, 16)
                sp.wait_ge(dve, marks["all"])
                for j in range(2):
                    sp.dma_start(tile_d[j, :].rearrange("(b p) -> p b", p=P), ti[:, j, :]).then_inc(moved, 16)
                sp.dma_start(win_d[0, :].rearrange("(b p) -> p b", p=P), wm[:, :]).then_inc(moved, 16)
            sp.wait_ge(moved, 64 + 48)


def aggregate(nc, name, s, nt, nk, acc, cols, tile_d, win_d, iota_in, load, gather, weigh, rhs, dst_col):
    iota = s.sb("iota", [P, P])
    wb = s.sb("wb", [P, nk])
    tt = s.sb("tt", [1, 2, nk], I32)
    hot = s.sb("hot", [P, U, P])
    part = [s.ps(f"part{u}", [P, 512]) for u in range(U)]
    ticks_sp, ticks_act, ticks_pool = s.sem("ticks_agg"), s.sem("ticks_agg_act"), s.sem("ticks_pool")
    consts, cleared = s.sem("consts"), s.sem("cleared")
    loaded, gathered, hotted, weighed, summed, added = (
        s.sems(n, U) for n in ("loaded", "gathered", "hotted", "weighed", "summed", "added"))
    block = s.block()

    def loads(eng, first, ticks):
        with eng.Fori(0, nk // U) as i:
            _, tiles = nc.values_load_multi_w_load_instructions(
                tt[0:1, 0, bass.ds(i * U, U)], engines=[eng.engine], min_val=0, max_val=nt - 1,
                skip_runtime_bounds_check_because="the worklist clamps its tiles")
            for u in range(first, U, 2):
                t = tiles[u]
                eng.wait_ge(summed[u], i + 1)
                eng.sem_inc(ticks, 1)
                load(eng, u, t, loaded[u])

    @block.sync
    def _(sp):
        sp.dma_start(iota[:, :], iota_in.to_broadcast([P, P])).then_inc(consts, 16)
        sp.dma_start(wb[:, :], win_d[:, 0:nk].to_broadcast([P, nk])).then_inc(consts, 16)
        sp.dma_start(tt[0:1, :, :], tile_d[:, 0:nk].rearrange("(o j) n -> o j n", o=1)).then_inc(consts, 16)
        sp.wait_ge(consts, 48)
        loads(sp, 0, ticks_sp)

    @block.scalar
    def _(act):
        act.wait_ge(consts, 48)
        loads(act, 1, ticks_act)

    @block.gpsimd
    def _(pool):
        for u in range(U):
            pool.sem_inc(weighed[u], 1)
        with pool.Fori(0, nk // U) as i:
            for u in range(U):
                pool.wait_ge(loaded[u], (i + 1) * 16)
                pool.wait_ge(weighed[u], i + 1)
                pool.sem_inc(ticks_pool, 1)
                gather(pool, u).then_inc(gathered[u], 16)

    @block.tensor
    def _(pe):
        for u in range(U):
            pe.sem_inc(summed[u], 1)
        with pe.Fori(0, nk // U) as i:
            for u in range(U):
                pe.wait_ge(weighed[u], i + 2)
                pe.wait_ge(hotted[u], i + 1)
                pe.wait_ge(added[u], i + 1)
                nc.tensor.matmul(part[u][:, 0:cols], hot[:, u, :], rhs(u), start=True, stop=True)\
                    .then_inc(summed[u], 1)

    @block.vector
    def _(v):
        nc.vector.memset(acc[:, :, :], 0.0).then_inc(cleared, 1)
        for u in range(U):
            v.sem_inc(added[u], 1)
        v.wait_ge(consts, 48)
        v.wait_ge(cleared, 1)

        def steps(i, us, windows):
            for n, u in enumerate(us):
                if u < U:
                    v.wait_ge(loaded[u], (i + 1) * 16)
                    v.wait_ge(summed[u], i + 1)
                    nc.vector.tensor_scalar(hot[:, u, :], iota[:, :], wb[:, bass.ds(i * U + u, 1)], dst_col(u),
                                            ALU.add, ALU.is_equal).then_inc(hotted[u], 1)
                    v.wait_ge(gathered[u], (i + 1) * 16)
                    weigh(u).then_inc(weighed[u], 1)
                if windows[n] is not None:
                    at, body = ((u - 2) % U, i if u >= 2 else i - 1)
                    v.wait_ge(summed[at], body + 2)
                    v.wait_ge(added[(at - 1) % U], body + (2 if at else 1))
                    nc.vector.tensor_tensor(acc[:, bass.ds(windows[n], 1), :].rearrange("p o n -> p (o n)"),
                                            acc[:, bass.ds(windows[n], 1), :].rearrange("p o n -> p (o n)"),
                                            part[at][:, 0:cols], ALU.add).then_inc(added[at], 1)

        def windows_of(at):
            return list(nc.values_load_multi_w_load_instructions(
                tt[0:1, 1, at], engines=[v.engine], min_val=0, max_val=NW - 1,
                skip_runtime_bounds_check_because="the worklist clamps its windows")[1])

        steps(0, range(U), [None, None] + windows_of(slice(0, U)))
        with v.Fori(1, nk // U) as i:
            steps(i, range(U), windows_of(bass.ds(i * U - 2, U)))
        steps(nk // U - 1, range(U, U + 2), windows_of(slice(nk - 2, nk)))


def aggregate_nodes(nc, acc, rec_d, xl_d, tile_d, win_d, iota_in):
    with Stage(nc, "aggr") as s:
        ticks, ticks_sp = s.sem("ticks"), s.sem("ticks_sp")
        row = s.sb("row", [P, U, ROW])
        xg = s.sb("xg", [P, U, D])
        ones = s.sem("ones")
        with nc.Block() as block:
            @block.vector
            def _(v):
                nc.vector.memset(row[:, :, RV - 1:RV], 1.0).then_inc(ones, 1)
                v.wait_ge(ones, 1)

        def load(sp, u, t, loaded):
            at = bass.ds(t * P, P)
            sp.dma_start(row[:, u, 0:RV - 1], rec_d[at, :]).then_inc(loaded, 16)

        def gather(pool, u):
            return pool.indirect_dma_start(
                out=xg[:, u, :], out_offset=None, in_=xl_d,
                in_offset=bass.IndirectOffsetOnAxis(ap=row[:, u, 0:1].bitcast(I32), axis=0))

        def weigh(u):
            return nc.vector.tensor_tensor(
                row[:, u, RV:].rearrange("p (h c) -> p h c", h=H), xg[:, u, :].rearrange("p (h c) -> p h c", h=H),
                row[:, u, 2:2 + H].unsqueeze(2).to_broadcast([P, H, C]), ALU.mult)

        aggregate(nc, "aggr", s, NTG, KG, acc, CG, tile_d, win_d, iota_in, load, gather, weigh,
                  lambda u: row[:, u, 2:], lambda u: row[:, u, 1:2])


def aggregate_gate(nc, acc, rec_d, tile_d, win_d, iota_in):
    B = 2 * U
    bodies, groups = KF // B, -(-NTF // B)
    with Stage(nc, "gaggr") as s:
        ticks_pool = s.sem("ticks_pool")
        SLOTS = 3
        row = s.sb("row", [P, SLOTS, B, CF])
        sums = s.sb("sums", [P, 2, NW, 3 * CF])
        parts = s.sb("parts", [P, NTF, 3, CF], BF16)
        dst = s.sb("dst", [P, NTF])
        iota = s.sb("iota", [P, P])
        base = s.sb("base", [P, KF])
        tt = s.sb("tt", [1, 2, KF], I32)
        rel = s.sb("rel", [P, 2, U])
        hot = s.sb("hot", [P, 2, U, P], BF16)
        part = [s.ps(f"part{u}", [P, 3 * CF]) for u in range(U)]
        consts, cleared, weighed, shifted = s.sem("consts"), s.sem("cleared"), s.sem("weighed"), s.sem("shifted")
        joined = s.sem("joined")
        own = s.sem("own")
        loaded = s.sems("loaded", groups)
        relative, hotted = s.sems("relative", 2), s.sems("hotted", 2)
        summed, added = s.sems("summed", U), s.sems("added", U)
        block = s.block()

        def values(eng, row, at):
            return nc.values_load_multi_w_load_instructions(
                tt[0:1, row, at], engines=[eng.engine], min_val=0, max_val=(NTF, NW)[row] - 1,
                skip_runtime_bounds_check_because="the worklist clamps its tiles and windows")[1]

        @block.sync
        def _(sp):
            sp.dma_start(tt[0:1, :, :], tile_d[:, 0:KF].rearrange("(o j) n -> o j n", o=1)).then_inc(consts, 16)
            sp.dma_start(base[:, :], win_d[:, 0:KF].to_broadcast([P, KF])).then_inc(consts, 16)
            sp.dma_start(iota[:, :], iota_in.to_broadcast([P, P])).then_inc(consts, 16)
            for g in range(groups):
                n = min(B, NTF - g * B)
                if g >= SLOTS:
                    sp.wait_ge(weighed, g - SLOTS + 1)
                sp.dma_start(row[:, g % SLOTS, 0:n, :], rec_d[g * B * P:(g * B + n) * P, H:]
                             .rearrange("(t p) n -> p t n", p=P)).then_inc(loaded[g], 16)

        @block.gpsimd
        def _(pool):
            step = Chain(own)
            for g in range(groups):
                at = slice(g * B, min((g + 1) * B, NTF))
                n = at.stop - at.start
                r = row[:, g % SLOTS, 0:n, :]
                pool.wait_ge(loaded[g], 16)
                step(pool, nc.gpsimd.tensor_tensor(
                    r[:, :, 0:HX].rearrange("p t (h c) -> p t h c", h=H),
                    r[:, :, 0:HX].rearrange("p t (h c) -> p t h c", h=H),
                    r[:, :, HX + 1:].unsqueeze(3).to_broadcast([P, n, H, NX]), ALU.mult))
                nc.gpsimd.tensor_copy(dst[:, at], r[:, :, HX])
                for j in range(2):
                    step(pool, nc.gpsimd.tensor_copy(parts[:, at, j, :], r))
                    step(pool, nc.gpsimd.tensor_tensor(r, r, parts[:, at, j, :], ALU.subtract))
                nc.gpsimd.tensor_copy(parts[:, at, 2, :], r).then_inc(weighed, 1)
            pool.wait_ge(weighed, groups)
            for g in range(groups, bodies):
                pool.sem_inc(weighed, 1)

        @block.scalar
        def _(act):
            act.wait_ge(consts, 48)
            act.wait_ge(shifted, 1)
            for h in range(2):
                act.sem_inc(hotted[h], 1)
            with act.Fori(0, bodies) as i:
                tiles = values(act, 0, bass.ds(i * B, B))
                act.wait_ge(weighed, i + 1)
                for h in range(2):
                    act.wait_ge(hotted[h], i + 1)
                    for u in range(U):
                        k = h * U + u
                        done = nc.scalar.activation(
                            rel[:, h, u:u + 1], dst[:, bass.ds(tiles[k], 1)],
                            ACT.Identity, bias=base[:, bass.ds(i * B + k, 1)])
                    done.then_inc(relative[h], 1)

        @block.tensor
        def _(pe):
            pe.wait_ge(consts, 48)
            for u in range(U):
                pe.sem_inc(added[u], 1)
            with pe.Fori(0, bodies) as i:
                tiles = values(pe, 0, bass.ds(i * B, B))
                pe.wait_ge(weighed, i + 1)
                for h in range(2):
                    pe.wait_ge(hotted[h], i + 2)
                    for u in range(U):
                        pe.wait_ge(added[u], 2 * i + h + 1)
                        nc.tensor.matmul(
                            part[u][:, :], hot[:, h, u, :],
                            parts[:, bass.ds(tiles[h * U + u], 1), :, :].rearrange("p o j n -> p (o j n)"),
                            start=True, stop=True).then_inc(summed[u], 1)

        @block.vector
        def _(v):
            nc.vector.memset(sums[:, :, :, :], 0.0).then_inc(cleared, 1)
            v.wait_ge(consts, 48)
            nc.vector.tensor_scalar(base[:, :], base[:, :], -1.0, None, ALU.mult).then_inc(shifted, 1)
            v.wait_ge(cleared, 1)

            def compare(i, h):
                v.wait_ge(relative[h], i + 1)
                nc.vector.tensor_tensor(hot[:, h, :, :], iota[:, :].unsqueeze(1).to_broadcast([P, U, P]),
                                        rel[:, h, :].unsqueeze(2).to_broadcast([P, U, P]), ALU.is_equal)\
                    .then_inc(hotted[h], 1)

            def add(i, h, windows):
                for u in range(U):
                    v.wait_ge(summed[u], 2 * i + h + 1)
                    v.wait_ge(added[(u - 2) % U], 2 * i + h + (2 if u >= 2 else 1))
                    at = bass.ds(windows[u], 1)
                    to = sums[:, u % 2, at, :].rearrange("p o n -> p (o n)")
                    nc.vector.tensor_tensor(to, to, part[u][:, :], ALU.add).then_inc(added[u], 1)

            windows = values(v, 1, slice(0, U))
            compare(0, 0)
            compare(0, 1)
            add(0, 0, windows)
            with v.Fori(1, bodies) as i:
                windows = values(v, 1, bass.ds(i * B - U, B))
                compare(i, 0)
                add(i - 1, 1, windows[0:U])
                compare(i, 1)
                add(i, 0, windows[U:])
            add(bodies - 1, 1, values(v, 1, slice(KF - U, KF)))
            for u in (U - 2, U - 1):
                v.wait_ge(added[u], 2 * bodies + 1)
            step = Chain(joined)
            step(v, nc.vector.tensor_tensor(sums[:, 0, :, :], sums[:, 0, :, :], sums[:, 1, :, :], ALU.add))
            step(v, nc.vector.tensor_tensor(acc[:, :, :], sums[:, 0, :, 0:CF], sums[:, 0, :, CF:2 * CF], ALU.add))
            step(v, nc.vector.tensor_tensor(acc[:, :, :], acc[:, :, :], sums[:, 0, :, 2 * CF:], ALU.add))


def nodes_after(nc, acc, xl_d, xr_d, res_d, x_d, w_e, att_bc, w_gat, asrc_bc, adst_bc, x2_d, yT_d, tab_d, ad_d,
                ident_in):
    with Stage(nc, "after") as s:
        ticks, ticks_sp = s.sem("ticks"), s.sem("ticks_sp")
        we = s.sb("we", [ED, D])
        wg = s.sb("wg", [P, 2, HX])
        att = s.sb("att", [P, D])
        asr = s.sb("asr", [P, 2, HX])
        ident = s.sb("ident", [P, P])
        eps = s.sb("eps", [P, 1])
        xl = s.sb("xl", [P, 2, D])
        xr = s.sb("xr", [P, 2, D])
        rs = s.sb("res", [P, 2, D])
        xx = s.sb("x", [P, 2, D])
        la = s.sb("la", [P, NW, ED])
        las = s.sb("las", [P, 2, ED])
        laT = s.sb("laT", [ED, 2, P])
        cnt = s.sb("cnt", [P, NW])
        ml = s.sb("ml", [P, NW, H])
        slf = s.sb("slf", [P, NW, H])
        mx = s.sb("mx", [P, NW, H])
        c1 = s.sb("c1", [P, NW, H])
        c2 = s.sb("c2", [P, NW, H])
        den = s.sb("den", [P, NW, H])
        t = s.sb("t", [P, 2, D])
        q = s.sb("q", [P, 2, D])
        st = s.sb("st", [P, 2, 6])
        mv = s.sb("mv", [P, 2, 2])
        sd = s.sb("sd", [P, 2])
        rq = s.sb("rq", [P, 2])
        yT = s.sb("yT", [P, 2, 2, P])
        tab = s.sb("tab", [P, 2, H + HX])
        pr = s.sb("pr", [P, 2, 2, HX])
        ad = s.sb("ad", [P, 2, H])
        pL = [s.ps(f"pL{u}", [ED, P]) for u in range(2)]
        pE = [s.ps(f"pE{u}", [P, D]) for u in range(2)]
        pT = [s.ps(f"pT{u}", [P, 2, P]) for u in range(2)]
        pH = [s.ps(f"pH{u}", [P, HX]) for u in range(2)]
        consts, dve, expd = s.sem("consts"), s.sem("dve"), s.sem("expd")
        counts = {}

        def sems(names):
            for n in names.split():
                counts[n] = s.sems(n, 2)
            return counts

        S = sems("loaded picked turned copied edge s1 s2 s3 s4 s5")
        with nc.Block() as block:
            @block.sync
            def _(sp):
                sp.dma_start(we[:, :], w_e).then_inc(consts, 16)
                sp.dma_start(att[:, :], att_bc.to_broadcast([P, D])).then_inc(consts, 16)
                sp.dma_start(ident[:, :], ident_in).then_inc(consts, 16)
                sp.dma_start(wg[:, :, :], w_gat.rearrange("(c p) n -> p c n", p=P)).then_inc(consts, 16)
                sp.dma_start(asr[:, 0, :], asrc_bc.to_broadcast([P, HX])).then_inc(consts, 16)
                sp.dma_start(asr[:, 1, :], adst_bc.to_broadcast([P, HX])).then_inc(consts, 16)
                with sp.Fori(0, NW // 2) as i:
                    for u in range(2):
                        at = bass.ds((i * 2 + u) * P, P)
                        sp.wait_ge(S["s5"][u], i + 1)
                        sp.sem_inc(ticks_sp, 1)
                        sp.dma_start(xl[:, u, :], xl_d[at, :]).then_inc(S["loaded"][u], 16)
                        sp.dma_start(xr[:, u, :], xr_d[at, :]).then_inc(S["loaded"][u], 16)

            @block.vector
            def _(v):
                step = Chain(dve)
                step(v, nc.vector.memset(eps[:, :], EPS))
                step(v, nc.vector.tensor_scalar(cnt[:, :], acc[:, :, 2 * H + ED], 1.0, None, ALU.max))
                step(v, nc.vector.reciprocal(cnt[:, :], cnt[:, :]))
                step(v, nc.vector.tensor_tensor(la[:, :, :], acc[:, :, 2 * H:2 * H + ED],
                                                cnt[:, :].unsqueeze(2).to_broadcast([P, NW, ED]), ALU.mult))
                for u in range(2):
                    v.sem_inc(S["s5"][u], 1)
                v.wait_ge(consts, 96)
                with v.Fori(0, NW // 2) as i:
                    for u in range(2):
                        v.wait_ge(S["edge"][u], i + 1)
                        v.wait_ge(S["loaded"][u], (i + 1) * 32)
                        nc.vector.tensor_tensor(t[:, u, :], xl[:, u, :], pE[u][:, :], ALU.add)\
                            .then_inc(S["s1"][u], 1)
                    for u in range(2):
                        v.wait_ge(S["s1"][u], i + 1)
                        nc.vector.tensor_tensor(t[:, u, :], t[:, u, :], xr[:, u, :], ALU.add)\
                            .then_inc(S["s2"][u], 1)
                    for u in range(2):
                        v.wait_ge(S["s2"][u], i + 1)
                        nc.vector.scalar_tensor_tensor(t[:, u, :], t[:, u, :], SLOPE, t[:, u, :],
                                                       ALU.mult, ALU.max).then_inc(S["s3"][u], 1)
                    for u in range(2):
                        v.wait_ge(S["s3"][u], i + 1)
                        nc.vector.tensor_tensor(t[:, u, :], t[:, u, :], att[:, :], ALU.mult)\
                            .then_inc(S["s4"][u], 1)
                    for u in range(2):
                        v.wait_ge(S["s4"][u], i + 1)
                        nc.vector.tensor_reduce(
                            slf[:, bass.ds(i * 2 + u, 1), :].rearrange("p o h -> p (o h)"),
                            t[:, u, :].rearrange("p (h c) -> p h c", h=H), AX.X, ALU.add)\
                            .then_inc(S["s5"][u], 1)
                v.wait_ge(S["s5"][1], NW // 2 + 1)
                step(v, nc.vector.tensor_scalar(cnt[:, :], acc[:, :, 2 * H + ED], 0.0, -BIG, ALU.is_equal, ALU.mult))
                step(v, nc.vector.tensor_tensor(ml[:, :, :], acc[:, :, H:2 * H],
                                                cnt[:, :].unsqueeze(2).to_broadcast([P, NW, H]), ALU.add))
                step(v, nc.vector.tensor_tensor(mx[:, :, :], ml[:, :, :], slf[:, :, :], ALU.max))
                step(v, nc.vector.tensor_tensor(ml[:, :, :], ml[:, :, :], mx[:, :, :], ALU.subtract))
                step(v, nc.vector.tensor_tensor(slf[:, :, :], slf[:, :, :], mx[:, :, :], ALU.subtract))
                counts["shifted"] = step.n
                v.wait_ge(expd, 2)
                step(v, nc.vector.tensor_tensor(den[:, :, :], acc[:, :, 0:H], c1[:, :, :], ALU.mult))
                step(v, nc.vector.tensor_tensor(den[:, :, :], den[:, :, :], c2[:, :, :], ALU.add))
                step(v, nc.vector.reciprocal(den[:, :, :], den[:, :, :]))
                step(v, nc.vector.tensor_tensor(c1[:, :, :], c1[:, :, :], den[:, :, :], ALU.mult))
                step(v, nc.vector.tensor_tensor(c2[:, :, :], c2[:, :, :], den[:, :, :], ALU.mult))

            @block.tensor
            def _(pe):
                pe.wait_ge(consts, 96)
                pe.wait_ge(dve, 4)
                with pe.Fori(0, NW // 2) as i:
                    for u in range(2):
                        pe.wait_ge(S["picked"][u], i + 1)
                        nc.tensor.transpose(pL[u][:, :], las[:, u, :], ident[:, :]).then_inc(S["turned"][u], 1)
                    for u in range(2):
                        pe.wait_ge(S["copied"][u], i + 1)
                        pe.wait_ge(S["s5"][u], i + 1)
                        nc.tensor.matmul(pE[u][:, :], laT[:, u, :], we[:, :], start=True, stop=True)\
                            .then_inc(S["edge"][u], 1)

            @block.scalar
            def _(act):
                act.wait_ge(dve, 4)
                for u in range(2):
                    act.sem_inc(S["edge"][u], 1) if False else None
                with act.Fori(0, NW // 2) as i:
                    for u in range(2):
                        act.wait_ge(S["s5"][u], i + 1)
                        nc.scalar.copy(las[:, u, :], la[:, bass.ds(i * 2 + u, 1), :]
                                       .rearrange("p o n -> p (o n)")).then_inc(S["picked"][u], 1)
                    for u in range(2):
                        act.wait_ge(S["turned"][u], i + 1)
                        nc.scalar.copy(laT[:, u, :], pL[u][:, :]).then_inc(S["copied"][u], 1)
                act.wait_ge(dve, counts["shifted"])
                nc.scalar.activation(c1[:, :, :], ml[:, :, :], ACT.Exp).then_inc(expd, 1)
                nc.scalar.activation(c2[:, :, :], slf[:, :, :], ACT.Exp).then_inc(expd, 1)

        R = {n: s.sems(f"b_{n}", 2) for n in ("loaded", "w", "wl", "o", "o2", "mn", "ex", "m1", "el", "x2",
                                              "st", "ag", "sq", "rc", "y", "turn", "cp", "h", "hc", "pr", "tb",
                                              "store")}
        with nc.Block() as block:
            @block.sync
            def _(sp):
                for u in range(2):
                    sp.sem_inc(R["loaded"][u], 64)
                with sp.Fori(0, NW // 2) as i:
                    for u in range(2):
                        at = bass.ds((i * 2 + u) * P, P)
                        sp.wait_ge(R["y"][u], i + 1)
                        sp.sem_inc(ticks_sp, 1)
                        sp.wait_ge(R["store"][u], (i + 1) * 64)
                        sp.sem_inc(ticks_sp, 1)
                        sp.dma_start(xl[:, u, :], xl_d[at, :]).then_inc(R["loaded"][u], 16)
                        sp.dma_start(rs[:, u, :], res_d[at, :]).then_inc(R["loaded"][u], 16)
                        sp.dma_start(xx[:, u, :], x_d[at, :]).then_inc(R["loaded"][u], 16)
                    for u in range(2):
                        at = bass.ds((i * 2 + u) * P, P)
                        sp.wait_ge(R["tb"][u], i + 1)
                        sp.sem_inc(ticks_sp, 1)
                        sp.dma_start(tab_d[at, :], tab[:, u, :]).then_inc(R["store"][u], 16)
                        sp.dma_start(ad_d[at, :], ad[:, u, :]).then_inc(R["store"][u], 16)
                for u in range(2):
                    sp.wait_ge(R["store"][u], 64 * (NW // 2 + 1))

            @block.vector
            def _(v):
                for u in range(2):
                    v.sem_inc(R["y"][u], 1)
                with v.Fori(0, NW // 2) as i:
                    def each(first, fn, done):
                        for u in range(2):
                            for sem, plus in first:
                                v.wait_ge(R[sem][u], (i + plus) if sem not in ("loaded", "store") else
                                          (i + plus) * (48 if sem == "loaded" else 64))
                            if done == "ag":
                                v.sem_inc(ticks, 1)
                            fn(u).then_inc(R[done][u], 1)

                    def win(buf, lo, hi):
                        return lambda u: buf[:, bass.ds(i * 2 + u, 1), lo:hi].rearrange("p o n -> p (o n)")

                    def heads(ap):
                        return ap.rearrange("p (h c) -> p h c", h=H)

                    tt = nc.vector.tensor_tensor
                    values, w1, w2 = win(acc, CG - D, CG), win(c1, 0, H), win(c2, 0, H)
                    each([("y", 1)], lambda u: tt(
                        heads(t[:, u, :]), heads(values(u)), w1(u).unsqueeze(2).to_broadcast([P, H, C]),
                        ALU.mult), "w")
                    for u in range(2):
                        v.wait_ge(R["loaded"][u], (i + 1) * 48 + 64)
                        tt(heads(q[:, u, :]), heads(xl[:, u, :]), w2(u).unsqueeze(2).to_broadcast([P, H, C]),
                           ALU.mult).then_inc(R["wl"][u], 1)
                    each([("w", 1), ("wl", 1)], lambda u: tt(t[:, u, :], t[:, u, :], q[:, u, :], ALU.add), "o")
                    each([("o", 1)], lambda u: tt(t[:, u, :], t[:, u, :], rs[:, u, :], ALU.add), "o2")
                    each([("o2", 1)], lambda u: nc.vector.tensor_scalar(q[:, u, :], t[:, u, :], 0.0, None, ALU.min), "mn")
                    each([("o2", 1)], lambda u: nc.vector.tensor_scalar(t[:, u, :], t[:, u, :], 0.0, -1.0, ALU.max,
                                                                        ALU.add), "m1")
                    each([("ex", 1), ("m1", 1)], lambda u: tt(t[:, u, :], t[:, u, :], q[:, u, :], ALU.add), "el")
                    each([("el", 1), ("store", 1)], lambda u: tt(xx[:, u, :], xx[:, u, :], t[:, u, :], ALU.add), "x2")
                    each([("x2", 1)], lambda u: nc.vector.bn_stats(st[:, u, :], xx[:, u, :]), "st")
                    each([("st", 1)], lambda u: nc.vector.bn_aggr(mv[:, u, :], st[:, u, :]), "ag")
                    each([("sq", 1)], lambda u: nc.vector.reciprocal(rq[:, u:u + 1], sd[:, u:u + 1]), "rc")
                    each([("rc", 1), ("turn", 1)], lambda u: nc.vector.tensor_scalar(
                        q[:, u, :], xx[:, u, :], mv[:, u, 0:1], rq[:, u:u + 1], ALU.subtract, ALU.mult), "y")
                    each([("h", 1)], lambda u: nc.vector.tensor_copy(tab[:, u, H:], pH[u][:, :]), "hc")
                    each([("hc", 1)], lambda u: tt(
                        pr[:, u, :, :], asr[:, :, :], tab[:, u, H:].unsqueeze(1).to_broadcast([P, 2, HX]),
                        ALU.mult), "pr")
                    for u in range(2):
                        v.wait_ge(R["pr"][u], i + 1)
                        nc.vector.tensor_reduce(tab[:, u, 0:H], pr[:, u, 0, :].rearrange("p (h c) -> p h c", h=H),
                                                AX.X, ALU.add)
                        nc.vector.tensor_reduce(ad[:, u, :], pr[:, u, 1, :].rearrange("p (h c) -> p h c", h=H),
                                                AX.X, ALU.add).then_inc(R["tb"][u], 1)

            @block.scalar
            def _(act):
                for u in range(2):
                    act.sem_inc(R["store"][u], 64)
                with act.Fori(0, NW // 2) as i:
                    for u in range(2):
                        act.wait_ge(R["mn"][u], i + 1)
                        nc.scalar.activation(q[:, u, :], q[:, u, :], ACT.Exp).then_inc(R["ex"][u], 1)
                    for u in range(2):
                        act.wait_ge(R["x2"][u], i + 1)
                        act.dma_start(x2_d[bass.ds((i * 2 + u) * P, P), :], xx[:, u, :]).then_inc(R["store"][u], 16)
                    for u in range(2):
                        act.wait_ge(R["ag"][u], i + 1)
                        nc.scalar.activation(sd[:, u:u + 1], mv[:, u, 1:2], ACT.Sqrt, bias=eps[:, 0:1])\
                            .then_inc(R["sq"][u], 1)
                    for u in range(2):
                        act.wait_ge(R["turn"][u], i + 2)
                        act.wait_ge(R["store"][u], (i + 1) * 64)
                        nc.scalar.copy(yT[:, u, :, :], pT[u][:, :, :]).then_inc(R["cp"][u], 1)
                    for u in range(2):
                        act.wait_ge(R["cp"][u], i + 1)
                        act.dma_start(yT_d[bass.ds(i * 2 + u, 1), :, :].rearrange("o p n -> (o p) n"),
                                      yT[:, u, :, :].rearrange("p c n -> p (c n)")).then_inc(R["store"][u], 16)

            @block.tensor
            def _(pe):
                for u in range(2):
                    pe.sem_inc(R["turn"][u], 1)
                with pe.Fori(0, NW // 2) as i:
                    for u in range(2):
                        pe.wait_ge(R["y"][u], i + 2)
                        nc.tensor.transpose(pT[u][:, 0, :], q[:, u, 0:P], ident[:, :])
                        nc.tensor.transpose(pT[u][:, 1, :], q[:, u, P:], ident[:, :]).then_inc(R["turn"][u], 1)
                    for u in range(2):
                        pe.wait_ge(R["cp"][u], i + 1)
                        for c in range(2):
                            last = nc.tensor.matmul(pH[u][:, :], yT[:, u, c, :], wg[:, c, :],
                                                    start=(c == 0), stop=(c == 1))
                        last.then_inc(R["h"][u], 1)


def sort_by_destination(nc, dst_tab, rec_in, low_d, first_d, sorted_d, ident_in, iota_in, tri_in, part_in):
    with Stage(nc, "sort") as s:
        ticks, ticks_sp = s.sem("ticks"), s.sem("ticks_sp")
        iota = s.sb("iota", [P, P])
        ident = s.sb("ident", [P, P])
        tri = s.sb("tri", [P, P])
        part = s.sb("part", [P, 1])
        dt_i = s.sb("dt_i", [P, NTF], I32)
        tmp_i = s.sb("tmp_i", [P, NTF], I32)
        rows = s.sb("rows", [P, NTF, 2], I32)
        lo = s.sb("lo", [P, NTF])
        hi = s.sb("hi", [P, NTF])
        hot_lo = s.sb("hot_lo", [P, 2, HALF, P], BF16)
        hot_hi = s.sb("hot_hi", [P, 2, HALF, HI], BF16)
        tri_b = s.sb("tri_b", [P, P], BF16)
        lrow = s.sb("lrow", [P, 2, HALF * P], BF16)
        hot_t = s.sb("hot_t", [P, 2, HALF * P])
        same = s.sb("same", [P, U, P], BF16)
        cur = s.sb("cur", [P, 2, HI])
        picked = s.sb("picked", [P, 2, HALF, HI])
        pos = s.sb("pos", [P, 2, HALF])
        posi = s.sb("posi", [P, 2, HALF], I32)
        rec = s.sb("rec", [P, 2, HALF, 2], I32)
        pl = [s.ps(f"pl{h}", [P, HALF, HI]) for h in range(2)]
        pn = [s.ps(f"pn{u}", [P, HI]) for u in range(2)]
        consts, dve = s.sem("consts"), s.sem("dve")
        GROUPS = NTF // U

        with nc.Block() as block:
            @block.vector
            def _(v):
                step = Chain(dve)
                v.wait_ge(consts, 112)
                step(v, nc.vector.tensor_copy(tri_b[:, :], tri[:, :]))
                step(v, nc.vector.tensor_scalar(rows[:, :, 0], rows[:, :, 0], float(N - 1), None, ALU.min))
                split_destinations(nc, v, step, dt_i, tmp_i, lo, hi)

            @block.sync
            def _(sp):
                sp.dma_start(iota[:, :], iota_in.to_broadcast([P, P])).then_inc(consts, 16)
                sp.dma_start(ident[:, :], ident_in).then_inc(consts, 16)
                sp.dma_start(tri[:, :], tri_in).then_inc(consts, 16)
                sp.dma_start(part[:, :], part_in).then_inc(consts, 16)
                sp.dma_start(dt_i[:, :], dst_tab).then_inc(consts, 16)
                sp.dma_start(rows[:, :, :], rec_in).then_inc(consts, 16)
                sp.dma_start(cur[:, 0, :], first_d).then_inc(consts, 16)

        loaded, hots, masks, picks, sums, placed, freed = (
            s.sems(f"r_{n}", 2) for n in ("loaded", "hots", "masks", "picks", "sums", "placed", "freed"))
        counted, looked, wrote, current = (
            s.sems(f"r_{n}", U) for n in ("counted", "looked", "wrote", "current"))
        steps = s.sem("steps")
        with nc.Block() as block:
            @block.sync
            def _(sp):
                with sp.Fori(0, GROUPS) as i:
                    for h in range(2):
                        sp.wait_ge(masks[h], i + 1)
                        sp.sem_inc(ticks_sp, 1)
                        sp.dma_start(lrow[:, h, :], low_d[:, bass.ds((i * 2 + h) * HALF * P, HALF * P)]
                                     .to_broadcast([P, HALF * P])).then_inc(loaded[h], 16)

            @block.vector
            def _(v):
                for u in range(U):
                    v.sem_inc(looked[u], 1)
                for h in range(2):
                    v.sem_inc(masks[h], 1)

                def build_masks(i, h):
                    v.wait_ge(loaded[h], (i + 1) * 16)
                    for u in range(h * HALF, (h + 1) * HALF):
                        v.wait_ge(looked[u], i + 1)
                    v.wait_ge(picks[h], i + 1)
                    one_hots(nc, h, bass.ds(i * U + h * HALF, HALF), lo, hi, iota, hot_lo, hot_hi)\
                        .then_inc(hots[h], 1)
                    nc.vector.tensor_scalar(hot_t[:, h, :], lrow[:, h, :], part[:, 0:1], None, ALU.is_equal)
                    for k in range(HALF):
                        u = h * HALF + k
                        last = nc.vector.scalar_tensor_tensor(
                            same[:, u, :], lrow[:, h, k * P:(k + 1) * P], lo[:, bass.ds(i * U + u, 1)],
                            tri_b[:, :], ALU.is_equal, ALU.mult)
                    last.then_inc(masks[h], 1)

                def place(i, h):
                    v.wait_ge(looked[h * HALF + HALF - 1], i + 2)
                    nc.vector.tensor_tensor(picked[:, h, :, :], pl[h], hot_hi[:, h, :, :], ALU.mult)\
                        .then_inc(picks[h], 1)
                    v.wait_ge(picks[h], i + 2)
                    nc.vector.tensor_reduce(pos[:, h, :], picked[:, h, :, :], AX.X, ALU.add).then_inc(sums[h], 1)
                    v.wait_ge(sums[h], i + 1)
                    v.wait_ge(freed[h], i + 1)
                    nc.vector.tensor_copy(rec[:, h, :, :], rows[:, bass.ds(i * U + h * HALF, HALF), :])
                    nc.vector.tensor_copy(posi[:, h, :], pos[:, h, :]).then_inc(placed[h], 1)

                for h in range(2):
                    v.sem_inc(picks[h], 1)
                build_masks(0, 0)
                with v.Fori(0, GROUPS - 1) as i:
                    build_masks(i, 1)
                    place(i, 0)
                    build_masks(i + 1, 0)
                    place(i, 1)
                build_masks(GROUPS - 1, 1)
                place(GROUPS - 1, 0)
                place(GROUPS - 1, 1)

            @block.tensor
            def _(pe):
                for h in range(2):
                    pe.sem_inc(placed[h], 1)
                with pe.Fori(0, GROUPS) as i:
                    now, next_ = pe.snap(i + 1), pe.snap(i + 2)
                    for u in range(U):
                        h, k = divmod(u, HALF)
                        if k == 0:
                            pe.wait_ge(hots[h], now)
                            pe.wait_ge(masks[h], next_)
                            pe.wait_ge(placed[h], now)
                        pe.wait_ge(current[u], now)
                        nc.tensor.matmul(pn[u % 2][:, :], ident[:, :], cur[:, u % 2, :], start=True, stop=False)
                        nc.tensor.matmul(pn[u % 2][:, :], hot_lo[:, h, k, :], hot_hi[:, h, k, :],
                                         start=False, stop=True).then_inc(counted[u], 1)
                        nc.tensor.matmul(pl[h][:, k, :], hot_t[:, h, k * P:(k + 1) * P], cur[:, u % 2, :],
                                         start=True, stop=False)
                        nc.tensor.matmul(pl[h][:, k, :], same[:, u, :], hot_hi[:, h, k, :],
                                         start=False, stop=True).then_inc(looked[u], 1)

            @block.scalar
            def _(act):
                act.sem_inc(current[0], 1)
                with act.Fori(0, GROUPS) as i:
                    now, next_ = act.snap(i + 1), act.snap(i + 2)
                    for u in range(U):
                        act.wait_ge(counted[u], now)
                        act.wait_ge(looked[(u - 1) % U], next_ if u >= 1 else now)
                        nc.scalar.copy(cur[:, (u + 1) % 2, :], pn[u % 2][:, :]).then_inc(current[(u + 1) % U], 1)

            @block.gpsimd
            def _(pool):
                for h in range(2):
                    pool.sem_inc(freed[h], 1)
                def scatter(i, h):
                    pool.wait_ge(placed[h], i + 2)
                    pool.sem_inc(steps, 1)
                    for k in range(HALF):
                        pool.indirect_dma_start(
                            out=sorted_d, out_offset=bass.IndirectOffsetOnAxis(ap=posi[:, h, k:k + 1], axis=0),
                            in_=rec[:, h, k, :], in_offset=None).then_inc(wrote[h * HALF + k], 16)

                def written(count, h):
                    for k in range(HALF):
                        pool.wait_ge(wrote[h * HALF + k], count * 16)
                    pool.sem_inc(freed[h], 1)

                scatter(0, 0)
                scatter(0, 1)
                written(1, 0)
                with pool.Fori(1, GROUPS) as i:
                    scatter(i, 0)
                    written(i, 1)
                    scatter(i, 1)
                    written(i + 1, 0)
                written(GROUPS, 1)


def gate_rows_and_experts(nc, sorted_d, start_d, tab_d, ad_d, fill_d, rec_d, yT_d, w1_d, b1_d, w2_d, b2_d, z_d):
    with Stage(nc, "gate") as s:
        R = 3
        start = s.sb("start", [P, HI], I32)
        zeros = s.sb("zeros", [P, NTF * H])
        ad = s.sb("ad", [P, NW, H])
        idx = s.sb("idx", [P, R, HALF, 2], I32)
        tg = s.sb("tg", [P, R * HALF, H + HX])
        steps, consts, zeroed, filled, spread, ticks_sp = (
            s.sem(n) for n in ("steps", "consts", "zeroed", "filled", "spread", "ticks_sp"))
        loaded, stored = s.sems("loaded", R), s.sems("stored", R)
        got = s.sems("got", R * HALF)
        ROUNDS = NTF // (R * HALF)
        assert ROUNDS * R * HALF == NTF
        FB = FF // P
        w1 = s.sb("w1", [P, 2, NX * FF])
        w2 = s.sb("w2", [P, NX * FB, D])
        b1 = s.sb("b1", [P, NX * FB])
        b2 = s.sb("b2", [P, NX, D])
        yT = s.sb("yT", [P, 2, 2, P])
        hid = s.sb("hid", [P, NX * FB, 2 * P])
        z = s.sb("z", [P, NX, 2, D])
        pU = [s.ps(f"pU{k}", [P, 512]) for k in range(4)]
        pD = [s.ps(f"pD{k}", [P, 512]) for k in range(4)]
        weights = s.sem("weights")
        y_here = s.sem("y_here")
        z_out = s.sems("z_out", NX)
        up, hidden = s.sems("up", NX * FB), s.sems("hidden", NX * FB)
        down, biased = s.sems("down", NX * 2), s.sems("biased", NX * 2)
        ticks_act = s.sem("ticks_act")
        block = s.block()

        @block.sync
        def _(sp):
            def load_indices(i, h):
                at = bass.ds((i * R + h) * HALF * P + 1, HALF * P)
                sp.dma_start(idx[:, h, :, :], sorted_d[at, :].rearrange("(t p) w -> p t w", p=P))\
                    .then_inc(loaded[h], 16)

            def store_rows(i, h):
                for k in range(HALF):
                    sp.wait_ge(got[h * HALF + k], (i + 1) * 16)
                sp.sem_inc(ticks_sp, 1)
                at = bass.ds((i * R + h) * HALF * P, HALF * P)
                sp.dma_start(rec_d[at, 0:H + HX].rearrange("(t p) c -> p t c", p=P),
                             tg[:, h * HALF:(h + 1) * HALF, :]).then_inc(stored[h], 16)

            sp.dma_start(start[:, :], start_d).then_inc(consts, 16)
            sp.dma_start(ad[:, :, :], ad_d.rearrange("(w p) h -> p w h", p=P)).then_inc(consts, 16)
            sp.wait_ge(zeroed, 1)
            sp.dma_start(fill_d[1:NTF * P + 1, :].rearrange("(p n) h -> p (n h)", p=P), zeros[:, :])\
                .then_inc(filled, 16)
            for h in range(R):
                sp.sem_inc(stored[h], 16)
                load_indices(0, h)
            with sp.Fori(0, ROUNDS - 1) as i:
                for h in range(R):
                    store_rows(i, h)
                    load_indices(i + 1, h)
            for h in range(R):
                store_rows(ROUNDS - 1, h)
            for h in range(R):
                sp.wait_ge(stored[h], 16 * (ROUNDS + 1))

        @block.gpsimd
        def _(pool):
            with pool.Fori(0, ROUNDS) as i:
                for h in range(R):
                    pool.wait_ge(loaded[h], (i + 1) * 16)
                    pool.wait_ge(stored[h], (i + 1) * 16)
                    pool.sem_inc(steps, 1)
                    for k in range(HALF):
                        pool.indirect_dma_start(
                            out=tg[:, h * HALF + k, :], out_offset=None, in_=tab_d,
                            in_offset=bass.IndirectOffsetOnAxis(ap=idx[:, h, k, 0:1], axis=0))\
                            .then_inc(got[h * HALF + k], 16)
            pool.wait_ge(consts, 32)
            pool.wait_ge(filled, 16)
            windows = -(-N // P)
            for w in range(windows):
                n = min(P, N - w * P)
                pool.indirect_dma_start(
                    out=fill_d, out_offset=bass.IndirectOffsetOnAxis(ap=start[0:n, w:w + 1], axis=0),
                    in_=ad[0:n, w, :], in_offset=None).then_inc(spread, 16)
            pool.wait_ge(spread, 16 * windows)

        @block.tensor
        def _(pe):
            pe.wait_ge(weights, 16 * (2 * NX + 2))
            with pe.Fori(0, NW // 2) as i:
                pe.wait_ge(y_here, (i + 1) * 16)

                def rise(e):
                    for f in range(e * FB, (e + 1) * FB):
                        pe.wait_ge(hidden[(f - 4) % (NX * FB)], i + (2 if f >= 4 else 1))
                        for c in range(2):
                            last = nc.tensor.matmul(pU[f % 4][:, 0:2 * P].rearrange("p (w n) -> p w n", w=2),
                                                    w1[:, c, f * P:(f + 1) * P], yT[:, :, c, :],
                                                    start=(c == 0), stop=(c == 1))
                        last.then_inc(up[f], 1)

                def fall(e):
                    for w in range(2):
                        j = e * 2 + w
                        pe.wait_ge(biased[(j - 4) % (NX * 2)], i + (2 if j >= 4 else 1))
                        for f in range(FB):
                            if w == 0:
                                pe.wait_ge(hidden[e * FB + f], i + 2)
                            last = nc.tensor.matmul(pD[j % 4][:, 0:D], hid[:, e * FB + f, w * P:(w + 1) * P],
                                                    w2[:, e * FB + f, :], start=(f == 0), stop=(f == FB - 1))
                        last.then_inc(down[j], 1)

                rise(0)
                for e in range(1, NX):
                    rise(e)
                    fall(e - 1)
                fall(NX - 1)

        @block.scalar
        def _(act):
            for k in range(NX):
                act.dma_start(w1[:, :, k * FF:(k + 1) * FF], w1_d[k, :, :].rearrange("(c p) n -> p c n", p=P))\
                    .then_inc(weights, 16)
                act.dma_start(w2[:, k * FB:(k + 1) * FB, :], w2_d[k, :, :].rearrange("(c p) n -> p c n", p=P))\
                    .then_inc(weights, 16)
            act.dma_start(b1[:, :], b1_d).then_inc(weights, 16)
            act.dma_start(b2[:, :, :].rearrange("p k n -> p (k n)"), b2_d.to_broadcast([P, NX * D]))\
                .then_inc(weights, 16)
            act.wait_ge(weights, 16 * (2 * NX + 2))
            act.preload_act_table(ACT.Gelu)
            for f in range(NX * FB):
                act.sem_inc(hidden[f], 1)
            for e in range(NX):
                act.sem_inc(z_out[e], 16)

            def load_y(i):
                act.dma_start(yT[:, :, :, :].rearrange("p w c n -> p w (c n)"),
                              yT_d[bass.ds(i * 2, 2), :, :].rearrange("w p n -> p w n")).then_inc(y_here, 16)

            def body(i, last):
                for f in range(NX * FB):
                    act.wait_ge(up[f], i + 1)
                    act.wait_ge(down[f // FB * 2 + 1], i + 1)
                    nc.scalar.activation(hid[:, f, :], pU[f % 4][:, 0:2 * P], ACT.Gelu, bias=b1[:, f:f + 1])\
                        .then_inc(hidden[f], 1)
                if not last:
                    load_y(i + 1)
                for e in range(NX):
                    act.wait_ge(biased[e * 2 + 1], i + 2)
                    act.dma_start(z_d[e, bass.ds(i * 2 * P, 2 * P), :].rearrange("(w p) n -> p w n", p=P),
                                  z[:, e, :, :]).then_inc(z_out[e], 16)

            load_y(0)
            with act.Fori(0, NW // 2 - 1) as i:
                body(i, False)
            body(NW // 2 - 1, True)
            for e in range(NX):
                act.wait_ge(z_out[e], 16 * (NW // 2 + 1))

        @block.vector
        def _(v):
            nc.vector.memset(zeros[:, :], 0.0).then_inc(zeroed, 1)
            for j in range(NX * 2):
                v.sem_inc(biased[j], 1)
                if j % 2:
                    v.sem_inc(down[j], 1)
            v.wait_ge(weights, 16 * (2 * NX + 2))
            with v.Fori(0, NW // 2) as i:
                for e in range(NX):
                    v.wait_ge(z_out[e], (i + 1) * 16)
                    for w in range(2):
                        j = e * 2 + w
                        v.wait_ge(down[j], i + 1 + j % 2)
                        nc.vector.tensor_tensor(z[:, e, w, :], pD[j % 4][:, 0:D], b2[:, e, :], ALU.add)\
                            .then_inc(biased[j], 1)


def gate_weights(nc, acc, g, b_gat, gam, bet, below_in):
    with Stage(nc, "gatew") as s:
        ticks, ticks_sp = s.sem("ticks"), s.sem("ticks_sp")
        vec = s.sb("vec", [P, 3, HX])
        below = s.sb("below", [P, NX * NX])
        den = s.sb("den", [P, NW, H])
        a = s.sb("a", [P, NW, HX])
        b = s.sb("b", [P, NW, HX])
        m = s.sb("m", [P, NW])
        r = s.sb("r", [P, NW])
        sc = s.sb("sc", [P, NW, NX])
        cmp = s.sb("cmp", [P, NW, NX, NX])
        eq = s.sb("eq", [P, NW, NX, NX])
        rank = s.sb("rank", [P, NW, NX])
        k1 = s.sb("k1", [P, NW, NX])
        k2 = s.sb("k2", [P, NW, NX])
        s1 = s.sb("s1", [P, NW])
        s2 = s.sb("s2", [P, NW])
        eps = s.sb("eps", [P, 1])
        consts, dve, act_s = s.sem("consts"), s.sem("dve"), s.sem("act")
        block = s.block()
        marks = {}

        @block.sync
        def _(sp):
            for k, src in enumerate((b_gat, gam, bet)):
                sp.dma_start(vec[:, k, :], src.to_broadcast([P, HX])).then_inc(consts, 16)
            sp.dma_start(below[:, :], below_in.to_broadcast([P, NX * NX])).then_inc(consts, 16)

        @block.vector
        def _(v):
            step = Chain(dve)
            tt, ts = nc.vector.tensor_tensor, nc.vector.tensor_scalar

            def row(k):
                return vec[:, k, :].unsqueeze(1).to_broadcast([P, NW, HX])

            def wide(ap, n):
                return ap.unsqueeze(2).to_broadcast([P, NW, n])

            v.wait_ge(consts, 64)
            step(v, nc.vector.memset(eps[:, :], EPS))
            step(v, ts(den[:, :, :], acc[:, :, HX + 1:], 1e-16, None, ALU.add))
            step(v, nc.vector.reciprocal(den[:, :, :], den[:, :, :]))
            for h in range(H):
                step(v, tt(a[:, :, h * NX:(h + 1) * NX], acc[:, :, h * NX:(h + 1) * NX],
                           wide(den[:, :, h], NX), ALU.mult))
            step(v, tt(a[:, :, :], a[:, :, :], row(0), ALU.add))
            step(v, nc.vector.tensor_reduce(m[:, :], a[:, :, :], AX.X, ALU.add))
            step(v, ts(m[:, :], m[:, :], 1.0 / HX, None, ALU.mult))
            step(v, tt(a[:, :, :], a[:, :, :], wide(m[:, :], HX), ALU.subtract))
            step(v, tt(b[:, :, :], a[:, :, :], a[:, :, :], ALU.mult))
            step(v, nc.vector.tensor_reduce(r[:, :], b[:, :, :], AX.X, ALU.add))
            step(v, ts(r[:, :], r[:, :], 1.0 / HX, None, ALU.mult))
            marks["var"] = step.n
            v.wait_ge(act_s, 1)
            step(v, nc.vector.reciprocal(r[:, :], r[:, :]))
            step(v, tt(a[:, :, :], a[:, :, :], wide(r[:, :], HX), ALU.mult))
            step(v, tt(a[:, :, :], a[:, :, :], row(1), ALU.mult))
            step(v, tt(a[:, :, :], a[:, :, :], row(2), ALU.add))
            step(v, tt(sc[:, :, :], a[:, :, 0:NX], a[:, :, NX:2 * NX], ALU.add))
            step(v, tt(sc[:, :, :], sc[:, :, :], a[:, :, 2 * NX:3 * NX], ALU.add))
            step(v, tt(sc[:, :, :], sc[:, :, :], a[:, :, 3 * NX:], ALU.add))
            step(v, ts(sc[:, :, :], sc[:, :, :], 1.0 / H, None, ALU.mult))
            for i in range(NX):
                me = wide(sc[:, :, i], NX)
                step(v, tt(cmp[:, :, i, :], sc[:, :, :], me, ALU.is_gt))
                step(v, tt(eq[:, :, i, :], sc[:, :, :], me, ALU.is_equal))
                step(v, tt(eq[:, :, i, :], eq[:, :, i, :],
                           below[:, i * NX:(i + 1) * NX].unsqueeze(1).to_broadcast([P, NW, NX]), ALU.mult))
                step(v, tt(cmp[:, :, i, :], cmp[:, :, i, :], eq[:, :, i, :], ALU.add))
                step(v, nc.vector.tensor_reduce(rank[:, :, i], cmp[:, :, i, :], AX.X, ALU.add))
            step(v, ts(k1[:, :, :], rank[:, :, :], 0.0, None, ALU.is_equal))
            step(v, ts(k2[:, :, :], rank[:, :, :], 1.0, None, ALU.is_equal))
            step(v, tt(a[:, :, 0:NX], sc[:, :, :], k1[:, :, :], ALU.mult))
            step(v, nc.vector.tensor_reduce(s1[:, :], a[:, :, 0:NX], AX.X, ALU.add))
            step(v, tt(a[:, :, 0:NX], sc[:, :, :], k2[:, :, :], ALU.mult))
            step(v, nc.vector.tensor_reduce(s2[:, :], a[:, :, 0:NX], AX.X, ALU.add))
            step(v, tt(s2[:, :], s2[:, :], s1[:, :], ALU.subtract))
            marks["gap"] = step.n
            v.wait_ge(act_s, 2)
            step(v, ts(s1[:, :], s2[:, :], 1.0, None, ALU.add))
            step(v, nc.vector.reciprocal(s1[:, :], s1[:, :]))
            step(v, tt(s2[:, :], s2[:, :], s1[:, :], ALU.mult))
            step(v, tt(k1[:, :, :], k1[:, :, :], wide(s1[:, :], NX), ALU.mult))
            step(v, tt(k2[:, :, :], k2[:, :, :], wide(s2[:, :], NX), ALU.mult))
            step(v, tt(g[:, :, :], k1[:, :, :], k2[:, :, :], ALU.add))

        @block.scalar
        def _(act):
            act.wait_ge(dve, marks["var"])
            nc.scalar.activation(r[:, :], r[:, :], ACT.Sqrt, bias=eps[:, 0:1]).then_inc(act_s, 1)
            act.wait_ge(dve, marks["gap"])
            nc.scalar.activation(s2[:, :], s2[:, :], ACT.Exp).then_inc(act_s, 1)


def mix(nc, g, x2_d, z_d, out_d):
    with Stage(nc, "mix") as s:
        ticks_sp = s.sem("ticks_sp")
        x2 = s.sb("x2", [P, 2, 2, D])
        z = s.sb("z", [P, 2, NX, 2, D])
        here, mixed, out = s.sems("here", 2), s.sems("mixed", 2 * NX * 2), s.sems("out", 2)
        steps = NW // 2
        block = s.block()

        def at(i):
            return bass.ds(i * 2 * P, 2 * P)

        def load(eng, i, b):
            eng.dma_start(x2[:, b, :, :], x2_d[at(i), :].rearrange("(w p) n -> p w n", p=P)).then_inc(here[b], 16)
            for e in range(NX):
                eng.dma_start(z[:, b, e, :, :], z_d[e, at(i), :].rearrange("(w p) n -> p w n", p=P))\
                    .then_inc(here[b], 16)

        @block.sync
        def _(sp):
            load(sp, 0, 0)
            load(sp, 1, 1)
            with sp.Fori(0, steps // 2 - 1) as i:
                for b in range(2):
                    sp.wait_ge(out[b], (i + 1) * 16)
                    sp.sem_inc(ticks_sp, 1)
                    load(sp, i * 2 + 2 + b, b)
            sp.wait_ge(out[0], steps // 2 * 16)
            load(sp, steps - 1, 0)

        @block.vector
        def _(v):
            def blend(i, b, n):
                v.wait_ge(here[b], (n + 1) * 80)
                for e in range(NX):
                    for w in range(2):
                        j = (b * NX + e) * 2 + w
                        if e:
                            v.wait_ge(mixed[j - 2], n + 1)
                        gate = g[:, bass.ds(i * 2 + w, 1), e:e + 1].rearrange("p o n -> p (o n)")
                        nc.vector.scalar_tensor_tensor(x2[:, b, w, :], z[:, b, e, w, :], gate, x2[:, b, w, :],
                                                       ALU.mult, ALU.add).then_inc(mixed[j], 1)

            with v.Fori(0, steps // 2) as i:
                for b in range(2):
                    blend(i * 2 + b, b, i)
            blend(steps - 1, 0, steps // 2)

        @block.scalar
        def _(act):
            def store(i, b, n):
                for w in range(2):
                    act.wait_ge(mixed[(b * NX + NX - 1) * 2 + w], n + 1)
                act.dma_start(out_d[at(i), :].rearrange("(w p) n -> p w n", p=P), x2[:, b, :, :])\
                    .then_inc(out[b], 16)

            with act.Fori(0, steps // 2) as i:
                for b in range(2):
                    store(i * 2 + b, b, i)
            store(steps - 1, 0, steps // 2)
            act.wait_ge(out[0], 16 * (steps // 2 + 1))
            act.wait_ge(out[1], 16 * (steps // 2))


def build(nc, a, out_d):
    def scratch(name, shape, dt=F32):
        return nc.dram_tensor(name, shape, dt, kind="Internal").ap()

    xl_d, res_d, x2_d = (scratch(n, (NP, D)) for n in ("xl", "res", "x2"))
    xlx_d, xrx_d = (scratch(n, (NP, WX)) for n in ("xlx", "xrx"))
    yT_d = scratch("yT", (NW, P, D))
    z_d = scratch("z", (NX, NP, D))
    tab_d, ad_d = scratch("tab", (NP, H + HX)), scratch("ad", (NP, H))
    lg_d, rec_d = scratch("lg", (NTG * P, H)), scratch("rec", (NTG * P, RV - 1))
    rf_d, fill_d = scratch("rf", (NTF * P, FROW)), scratch("fill", (NTF * P + 2, H))
    sorted_d = scratch("sorted", (NTF * P + 2, 2), I32)
    low_d, start_d = scratch("low", (1, NTF * P), BF16), scratch("start", (P, HI), I32)
    first_d = scratch("first", (P, HI))
    ends_d, back_d = scratch("ends", (P, 2 * H + 2)), scratch("back", (2, H, P))
    key_d = scratch("key", (1, NTG))
    KB = -(-max(KG, KF) // P)
    tile_d, win_d = scratch("tile", (2, KB * P), I32), scratch("win", (1, KB * P))

    node_projections(nc, a["x"], a["w_cat"], a["b_cat"], a["att"], xl_d, xlx_d, xrx_d, res_d, a["ident"],
                     a["f_dst_tab"], a["f_dst_lin"], low_d, start_d, first_d, sorted_d, a["iota"], a["tri"])
    worklist(nc, "gwork", NTG, KG, a["last"], key_d, tile_d, win_d, a["kval"])
    edge_logits(nc, a["src_tab"], a["dst_lin"], a["eaT"], a["w_ex"], a["att"], xlx_d, xrx_d, tile_d, win_d,
                a["part"], lg_d)
    segment_max(nc, "gmax", NTG, a["dst_halo"], a["src_lin"], a["ea"], lg_d, rec_d, ends_d, back_d)
    with nc.sbuf_tensor("acc", [P, NW, CG], F32) as acc:
        aggregate_nodes(nc, acc, rec_d, xl_d, tile_d, win_d, a["iota"])
        nodes_after(nc, acc, xl_d, xrx_d[:, 0:D], res_d, a["x"], a["w_e"], a["att"], a["w_gat"], a["att_src"],
                    a["att_dst"], x2_d, yT_d, tab_d, ad_d, a["ident"])
    sort_by_destination(nc, a["f_dst_tab"], a["f_rec"], low_d, first_d, sorted_d, a["ident"],
                        a["iota"], a["tri"], a["part"])
    gate_rows_and_experts(nc, sorted_d, start_d, tab_d, ad_d, fill_d, rf_d, yT_d, a["w1"], a["b1"], a["w2"],
                          a["b2"], z_d)
    segment_max(nc, "fmax", NTF, sorted_d, None, None, rf_d[:, 0:H], rf_d, ends_d, back_d, ad_d, fill_d)
    worklist(nc, "fwork", NTF, KF,
             bass.AP(tensor=sorted_d.tensor, offset=sorted_d.offset + P * 2 + 1, ap=[[1, 1], [P * 2, NTF]]),
             key_d[:, 0:NTF], tile_d, win_d, a["kval"])
    with nc.sbuf_tensor("gates", [P, NW, NX], F32) as g:
        with nc.sbuf_tensor("facc", [P, NW, CF], F32) as facc:
            aggregate_gate(nc, facc, rf_d, tile_d, win_d, a["iota"])
            gate_weights(nc, facc, g, a["b_gat"], a["gamma"], a["beta"], a["below"])
        mix(nc, g, x2_d, z_d, out_d)


def lay_out(v):
    def padded(x, n, fill):
        out = np.full((n,) + x.shape[1:], fill, x.dtype)
        out[:x.shape[0]] = x
        return out

    v = {k: np.asarray(x) for k, x in v.items()}
    src = padded(v["src"], NTG * P, 0)
    dst = padded(v["dst"], NTG * P, NP - 1)
    ea = padded(v["edge_attr_16"], NTG * P, 0)
    loops = np.arange(N, dtype=np.int32)
    ei = v["L0_ffn_edge_index"]
    f_src = padded(np.concatenate([ei[0], loops]), NTF * P, 0)
    f_dst = padded(np.concatenate([ei[1], loops]), NTF * P, HI * P - 1)

    def room(rows, mark=0.0):
        return np.repeat(np.array([[0.0] * H + [mark]], np.float32), rows, 0)

    row = np.arange(P, dtype=np.float32)
    kb = -(-max(KG, KF) // P)
    return {
        "x": padded(v["x"], NP, 0),
        "w_cat": np.concatenate([v["L0_gnn_W_l"], room(D), v["L0_gnn_W_r"], room(D), v["L0_gnn_W_res"]], 1),
        "b_cat": np.concatenate([v["L0_gnn_b_l"][None], room(1), v["L0_gnn_b_r"][None], room(1, 1.0),
                                 v["L0_gnn_bias"][None]], 1),
        "w_e": v["L0_gnn_W_e"], "w_ex": np.concatenate([v["L0_gnn_W_e"], room(ED)], 1),
        "att": v["L0_gnn_att"].reshape(1, D),
        "src_tab": src.reshape(NTG, P).T, "dst_lin": dst[None],
        "eaT": ea.T, "ea": ea, "src_lin": src,
        "dst_halo": np.concatenate([[-1], dst, [-1]]).astype(np.int32)[:, None],
        "last": dst[P - 1::P][None],
        "w_gat": v["L0_ffn_W_gat"], "att_src": v["L0_ffn_att_src"].reshape(1, HX),
        "att_dst": v["L0_ffn_att_dst"].reshape(1, HX), "b_gat": v["L0_ffn_b_gat"][None],
        "gamma": v["L0_ffn_ln_gamma"][None], "beta": v["L0_ffn_ln_beta"][None],
        "w1": v["L0_ffn_W1"], "w2": v["L0_ffn_W2"],
        "b1": v["L0_ffn_b1"].reshape(NX * FF // P, P).T, "b2": v["L0_ffn_b2"].reshape(1, NX * D),
        "f_dst_tab": f_dst.reshape(NTF, P).T, "f_dst_lin": f_dst[None],
        "f_rec": np.stack([f_src, f_dst], 1).reshape(NTF, P, 2).transpose(1, 0, 2),
        "ident": np.eye(P, dtype=np.float32), "iota": row[None], "part": row[:, None],
        "tri": np.triu(np.ones((P, P), np.float32), 1),
        "kval": np.arange(kb * P, dtype=np.float32).reshape(kb, P).T,
        "below": np.tril(np.ones((NX, NX), np.float32), -1).reshape(1, NX * NX),
    }


def kernel(**inputs):
    import concourse.bacc as bacc
    from concourse.bass_utils import run_bass_kernel_spmd as run

    nc = bacc.Bacc("TRN2", target_bir_lowering=False, num_devices=1)
    arrays = {f"in_{k}": np.ascontiguousarray(x) for k, x in lay_out(inputs).items()}
    aps = {k[3:]: nc.dram_tensor(k, x.shape, mybir.dt.from_np(x.dtype), kind="ExternalInput").ap()
           for k, x in arrays.items()}
    out_d = nc.dram_tensor("out", (NP, D), F32, kind="ExternalOutput").ap()
    build(nc, aps, out_d)
    r = run(nc, [arrays], core_ids=[0])
    return r.results[0]["out"][:N]
```
